# Optimizing a Trainium2 kernel written in Bass

```python
import numpy as np
import jax
import jax.numpy as jnp

def _softmax(x, axis=-1):
    return jax.nn.softmax(x, axis=axis)

def _gelu(x):
    return jax.nn.gelu(x, approximate=True)

def _silu(x):
    return jax.nn.silu(x)

def _sigmoid(x):
    return jax.nn.sigmoid(x)

def _layernorm(x, axis=-1, eps=1e-05):
    m = jnp.mean(x, axis=axis, keepdims=True)
    v = jnp.var(x, axis=axis, keepdims=True)
    return (x - m) / jnp.sqrt(v + eps)

def _scatter_add(tgt, idx, src, axis=0):
    return tgt.at[idx].add(src)

def _segment_sum(src, seg, n):
    return jax.ops.segment_sum(src, seg, n)
kernel_name = 'mk_audio_tower_d2_tok_aud1d256_r4_42f6e2'

def setup_inputs(seed: int=0):
    np.random.seed(seed)
    _w = jnp.asarray

    def _rec_inputs():
        import jax
        import jax.numpy as jnp
        _rk = jax.random.key(seed)
        x = 0.000296351 + 0.99907 * jax.random.normal(jax.random.fold_in(_rk, 1), (16, 4096), jnp.float32)
        return x
    x = _rec_inputs()

    def _L0_tok_setup():
        import jax, jax.numpy as jnp
        import numpy as np
        B, L = (64, 4096)
        INTERP_FACTOR = 0.25
        WINDOW, STEP = (64, 64)
        ALPHA, BETA, TEMP = (0.12, 0.9, 1.0)
        A = -0.75

        def _cubic_w(t):
            at = jnp.abs(t)
            w_near = ((A + 2.0) * at - (A + 3.0)) * at * at + 1.0
            w_far = ((A * at - 5.0 * A) * at + 8.0 * A) * at - 4.0 * A
            return jnp.where(at <= 1.0, w_near, jnp.where(at < 2.0, w_far, 0.0))

        def cubic_interpolate_1d(signal, interp_factor):
            b, n = signal.shape
            num_points = int((n - 1) / interp_factor) + 1
            x = jnp.linspace(0.0, 1.0, num_points) * (n - 1)
            i0 = jnp.floor(x).astype(jnp.int32)
            frac = x - i0.astype(x.dtype)
            offs = jnp.arange(-1, 3)
            idx = jnp.clip(i0[:, None] + offs[None, :], 0, n - 1)
            w = _cubic_w(frac[:, None] - offs[None, :].astype(x.dtype))
            taps = signal[:, idx]
            return jnp.einsum('bpk,pk->bp', taps, w)

        def _apply_kernels(x):
            poly = (x + 1.3) ** 2
            gauss = jnp.exp(-0.5 * ((x - 0.7) / 1.0) ** 2)
            return 0.5 * poly + 0.5 * gauss

        def soft_minimum(a, b, temperature):
            b = jnp.broadcast_to(b, a.shape)
            stacked = jnp.stack([-a * temperature, -b * temperature], axis=0)
            return -jax.nn.logsumexp(stacked, axis=0) / temperature

        def _forward(signal):
            interp = cubic_interpolate_1d(signal, INTERP_FACTOR)
            n = interp.shape[1]
            n_windows = (n - WINDOW) // STEP + 1
            starts = jnp.arange(n_windows) * STEP
            idx = starts[:, None] + jnp.arange(WINDOW)[None, :]
            windows = interp[:, idx]
            kw = _apply_kernels(windows)
            M = jnp.abs(jnp.fft.fft(kw, axis=-1))
            Mmax = jnp.max(M, axis=-1, keepdims=True)
            thr = ALPHA * Mmax
            mask = jax.nn.sigmoid((M - thr) * TEMP)
            Mt = M * mask
            return soft_minimum(Mt, BETA * Mmax, TEMP)
        key = jax.random.key(seed)
        return {'signal': jax.random.normal(key, (B, L), dtype=jnp.float32)}
    _L0_tok_all = _L0_tok_setup()
    _L0_tok_in = {k: v for k, v in _L0_tok_all.items() if k in ()}
    del _L0_tok_all

    def _L0_attn_setup():
        import jax, jax.numpy as jnp
        import numpy as np
        from math import sqrt
        DIM = 64
        key = jax.random.key(seed)
        k1, k2, k3, k4 = jax.random.split(key, 4)
        B, T, D, H, R = (2, 1024, DIM, 8, 32)

        def xavier(k, shape, fan_in, fan_out):
            a = sqrt(6.0 / (fan_in + fan_out))
            return jax.random.uniform(k, shape, jnp.float32, -a, a)
        x = jax.random.normal(k1, (B, T, D), jnp.float32)
        Q = xavier(k2, (H, R, D), D, R)
        K = xavier(k3, (H, R, D), D, R)
        VO = xavier(k4, (H, D, D), D, D)
        return {'x': x, 'Q': Q, 'K': K, 'VO': VO}
    _L0_attn_all = _L0_attn_setup()
    _L0_attn_in = {k: v for k, v in _L0_attn_all.items() if k in ('Q', 'K', 'VO')}
    del _L0_attn_all

    def _L0_ffn_setup():
        import jax, jax.numpy as jnp
        import numpy as np
        B, S, H, F, E, K = (8, 1024, 64, 128, 16, 2)
        EPS = 1e-05
        key = jax.random.key(seed)
        ks = jax.random.split(key, 9)
        sc = 0.02
        return {'x': jax.random.normal(ks[0], (B, S, H), dtype=jnp.float32), 'gate_w': jax.random.normal(ks[1], (H, E), dtype=jnp.float32) * sc, 'gate_b': jnp.zeros((E,), dtype=jnp.float32), 'w1': jax.random.normal(ks[2], (E, H, F), dtype=jnp.float32) * sc, 'b1': jnp.zeros((E, F), dtype=jnp.float32), 'w2': jax.random.normal(ks[3], (E, F, H), dtype=jnp.float32) * sc, 'b2': jnp.zeros((E, H), dtype=jnp.float32), 'gamma': jnp.ones((H,), dtype=jnp.float32), 'beta': jnp.zeros((H,), dtype=jnp.float32)}
    _L0_ffn_all = _L0_ffn_setup()
    _L0_ffn_in = {k: v for k, v in _L0_ffn_all.items() if k in ('gate_w', 'gate_b', 'w1', 'b1', 'w2', 'b2', 'gamma', 'beta')}
    del _L0_ffn_all

    def _L1_attn_setup():
        import jax, jax.numpy as jnp
        import numpy as np
        B, N, C, H = (64, 75, 64, 8)
        STD = 0.02

        def _rel_indices(n):
            d = (jnp.arange(n)[None, :] - jnp.arange(n)[:, None]).astype(jnp.float32)
            return jnp.stack([d, jnp.zeros_like(d), d * d], axis=-1)
        key = jax.random.key(seed)
        ks = jax.random.split(key, 6)
        return {'x': jax.random.normal(ks[0], (B, N, C), jnp.float32), 'Wqk': jax.random.normal(ks[1], (2 * C, C), jnp.float32) * STD, 'Wv': jax.random.normal(ks[2], (C, C), jnp.float32) * STD, 'Wpos': jax.random.normal(ks[3], (H, 3), jnp.float32) * STD, 'bpos': jnp.zeros((H,), jnp.float32), 'Wproj': jax.random.normal(ks[4], (C, C), jnp.float32) * STD, 'bproj': jnp.zeros((C,), jnp.float32), 'gating': jnp.ones((H,), jnp.float32)}
    _L1_attn_all = _L1_attn_setup()
    _L1_attn_in = {k: v for k, v in _L1_attn_all.items() if k in ('Wqk', 'Wv', 'Wpos', 'bpos', 'Wproj', 'bproj', 'gating')}
    del _L1_attn_all

    def _L1_ffn_setup():
        import jax, jax.numpy as jnp
        import numpy as np
        NUM_EXPERTS = 8
        TOP_K = 2
        B, S, D = (8, 2048, 64)

        def _moe(tokens, router_w, w1, b1, w2, b2):
            N = tokens.shape[0]
            E = router_w.shape[0]
            logits = tokens.astype(jnp.float32) @ router_w.astype(jnp.float32).T
            probs = jax.nn.softmax(logits, axis=-1)
            rw, re = jax.lax.top_k(probs, TOP_K)
            if TOP_K > 1:
                rw = rw / jnp.maximum(rw.sum(-1, keepdims=True), 1e-12)
            rw = rw.astype(tokens.dtype)
            combine = jnp.zeros((N, E), tokens.dtype).at[jnp.arange(N)[:, None], re].set(rw)
            out = tokens
            for e in range(E):
                h = jax.nn.gelu(tokens @ w1[e] + b1[e], approximate=False)
                y = h @ w2[e] + b2[e]
                out = out + combine[:, e:e + 1] * y
            return out
        key = jax.random.key(seed)
        ks = jax.random.split(key, 4)
        scale = 1.0 / np.sqrt(D).astype(np.float32)
        return {'input_embeddings': jax.random.normal(ks[0], (B, S, D), jnp.float32), 'router_w': jax.random.normal(ks[1], (NUM_EXPERTS, D), jnp.float32) * scale, 'w1': jax.random.normal(ks[2], (NUM_EXPERTS, D, D), jnp.float32) * scale, 'b1': jnp.zeros((NUM_EXPERTS, D), jnp.float32), 'w2': jax.random.normal(ks[3], (NUM_EXPERTS, D, D), jnp.float32) * scale, 'b2': jnp.zeros((NUM_EXPERTS, D), jnp.float32)}
    _L1_ffn_all = _L1_ffn_setup()
    _L1_ffn_in = {k: v for k, v in _L1_ffn_all.items() if k in ('router_w', 'w1', 'b1', 'w2', 'b2')}
    del _L1_ffn_all
    return {'x': x, 'L0_attn_Q': _L0_attn_in['Q'], 'L0_attn_K': _L0_attn_in['K'], 'L0_attn_VO': _L0_attn_in['VO'], 'L0_ffn_gate_w': _L0_ffn_in['gate_w'], 'L0_ffn_gate_b': _L0_ffn_in['gate_b'], 'L0_ffn_w1': _L0_ffn_in['w1'], 'L0_ffn_b1': _L0_ffn_in['b1'], 'L0_ffn_w2': _L0_ffn_in['w2'], 'L0_ffn_b2': _L0_ffn_in['b2'], 'L0_ffn_gamma': _L0_ffn_in['gamma'], 'L0_ffn_beta': _L0_ffn_in['beta'], 'L1_attn_Wqk': _L1_attn_in['Wqk'], 'L1_attn_Wv': _L1_attn_in['Wv'], 'L1_attn_Wpos': _L1_attn_in['Wpos'], 'L1_attn_bpos': _L1_attn_in['bpos'], 'L1_attn_Wproj': _L1_attn_in['Wproj'], 'L1_attn_bproj': _L1_attn_in['bproj'], 'L1_attn_gating': _L1_attn_in['gating'], 'L1_ffn_router_w': _L1_ffn_in['router_w'], 'L1_ffn_w1': _L1_ffn_in['w1'], 'L1_ffn_b1': _L1_ffn_in['b1'], 'L1_ffn_w2': _L1_ffn_in['w2'], 'L1_ffn_b2': _L1_ffn_in['b2']}

def reference(x, L0_attn_Q, L0_attn_K, L0_attn_VO, L0_ffn_gate_w, L0_ffn_gate_b, L0_ffn_w1, L0_ffn_b1, L0_ffn_w2, L0_ffn_b2, L0_ffn_gamma, L0_ffn_beta, L1_attn_Wqk, L1_attn_Wv, L1_attn_Wpos, L1_attn_bpos, L1_attn_Wproj, L1_attn_bproj, L1_attn_gating, L1_ffn_router_w, L1_ffn_w1, L1_ffn_b1, L1_ffn_w2, L1_ffn_b2):
    import jax
    import jax.numpy as jnp

    def _L0_tok_ref(signal):
        import jax, jax.numpy as jnp
        import numpy as np
        B, L = (64, 4096)
        INTERP_FACTOR = 0.25
        WINDOW, STEP = (64, 64)
        ALPHA, BETA, TEMP = (0.12, 0.9, 1.0)
        A = -0.75

        def _cubic_w(t):
            at = jnp.abs(t)
            w_near = ((A + 2.0) * at - (A + 3.0)) * at * at + 1.0
            w_far = ((A * at - 5.0 * A) * at + 8.0 * A) * at - 4.0 * A
            return jnp.where(at <= 1.0, w_near, jnp.where(at < 2.0, w_far, 0.0))

        def cubic_interpolate_1d(signal, interp_factor):
            b, n = signal.shape
            num_points = int((n - 1) / interp_factor) + 1
            x = jnp.linspace(0.0, 1.0, num_points) * (n - 1)
            i0 = jnp.floor(x).astype(jnp.int32)
            frac = x - i0.astype(x.dtype)
            offs = jnp.arange(-1, 3)
            idx = jnp.clip(i0[:, None] + offs[None, :], 0, n - 1)
            w = _cubic_w(frac[:, None] - offs[None, :].astype(x.dtype))
            taps = signal[:, idx]
            return jnp.einsum('bpk,pk->bp', taps, w)

        def _apply_kernels(x):
            poly = (x + 1.3) ** 2
            gauss = jnp.exp(-0.5 * ((x - 0.7) / 1.0) ** 2)
            return 0.5 * poly + 0.5 * gauss

        def soft_minimum(a, b, temperature):
            b = jnp.broadcast_to(b, a.shape)
            stacked = jnp.stack([-a * temperature, -b * temperature], axis=0)
            return -jax.nn.logsumexp(stacked, axis=0) / temperature

        def _forward(signal):
            interp = cubic_interpolate_1d(signal, INTERP_FACTOR)
            n = interp.shape[1]
            n_windows = (n - WINDOW) // STEP + 1
            starts = jnp.arange(n_windows) * STEP
            idx = starts[:, None] + jnp.arange(WINDOW)[None, :]
            windows = interp[:, idx]
            kw = _apply_kernels(windows)
            M = jnp.abs(jnp.fft.fft(kw, axis=-1))
            Mmax = jnp.max(M, axis=-1, keepdims=True)
            thr = ALPHA * Mmax
            mask = jax.nn.sigmoid((M - thr) * TEMP)
            Mt = M * mask
            return soft_minimum(Mt, BETA * Mmax, TEMP)
        return _forward(signal)

    def _L0_attn_ref(x, Q, K, VO):
        import jax, jax.numpy as jnp
        import numpy as np
        from math import sqrt
        DIM = 64
        d = x.shape[-1]
        q = jnp.einsum('btd,hrd->bhtr', x, Q)
        k = jnp.einsum('bud,hrd->bhur', x, K)
        scores = jnp.einsum('bhtr,bhur->bhtu', q, k) / sqrt(d)
        attn = jax.nn.softmax(scores, axis=-1)
        ctx = jnp.einsum('bhtu,bud->bhtd', attn, x)
        out = jnp.einsum('bhtd,hde->bte', ctx, VO)
        return out

    def _L0_ffn_ref(x, gate_w, gate_b, w1, b1, w2, b2, gamma, beta):
        import jax, jax.numpy as jnp
        import numpy as np
        B, S, H, F, E, K = (8, 1024, 64, 128, 16, 2)
        EPS = 1e-05
        gate_logits = x @ gate_w + gate_b
        topk_vals, topk_idx = jax.lax.top_k(gate_logits, K)
        topk_w = jax.nn.softmax(topk_vals, axis=-1)
        h = jax.nn.relu(jnp.einsum('bsh,ehf->bsef', x, w1) + b1)
        expert_out = jnp.einsum('bsef,efh->bseh', h, w2) + b2
        sel = jnp.take_along_axis(expert_out, topk_idx[:, :, :, None], axis=2)
        moe = jnp.sum(topk_w[..., None] * sel, axis=2)
        y = x + moe
        mu = jnp.mean(y, axis=-1, keepdims=True)
        var = jnp.var(y, axis=-1, keepdims=True)
        return (y - mu) / jnp.sqrt(var + EPS) * gamma + beta

    def _L1_attn_ref(x, Wqk, Wv, Wpos, bpos, Wproj, bproj, gating):
        import jax, jax.numpy as jnp
        import numpy as np
        B, N, C, H = (64, 75, 64, 8)
        STD = 0.02

        def _rel_indices(n):
            d = (jnp.arange(n)[None, :] - jnp.arange(n)[:, None]).astype(jnp.float32)
            return jnp.stack([d, jnp.zeros_like(d), d * d], axis=-1)
        Bb, Nn, Cc = x.shape
        Hh = gating.shape[0]
        hd = Cc // Hh
        scale = hd ** (-0.5)
        qk = (x @ Wqk.T).reshape(Bb, Nn, 2, Hh, hd)
        q = qk[:, :, 0].transpose(0, 2, 1, 3)
        k = qk[:, :, 1].transpose(0, 2, 1, 3)
        patch_score = jax.nn.softmax(jnp.einsum('bhnd,bhmd->bhnm', q, k) * scale, axis=-1)
        rel = _rel_indices(Nn)
        pos_score = (rel @ Wpos.T + bpos).transpose(2, 0, 1)
        pos_score = jax.nn.softmax(pos_score, axis=-1)
        g = jax.nn.sigmoid(gating)[None, :, None, None]
        attn = (1.0 - g) * patch_score + g * pos_score[None]
        attn = attn / attn.sum(axis=-1, keepdims=True)
        v = (x @ Wv.T).reshape(Bb, Nn, Hh, hd).transpose(0, 2, 1, 3)
        out = jnp.einsum('bhnm,bhmd->bhnd', attn, v)
        out = out.transpose(0, 2, 1, 3).reshape(Bb, Nn, Cc)
        return out @ Wproj.T + bproj

    def _L1_ffn_ref(input_embeddings, router_w, w1, b1, w2, b2):
        import jax, jax.numpy as jnp
        import numpy as np
        NUM_EXPERTS = 8
        TOP_K = 2
        B, S, D = (8, 2048, 64)

        def _moe(tokens, router_w, w1, b1, w2, b2):
            N = tokens.shape[0]
            E = router_w.shape[0]
            logits = tokens.astype(jnp.float32) @ router_w.astype(jnp.float32).T
            probs = jax.nn.softmax(logits, axis=-1)
            rw, re = jax.lax.top_k(probs, TOP_K)
            if TOP_K > 1:
                rw = rw / jnp.maximum(rw.sum(-1, keepdims=True), 1e-12)
            rw = rw.astype(tokens.dtype)
            combine = jnp.zeros((N, E), tokens.dtype).at[jnp.arange(N)[:, None], re].set(rw)
            out = tokens
            for e in range(E):
                h = jax.nn.gelu(tokens @ w1[e] + b1[e], approximate=False)
                y = h @ w2[e] + b2[e]
                out = out + combine[:, e:e + 1] * y
            return out
        b, s, d = input_embeddings.shape
        tokens = input_embeddings.reshape(b * s, d)
        return _moe(tokens, router_w, w1, b1, w2, b2).reshape(b, s, d)
    h = _L0_tok_ref(x)
    h = h + _L0_attn_ref(_layernorm(h, axis=-1), L0_attn_Q, L0_attn_K, L0_attn_VO)
    h = h + _L0_ffn_ref(_layernorm(h, axis=-1), L0_ffn_gate_w, L0_ffn_gate_b, L0_ffn_w1, L0_ffn_b1, L0_ffn_w2, L0_ffn_b2, L0_ffn_gamma, L0_ffn_beta)
    h = h + _L1_attn_ref(_layernorm(h, axis=-1), L1_attn_Wqk, L1_attn_Wv, L1_attn_Wpos, L1_attn_bpos, L1_attn_Wproj, L1_attn_bproj, L1_attn_gating)
    h = h + _L1_ffn_ref(_layernorm(h, axis=-1), L1_ffn_router_w, L1_ffn_w1, L1_ffn_b1, L1_ffn_w2, L1_ffn_b2)
    return h

_drawn_inputs = setup_inputs


def setup_inputs(seed=0):
    import zlib

    import numpy as np

    out = dict(_drawn_inputs(seed))
    spreads = {'L0_ffn_gate_b': (0.0, 0.8),
     'L0_ffn_b1': (0.0, 2.0),
     'L0_ffn_b2': (0.0, 2.0),
     'L0_ffn_gamma': (1.0, 0.6),
     'L0_ffn_beta': (0.0, 0.8),
     'L1_attn_bpos': (0.0, 2.0),
     'L1_attn_bproj': (0.0, 0.8),
     'L1_attn_gating': (1.0, 0.6),
     'L1_ffn_b1': (0.0, 2.0),
     'L1_ffn_b2': (0.0, 0.8)}
    factors = {'L0_attn_Q': 5.649,
     'L0_attn_K': 6.835,
     'L0_ffn_gate_w': 8.0,
     'L0_ffn_w1': 8.0,
     'L0_ffn_w2': 8.0,
     'L1_attn_Wqk': 200.0,
     'L1_attn_Wv': 8.0,
     'L1_attn_Wpos': 64.024,
     'L1_attn_Wproj': 8.0}
    for name, (base, spread) in spreads.items():
        noise = np.random.default_rng([zlib.crc32(name.encode()), seed]).standard_normal(out[name].shape)
        drawn = base * np.exp(spread * noise) if base else spread * noise
        out[name] = jnp.asarray(drawn.astype(out[name].dtype))
    for name, factor in factors.items():
        out[name] = (out[name] * factor).astype(out[name].dtype)
    return out
```

```python
from contextlib import ExitStack

import numpy as np

import concourse.bass as bass
from concourse import mybir

ALU = mybir.AluOpType
ACT = mybir.ActivationFunctionType
AX = mybir.AxisListType
F32 = mybir.dt.float32
F32R = mybir.dt.float32r
BF16 = mybir.dt.bfloat16
U32 = mybir.dt.uint32

P = 128
B, SIG = 16, 4096
UP = 4
WIN = 64
NW = 255
HOP = WIN // UP
TAPS = 5
REACH = HOP + TAPS - 1
NB = WIN // 2 + 1
D = WIN
NT = 2 * B
H = 8
PAIRS = H // 2
UNITS = B * PAIRS
CH = 8
TC = NT // CH
EPS = 1e-5
ALPHA, BETA = 0.12, 0.9
VW = D + 1
OW = D + H
VS = OW + D // H


def bc(ap, shape):
    return ap.broadcast_to(shape)


def span(start, n):
    return slice(start, start + n) if isinstance(start, int) else bass.ds(start, n)


class Chain:

    def __init__(self, eng, sem):
        self.eng, self.sem, self.n, self.base = eng, sem, 0, 0

    def __call__(self, ins):
        self.n += 1
        ins.then_inc(self.sem, 1)
        self.eng.wait_ge(self.sem, self.base + self.n)

    def loop(self, body, first, end, per):
        start = self.n
        with self.eng.Fori(first, end) as j:
            self.base = j * per - first * per
            body(j)
            assert self.n - start == per, (self.n - start, per)
            self.base = 0
        self.n = start + per * (end - first)


def tower(nc, x, taps, consts, wq0, wk0, vo, gate_w0, gate_b0, w1_0, b1_0, w2_0, b2_0, gamma,
          wq1, wk1, wv1, wpos, wproj, bproj, router, w1_1, b1_1, w2_1, b2_1, out):
    with ExitStack() as ctx:
        def sb(name, shape, dt=F32):
            return ctx.enter_context(nc.sbuf_tensor(name, shape, dt))

        ps = ctx.enter_context(nc.psum_tensor("ps", [P, 8, 512], F32))
        res = sb("res", [P, NT, D])
        xh = sb("xh", [P, NT, D])
        xT = sb("xT", [D, B + 1, 2 * P])
        cst = sb("cst", [P, consts.shape[1]])
        ident_b = sb("ident_b", [P, P], BF16)
        selm = sb("selm", [P, P], BF16)
        small = sb("small", [P, 4])
        rowsc = sb("rowsc", [P, 3, NT])
        w0 = {"q": sb("wq0s", [D, 2 * P]), "k": sb("wk0s", [D, 2 * P])}
        w1 = {"q": sb("wq1s", [D, 2, 4, 32]), "k": sb("wk1s", [D, 2, 4, 32])}
        vos = sb("vos", [D, H * D])
        wvs, wps = sb("wvs", [D, D]), sb("wps", [P, D])
        bprojb = sb("bprojb", [P, D])
        gb = sb("gb", [P, 2, D])
        posw = sb("posw", [P, 5, H])
        gws = [sb("gws0", [D, 16]), sb("gws1", [D, 8])]
        gbs = sb("gbs", [16, 1])
        b1s = [sb("b1s0", [P, 16]), sb("b1s1", [P, 4])]
        w2s = [sb("w2s0", [P, 16, D]), sb("w2s1", [P, 4, D])]
        wst = [sb("wst0", [P, 3, 16 * P], BF16), sb("wst1", [P, 3, 4 * P], BF16)]
        b2p = [sb("b2p0", [P, 3, D], BF16), sb("b2p1", [P, 3, D], BF16)]
        selb = sb("selb", [P, 16, P], BF16)
        big = sb("big", [P, 8 * 2048])
        mid = sb("mid", [P, 6 * 1024])

        o_id = 0
        o_dft = o_id + P
        o_iota = o_dft + P
        o_dist = o_iota + 16
        o_selm = o_dist + 2 * 256
        o_sel0 = o_selm + P
        o_sel1 = o_sel0 + 16 * P
        ident = cst[:, o_id:o_id + P]
        dft = cst[:, o_dft:o_dft + P]
        iota = cst[:, o_iota:o_iota + 16]
        dist = cst[:, o_dist:o_dist + 512].rearrange("p (t k) -> p t k", t=2)

        held = []

        def sem(name):
            held.append(nc.alloc_semaphore(name))
            return held[-1]

        def phase(program, *args):
            program(*args)
            nc.clear_and_free_semaphores(held)
            held.clear()
            nc.all_engine_barrier()

        def chain(eng, name):
            return Chain(eng, sem(name))

        def tokens():
            sig = mid[:, 0:2 * B * REACH].rearrange("p (t b s) -> p t b s", t=2, b=B)
            tw = mid[:, 640:640 + 2 * TAPS * WIN].rearrange("p (t k j) -> p t k j", t=2, k=TAPS)
            tmp = mid[:, 1280:1280 + 2048].rearrange("p (t b j) -> p t b j", t=2, b=B)
            area = lambda n: big[:, 2048 * n:2048 * (n + 1)].rearrange("p (t b j) -> p t b j", t=2, b=B)
            z, poly, gauss, power = area(0), area(1), area(2), area(3)
            kT = big[:, 8192:8192 + 2048].rearrange("p (g k) -> p g k", g=4)
            spec = lambda n: big[:, 10240 + 1056 * n:10240 + 1056 * (n + 1)].rearrange(
                "p (t b k) -> p t b k", t=2, b=B)
            mag, arg, mask, mt = spec(0), spec(1), spec(2), spec(3)
            low = spec(4)
            top, cap = rowsc[:, 0, :], rowsc[:, 1, :]

            s_sig, s_cst, s_w, s_wz = sem("tok_signal_in"), sem("tok_consts_in"), sem("weights_in"), sem("w_zeroed")
            s_z, s_sq, s_kw = [sem("tok_interp0"), sem("tok_interp1")], sem("tok_window_parts"), sem("tok_kernelled")
            s_tr, s_kT, s_ft, s_pw = sem("tok_turned"), sem("tok_turned_out"), sem("tok_ft"), sem("tok_power")
            s_m2, s_mag, s_arg, s_mask = sem("tok_power_sum"), sem("tok_mag"), sem("tok_arg"), sem("tok_mask")
            s_abs, s_log, s_sm = sem("tok_abs"), sem("tok_log"), sem("tok_small")

            with nc.Block() as block:
                def squares(act, g):
                    nc.scalar.activation(power[:, g // 2, 8 * (g % 2):8 * (g % 2) + 8],
                                         ps[:, 2 + g % 2].rearrange("p (b k) -> p b k", b=8), ACT.Square).then_inc(s_pw, 1)

                def interpolate(eng, ch, t):
                    ch.eng.wait_ge(s_cst, 32)
                    shape = [P, B, HOP, UP]
                    first = lambda k: bc(sig[:, t, :, k:k + HOP].unsqueeze(3), shape)
                    weight = lambda k: bc(tw[:, t, k].rearrange("p (m r) -> p m r", r=UP).unsqueeze(1), shape)
                    zz = z[:, t].rearrange("p b (m r) -> p b m r", r=UP)
                    tt = tmp[:, t].rearrange("p b (m r) -> p b m r", r=UP)
                    ch(eng.tensor_tensor(zz, first(1), weight(1), ALU.mult))
                    for k in range(2, TAPS):
                        ch(eng.tensor_tensor(tt, first(k), weight(k), ALU.mult))
                        ch(eng.tensor_tensor(zz, zz, tt, ALU.add))
                    w = bc(tw[:, t, 0, 0:WIN:UP].unsqueeze(1), [P, B, HOP])
                    ch(eng.tensor_tensor(tt[:, :, :, 0], sig[:, t, :, 0:HOP], w, ALU.mult))
                    return eng.tensor_tensor(zz[:, :, :, 0], zz[:, :, :, 0], tt[:, :, :, 0], ALU.add)

                @block.sync
                def _(sp):
                    sp.dma_start(cst[:], consts).then_inc(s_cst, 16)
                    sp.dma_start(tw, taps).then_inc(s_cst, 16)
                    t0 = x.tensor
                    for b in range(B):
                        sp.dma_start(sig[1:P, 0, b], bass.AP(tensor=t0, offset=b * SIG + HOP - 2,
                                                              ap=[[HOP, P - 1], [1, REACH]])).then_inc(s_sig, 16)
                    sp.dma_start(sig[0:1, 0, :, 2:REACH], bass.AP(tensor=t0, offset=0, ap=[[SIG, 1], [SIG, B], [1, REACH - 2]])).then_inc(s_sig, 16)
                    sp.wait_ge(s_wz, 2)
                    for g in range(2):
                        for w, src in ((w1["q"], wq1), (w1["k"], wk1)):
                            sp.dma_start(w[:, g, :, 0:8], src[:, g]).then_inc(s_w, 16)
                    for dst, src in ((w0["q"][:], wq0), (w0["k"][:], wk0), (vos[:], vo), (wvs[:], wv1), (wps[:], wproj),
                                     (gws[0][:], gate_w0), (gws[1][:], router), (gbs[:], gate_b0),
                                     (b1s[0][:], b1_0), (b1s[1][:], b1_1)):
                        sp.dma_start(dst, src).then_inc(s_w, 16)
                    sp.wait_ge(s_w, 16 * 14)
                    sp.wait_ge(s_cst, 32)

                @block.scalar
                def _(act):
                    act.dma_start(sig[P - 1:P, 1], bass.AP(tensor=x.tensor, offset=HOP * (NW - 1) - 2, ap=[[SIG, 1], [SIG, B], [1, REACH]])).then_inc(s_sig, 16)
                    for b in range(B):
                        act.dma_start(sig[0:P - 1, 1, b], bass.AP(tensor=x.tensor, offset=b * SIG + HOP * P - 2,
                                                                   ap=[[HOP, P - 1], [1, REACH]])).then_inc(s_sig, 16)
                    act.wait_ge(s_sm, 3)
                    for t in (0, 1):
                        act.wait_ge(s_z[t], 1)
                        nc.scalar.activation(poly[:, t], z[:, t], ACT.Square, bias=small[:, 0:1], scale=float(np.sqrt(0.5))).then_inc(s_sq, 1)
                        nc.scalar.activation(gauss[:, t], z[:, t], ACT.Square, bias=small[:, 1:2]).then_inc(s_sq, 1)
                        act.wait_ge(s_sq, 3 * t + 2)
                        nc.scalar.activation(gauss[:, t], gauss[:, t], ACT.Exp, scale=-0.5).then_inc(s_sq, 1)
                    for g in range(4):
                        act.wait_ge(s_tr, g + 1)
                        nc.scalar.activation(kT[:, g], ps[:, g % 2], ACT.Copy).then_inc(s_kT, 1)
                        if g:
                            act.wait_ge(s_ft, g)
                            squares(act, g - 1)
                    act.wait_ge(s_ft, 4)
                    squares(act, 3)
                    act.wait_ge(s_m2, 1)
                    nc.scalar.activation(mag, power[:, :, :, 0:NB], ACT.Sqrt).then_inc(s_mag, 1)
                    act.wait_ge(s_arg, 1)
                    nc.scalar.activation(mask, arg, ACT.Sigmoid).then_inc(s_mask, 1)
                    act.wait_ge(s_abs, 1)
                    nc.scalar.activation(arg, arg, ACT.Abs).then_inc(s_log, 1)
                    act.wait_ge(s_log, 1)
                    nc.scalar.activation(arg, arg, ACT.Exp, scale=-1.0).then_inc(s_log, 1)
                    act.wait_ge(s_log, 2)
                    nc.scalar.activation(arg, arg, ACT.Ln, bias=small[:, 2:3]).then_inc(s_log, 1)

                @block.vector
                def _(dve):
                    link = chain(dve, "tok_dve")
                    nc.vector.memset(small[:, 0:1], 1.3 * float(np.sqrt(0.5))).then_inc(s_sm, 1)
                    nc.vector.memset(small[:, 1:2], -0.7).then_inc(s_sm, 1)
                    nc.vector.memset(small[:, 2:3], 1.0).then_inc(s_sm, 1)
                    dve.wait_ge(s_sig, 16 * (2 * B + 2))
                    link(nc.vector.tensor_copy(sig[0:1, 0, :, 0:2], bc(sig[0:1, 0, :, 2:3], [1, B, 2])))
                    interpolate(nc.vector, link, 0).then_inc(s_z[0], 1)
                    for t in (0, 1):
                        dve.wait_ge(s_sq, 3 * t + 3)
                        nc.vector.scalar_tensor_tensor(out=z[:, t].rearrange("p b j -> p (b j)"), in0=gauss[:, t].rearrange("p b j -> p (b j)"), scalar=0.5,
                                                       in1=poly[:, t].rearrange("p b j -> p (b j)"), op0=ALU.mult, op1=ALU.add).then_inc(s_kw, 1)
                    dve.wait_ge(s_pw, 4)
                    nc.vector.tensor_tensor(power[:, :, :, 1:32], power[:, :, :, 1:32], power[:, :, :, 33:64], ALU.add).then_inc(s_m2, 1)
                    dve.wait_ge(s_mag, 1)
                    flat = lambda a: a.rearrange("p t b k -> p (t b) k")
                    over = lambda a: bc(a.unsqueeze(2), [P, NT, NB])
                    link(nc.vector.tensor_reduce(top, flat(mag), AX.X, ALU.max))
                    link(nc.vector.tensor_scalar(cap, top, -ALPHA, None, ALU.mult))
                    nc.vector.tensor_tensor(flat(arg), flat(mag), over(cap), ALU.add).then_inc(s_arg, 1)
                    dve.wait_ge(s_arg, 1)
                    link(nc.vector.tensor_scalar(cap, top, BETA, None, ALU.mult))
                    dve.wait_ge(s_mask, 1)
                    link(nc.vector.tensor_tensor(flat(mt), flat(mag), flat(mask), ALU.mult))
                    nc.vector.tensor_tensor(flat(arg), flat(mt), over(cap), ALU.subtract).then_inc(s_abs, 1)
                    link(nc.vector.tensor_tensor(flat(low), flat(mt), over(cap), ALU.min))
                    dve.wait_ge(s_log, 3)
                    rows = res[:].rearrange("p (b t) d -> p t b d", t=2)
                    for t in (0, 1):
                        link(nc.vector.tensor_tensor(rows[:, t, :, 0:NB], low[:, t], arg[:, t], ALU.subtract))
                        link(nc.vector.tensor_tensor(rows[:, t, :, NB:WIN], low[:, t, :, NB - 2:0:-1], arg[:, t, :, NB - 2:0:-1], ALU.subtract))

                @block.gpsimd
                def _(pool):
                    link = chain(pool, "tok_pool")
                    nc.gpsimd.memset(w1["q"][:], 0.0).then_inc(s_wz, 1)
                    nc.gpsimd.memset(w1["k"][:], 0.0).then_inc(s_wz, 1)
                    pool.wait_ge(s_sig, 16 * (2 * B + 2))
                    interpolate(nc.gpsimd, link, 1).then_inc(s_z[1], 1)
                    link(nc.gpsimd.memset(xT[:, B], 0.0))
                    link(nc.gpsimd.tensor_copy(ident_b[:], ident))
                    link(nc.gpsimd.tensor_copy(selm[:], cst[:, o_selm:o_selm + P]))

                @block.tensor
                def _(pe):
                    pe.wait_ge(s_cst, 32)
                    for g in range(5):
                        if g < 4:
                            pe.wait_ge(s_kw, g // 2 + 1)
                            if g >= 2:
                                pe.wait_ge(s_kT, g - 1)
                            for c in range(4):
                                pair = z[:, g // 2, 8 * (g % 2) + 2 * c:8 * (g % 2) + 2 * c + 2].rearrange("p b j -> p (b j)")
                                last = nc.tensor.transpose(ps[:, g % 2, P * c:P * c + P], pair, ident)
                            last.then_inc(s_tr, 1)
                        if g:
                            pe.wait_ge(s_kT, g)
                            if g >= 3:
                                pe.wait_ge(s_pw, g - 2)
                            for c in range(4):
                                last = nc.tensor.matmul(ps[:, 2 + (g - 1) % 2, P * c:P * c + P], kT[:, g - 1, P * c:P * c + P], dft, start=True, stop=True)
                            last.then_inc(s_ft, 1)

        def norm_all(tag, after_norm_pe, after_norm_act, after_norm_dve, pool_work=None, sp_work=None, doubled=None):
            sq = mid[:, 0:2048].rearrange("p (t d) -> p t d", t=NT)
            s_xc, s_sq, s_var, s_sd, s_xh = (sem(f"{tag}_{n}") for n in ("centred", "squared", "var", "sd", "normed"))
            half = NT // 2
            mean, var, sd = rowsc[:, 0], rowsc[:, 1], rowsc[:, 2]
            with nc.Block() as block:
                @block.vector
                def _(dve):
                    link = chain(dve, f"{tag}_dve")
                    for n in (0, 1):
                        s = slice(half * n, half * n + half)
                        link(nc.vector.tensor_reduce(mean[:, s], res[:, s], AX.X, ALU.add))
                        link(nc.vector.tensor_scalar(mean[:, s], mean[:, s], -1.0 / D, None, ALU.mult))
                        nc.vector.tensor_tensor(xh[:, s], res[:, s], bc(mean[:, s].unsqueeze(2), [P, half, D]), ALU.add).then_inc(s_xc, 1)
                    for n in (0, 1):
                        s = slice(half * n, half * n + half)
                        dve.wait_ge(s_sq, n + 1)
                        link(nc.vector.tensor_reduce(var[:, s], sq[:, s], AX.X, ALU.add))
                        nc.vector.tensor_scalar(var[:, s], var[:, s], 1.0 / D, EPS, ALU.mult, ALU.add).then_inc(s_var, 1)
                    for n in (0, 1):
                        s = slice(half * n, half * n + half)
                        dve.wait_ge(s_sd, n + 1)
                        link(nc.vector.reciprocal(sd[:, s], sd[:, s]))
                        last = nc.vector.tensor_tensor(xh[:, s], xh[:, s], bc(sd[:, s].unsqueeze(2), [P, half, D]), ALU.mult)
                        if doubled is not None:
                            link(last)
                            last = nc.vector.tensor_copy(doubled[:, s], bc(xh[:, s].unsqueeze(2), [P, half, 2, D]))
                        last.then_inc(s_xh, 1)
                    after_norm_dve(dve, link)

                @block.scalar
                def _(act):
                    for n in (0, 1):
                        act.wait_ge(s_xc, n + 1)
                        s = slice(half * n, half * n + half)
                        nc.scalar.activation(sq[:, s], xh[:, s], ACT.Square).then_inc(s_sq, 1)
                    for n in (0, 1):
                        s = slice(half * n, half * n + half)
                        act.wait_ge(s_var, n + 1)
                        nc.scalar.activation(sd[:, s], var[:, s], ACT.Sqrt).then_inc(s_sd, 1)
                    after_norm_act(act)

                @block.tensor
                def _(pe):
                    after_norm_pe(pe, s_xh)

                if pool_work:
                    @block.gpsimd
                    def _(pool):
                        pool_work(pool)

                if sp_work:
                    @block.sync
                    def _(sp):
                        sp_work(sp)

        def turned(c, bank, src):
            width = src.shape[2]
            for k in range(TC):
                last = nc.tensor.transpose(ps[0:width, bank, P * k:P * k + P], src[:, TC * c + k], ident)
            return last

        def attention_prep0():
            s_tr, s_xT = sem("a0_turned"), sem("a0_xT")
            s_w, s_rest = sem("a0_weights_in"), sem("a0_rest")

            def pe_work(pe, s_xh):
                for c in range(CH):
                    pe.wait_ge(s_xh, c // (CH // 2) + 1)
                    if c >= 2:
                        pe.wait_ge(s_xT, c - 1)
                    turned(c, c % 2, xh[:]).then_inc(s_tr, 1)

            def act_work(act):
                for c in range(CH):
                    act.wait_ge(s_tr, c + 1)
                    nc.scalar.activation(xT[:, 2 * c:2 * c + 2], ps[0:D, c % 2].rearrange("p (b q) -> p b q", b=2), ACT.Copy).then_inc(s_xT, 1)

            def sp_work(sp):
                n = 0
                for dst, src in ((w2s[0][:], w2_0), (w2s[1][:], w2_1), (bprojb[:], bproj), (gb[:], gamma_beta),
                                 (posw[:], pos_in)):
                    sp.dma_start(dst, src).then_inc(s_w, 16)
                    n += 16
                sp.wait_ge(s_w, n)

            norm_all("a0", pe_work, act_work, lambda dve, link: None, None, sp_work)

        gamma_beta = bass.AP(tensor=gamma.tensor, offset=0, ap=[[0, P], [D, 2], [1, D]])
        pos_in = bass.AP(tensor=wpos.tensor, offset=0, ap=[[0, P], [H, 5], [1, H]])
        bproj = bass.AP(tensor=bproj.tensor, offset=0, ap=[[0, P], [1, D]])

        def attention(L):
            scale = D ** -0.5 if L == 0 else (D // H) ** -0.5
            w = w0 if L == 0 else w1
            wl = {n: (w[n][:] if L == 0 else w[n][:].rearrange("p g h d -> p (g h d)")) for n in "qk"}

            pos = [0]
            def take(n, dt=F32):
                a = big[:, pos[0]:pos[0] + n] if pos[0] + n <= 16384 else None
                assert a is not None
                pos[0] += n
                return a
            q32 = [take(512).rearrange("p (g q) -> p g q", g=2) for _ in range(2)]
            k32 = [take(512).rearrange("p (g q) -> p g q", g=2) for _ in range(2)]
            e_sb = [take(1024).rearrange("p (j c q) -> p j c q", j=2, c=2) for _ in range(2)]
            if L == 0:
                val = [take(2 * H * VW).rearrange("p (c v) -> p c v", c=2) for _ in range(2)]
                heads = take(H * 2 * D).rearrange("p (h t d) -> p h t d", h=H, t=2)
            else:
                val = v1pad
            xs = [take(256)[0:D] for _ in range(2)]
            o_rows = VW if L == 0 else OW
            o_sb = [take(512)[0:o_rows] for _ in range(2)]
            work = take(1024)
            mx = work[:, 0:4].rearrange("p (j t) -> p j t", j=2)
            hsum = work[:, 16:16 + 2 * D].rearrange("p (t d) -> p t d", t=2)
            rinv = work[:, 144:160]
            rgate = work[:, 160:176].rearrange("p (t h) -> p t h", t=2)
            asum = work[:, 176:192].rearrange("p (t h) -> p t h", t=2)
            blend = work[:, 192:192 + 2 * D].rearrange("p (t d) -> p t d", t=2)
            oT_sb = work[:, 320:320 + P]
            mt_sb, mhl, q_r, k_r = mt_t[L], mhl_t[L], qr_t, kr_t

            S = ps[:, 0:2].rearrange("p j (t k) -> p j t k", t=2)
            T = ps[:, 2:4].rearrange("p j (c q) -> p j c q", c=2)
            O = ps[:, 4].rearrange("p (j q) -> p j q", j=2)
            PQ, PK = ps[:, 5], ps[:, 6]
            MT = ps[:, 7, 0:P].bitcast(BF16)
            if L == 0:
                OT = ps[:, 7, P:P + 4 * VW].rearrange("p (j t d) -> p j t d", j=2, t=2)
            else:
                OT = ps[:, 7, P:P + 2 * OW].rearrange("p (t d) -> p t d", t=2)

            t = f"L{L}_"
            s_xs, s_qkp, s_qk_act, s_qk_dve = (sem(t + n) for n in ("xs_ready", "qk_projected", "q_in_sbuf", "k_in_sbuf"))
            s_vp, s_v_act, s_v_dve = (sem(t + n) for n in ("v_projected", "v_even", "v_odd"))
            s_S, s_mhl, s_mtp, s_mt = (sem(t + n) for n in ("scores", "max_parts", "max_turned", "max_ready"))
            s_T, s_E, s_PV, s_O, s_OT, s_norm = (sem(t + n) for n in ("turned_scores", "exps", "outputs", "outputs_in_sbuf", "outputs_turned", "normed"))
            s_bl, s_oTp, s_oT, s_y, s_fin = (sem(t + n) for n in ("blended", "blended_turned", "blended_ready", "projected", "added"))
            s_ones = sem(t + "ones")

            def rows(p, j):
                r = 32 * (2 * (p % 2) + j)
                return slice(r, r + 32)

            def at(k):
                return (k // PAIRS) % 2, k % PAIRS

            with nc.Block() as block:
                @block.tensor
                def _(pe):
                    def project(b, par):
                        pe.wait_ge(s_xs, b + 1)
                        if L == 0:
                            if not isinstance(b, int) or b >= 1:
                                pe.wait_ge(s_v_act, b)
                                pe.wait_ge(s_v_dve, b)
                        elif not isinstance(b, int) or b >= 3:
                            pe.wait_ge(s_fin, b - 2)
                        for bank, n in ((PQ, "q"), (PK, "k")):
                            for g in range(2):
                                last = nc.tensor.matmul(bank[:, 256 * g:256 * g + 256], wl[n][:, P * g:P * g + P], xs[par], start=True, stop=True)
                        last.then_inc(s_qkp, 1)

                    def values(b, par):
                        pe.wait_ge(s_qk_act, 2 * (b + 1))
                        pe.wait_ge(s_qk_dve, 2 * (b + 1))
                        for c, bank in ((0, PQ), (1, PK)):
                            last = nc.tensor.matmul(bank, xs[par][:, P * c:P * c + P], vos[:], start=True, stop=True)
                        last.then_inc(s_vp, 1)

                    def scores(par, p):
                        for tq in range(2):
                            for j in range(2):
                                r = rows(p, j)
                                last = nc.tensor.matmul(S[:, j, tq], q_r[par][r, p // 2, P * tq:P * tq + P], k_r[par][r, p // 2], start=True, stop=True)
                        last.then_inc(s_S, 1)

                    def max_turn(k):
                        for tq in range(2):
                            last = nc.tensor.transpose(MT[:, P * tq:P * tq + P], mhl[k % 2][:, tq], ident_b[:])
                        last.then_inc(s_mtp, 1)

                    def turned_scores(k):
                        par, p = at(k)
                        for c in range(2):
                            for j in range(2):
                                r = rows(p, j)
                                nc.tensor.matmul(T[:, j, c], k32[par][r, p // 2, P * c:P * c + P], q32[par][r, p // 2], start=True, stop=False)
                                m = slice(r.start, r.start + 2)
                                last = nc.tensor.matmul(T[:, j, c], selm[m], mt_sb[k % 2][m], start=False, stop=True)
                        last.then_inc(s_T, 1)

                    def outputs(k):
                        par, p = at(k)
                        for j in range(2):
                            h = 2 * p + j
                            for c in range(2):
                                n = P - c
                                if L == 0:
                                    last = nc.tensor.matmul(O[0:VW, j], val[par][0:n, c, VW * h:VW * h + VW], e_sb[k % 2][0:n, j, c], start=(c == 0), stop=(c == 1))
                                else:
                                    last = nc.tensor.matmul(O[0:OW, par], val[par][0:n, c, OW * h:OW * h + OW], e_sb[k % 2][0:n, j, c],
                                                            start=(h == 0 and c == 0), stop=(h == H - 1 and c == 1))
                        last.then_inc(s_PV, 1)

                    def slot(j, k, do=("mt", "s", "pv", "turn", "t", "tail", "proj")):
                        U = 2 * PAIRS * j + k
                        known = isinstance(j, int)
                        par, p = at(k)
                        b = 2 * j + par
                        if "mt" in do:
                            pe.wait_ge(s_mhl, U + 1)
                            if not known or U >= 1:
                                pe.wait_ge(s_mt, U)
                            if L == 0 and (not known or U >= 4):
                                pe.wait_ge(s_norm, U - 3)
                            if L == 1 and p == 3 and (not known or b >= 1):
                                pe.wait_ge(s_bl, b)
                            max_turn(k)
                        if "s" in do:
                            par1, p1 = at(k + 1)
                            if p1 == 0:
                                pe.wait_ge(s_qk_act, 2 * (b + 2))
                                pe.wait_ge(s_qk_dve, 2 * (b + 2))
                            scores(par1, p1)
                        if "pv" in do and (not known or U >= 2):
                            pe.wait_ge(s_E, U - 1)
                            bl = b - 1 if p < 2 else b
                            if L == 0:
                                if p == 2:
                                    pe.wait_ge(s_v_act, bl + 1)
                                    pe.wait_ge(s_v_dve, bl + 1)
                                if not known or U >= 3:
                                    pe.wait_ge(s_O, U - 2)
                            elif p == 2:
                                pe.wait_ge(s_v_act, bl + 1)
                                if not known or bl >= 1:
                                    pe.wait_ge(s_O, bl)
                            outputs(k - 2)
                        if "turn" in do and (not known or U >= 3) and (L == 0 or p == 2) and (L == 0 or not known or b >= 1):
                            if "mt" in do:
                                pe.wait_ge(s_mt, U + 1)
                            if L == 0:
                                if "mt" not in do:
                                    pe.wait_ge(s_norm, U - 3)
                                pe.wait_ge(s_O, U - 2)
                                for jj in range(2):
                                    for tq in range(2):
                                        last = nc.tensor.transpose(OT[:, jj, tq], o_sb[(k + 1) % 2][:, 256 * jj + P * tq:256 * jj + P * tq + P], ident[0:VW, 0:VW])
                            else:
                                pe.wait_ge(s_O, b)
                                for tq in range(2):
                                    last = nc.tensor.transpose(OT[:, tq], o_sb[(par + 1) % 2][:, P * tq:P * tq + P], ident[0:OW, 0:OW])
                            last.then_inc(s_OT, 1)
                        if "t" in do:
                            pe.wait_ge(s_mt, U + 1)
                            if not known or U >= 1:
                                pe.wait_ge(s_E, U)
                            turned_scores(k)
                        if "tail" in do and L == 1:
                            if p == 3 and (not known or b >= 1):
                                pe.wait_ge(s_bl, b)
                                if "proj" in do:
                                    pe.wait_ge(s_qk_act, 2 * (b + 2))
                                    pe.wait_ge(s_qk_dve, 2 * (b + 2))
                                nc.tensor.transpose(PQ[:, 0:P], blend.rearrange("p t d -> p (t d)"), ident).then_inc(s_oTp, 1)
                            if p == 0 and (not known or b >= 2):
                                pe.wait_ge(s_oT, b - 1)
                                for tq in range(2):
                                    r = slice(D * tq, D * tq + D)
                                    last = nc.tensor.matmul(ps[:, 5 + tq, 0:D], oT_sb[r], wps[r], start=True, stop=True)
                                last.then_inc(s_y, 1)
                        if "proj" in do:
                            if p == 1:
                                project(b + 1, (par + 1) % 2)
                            if p == 2 and L == 0:
                                values(b + 1, (par + 1) % 2)

                    project(0, 0)
                    if L == 0:
                        values(0, 0)
                    pe.wait_ge(s_qk_act, 2)
                    pe.wait_ge(s_qk_dve, 2)
                    scores(0, 0)
                    for k in range(2 * PAIRS):
                        slot(0, k)
                    with pe.Fori(1, B // 2) as j:
                        for k in range(2 * PAIRS):
                            slot(j, k)
                    for k in range(5 if L else 3):
                        slot(B // 2, k, ("pv", "turn", "tail") if k < 2 else ("turn", "tail"))

                @block.scalar
                def _(act):
                    def q_out(b, par):
                        act.wait_ge(s_qkp, b + 1)
                        if not isinstance(b, int) or b >= 2:
                            act.wait_ge(s_T, PAIRS * (b - 1))
                        nc.scalar.activation(q32[par].rearrange("p g q -> p (g q)"), PQ, ACT.Copy).then_inc(s_qk_act, 1)
                        nc.scalar.activation(q_r[par][:].rearrange("p g q -> p (g q)"), PQ, ACT.Copy).then_inc(s_qk_act, 1)

                    def v_out(b, par):
                        act.wait_ge(s_vp, b + 1)
                        if not isinstance(b, int) or b >= 2:
                            act.wait_ge(s_PV, PAIRS * (b - 1))
                        nc.scalar.activation(val[par][:, 0].rearrange("p (h d) -> p h d", h=H)[:, :, 0:D],
                                             PQ.rearrange("p (h d) -> p h d", h=H), ACT.Copy).then_inc(s_v_act, 1)

                    def slot(j, k, do=("mt", "e", "o", "proj")):
                        U = 2 * PAIRS * j + k
                        known = isinstance(j, int)
                        par, p = at(k)
                        b = 2 * j + par
                        if "mt" in do:
                            act.wait_ge(s_mtp, U + 1)
                            if not known or U >= 2:
                                act.wait_ge(s_T, U - 1)
                            nc.scalar.activation(mt_sb[k % 2], MT, ACT.Copy).then_inc(s_mt, 1)
                        if "o" in do and L == 0 and (not known or U >= 2):
                            act.wait_ge(s_PV, U - 1)
                            if not known or U >= 4:
                                act.wait_ge(s_OT, U - 3)
                            nc.scalar.activation(o_sb[k % 2], ps[0:VW, 4], ACT.Copy).then_inc(s_O, 1)
                        if "o" in do and L == 1 and p == 1 and (not known or b >= 1):
                            act.wait_ge(s_PV, U - 1)
                            pl = (par + 1) % 2
                            if not known or b >= 3:
                                act.wait_ge(s_OT, b - 2)
                            nc.scalar.activation(o_sb[pl][:, 0:256], O[0:OW, pl], ACT.Copy).then_inc(s_O, 1)
                        if "e" in do:
                            act.wait_ge(s_T, U + 1)
                            if not known or U >= 2:
                                act.wait_ge(s_PV, U - 1)
                            nc.scalar.activation(e_sb[k % 2], T, ACT.Exp, scale=scale).then_inc(s_E, 1)
                        if "o" in do and L == 1 and p == 3 and (not known or b >= 1):
                            act.wait_ge(s_oTp, b)
                            if not known or b >= 2:
                                act.wait_ge(s_y, b - 1)
                            nc.scalar.activation(oT_sb, PQ[:, 0:P], ACT.Copy).then_inc(s_oT, 1)
                        if "proj" in do:
                            if p == 1:
                                q_out(b + 1, (par + 1) % 2)
                            if p == 2 and L == 0:
                                v_out(b + 1, (par + 1) % 2)

                    q_out(0, 0)
                    if L == 0:
                        act.wait_ge(s_ones, 4)
                        v_out(0, 0)
                    for k in range(2 * PAIRS):
                        slot(0, k)
                    with act.Fori(1, B // 2) as j:
                        for k in range(2 * PAIRS):
                            slot(j, k)
                    for k in range(4 if L else 2):
                        slot(B // 2, k, ("o",))

                @block.vector
                def _(dve):
                    link = chain(dve, t + "dve")

                    def k_out(b, par):
                        dve.wait_ge(s_qkp, b + 1)
                        if not isinstance(b, int) or b >= 2:
                            dve.wait_ge(s_T, PAIRS * (b - 1))
                        nc.vector.tensor_copy(k32[par].rearrange("p g q -> p (g q)"), PK).then_inc(s_qk_dve, 1)
                        nc.vector.tensor_copy(k_r[par][:].rearrange("p g q -> p (g q)"), PK).then_inc(s_qk_dve, 1)

                    def v_out(b, par):
                        dve.wait_ge(s_vp, b + 1)
                        if not isinstance(b, int) or b >= 2:
                            dve.wait_ge(s_PV, PAIRS * (b - 1))
                        nc.vector.tensor_copy(val[par][:, 1].rearrange("p (h d) -> p h d", h=H)[:, :, 0:D],
                                              PK.rearrange("p (h d) -> p h d", h=H)).then_inc(s_v_dve, 1)

                    def maxima(U, k):
                        dve.wait_ge(s_S, U + 1)
                        link(nc.vector.tensor_reduce(mx, S[:, :, :, 0:NW], AX.X, ALU.max))
                        if not isinstance(U, int) or U >= 2:
                            dve.wait_ge(s_mtp, U - 1)
                        i = 2 * (k % 2)
                        m = mhl[k % 2][:].rearrange("p t (i c) -> p t i c", i=4)[:, :, i:i + 2]
                        mt = mx.rearrange("p j t -> p t j")
                        link(nc.vector.tensor_copy(m[:, :, :, 0], mt))
                        nc.vector.tensor_tensor(m[:, :, :, 1], mt, m[:, :, :, 0], ALU.subtract).then_inc(s_mhl, 1)
                        dve.wait_ge(s_mhl, U + 1)

                    def slot(j, k, do=("m", "n", "proj")):
                        U = 2 * PAIRS * j + k
                        known = isinstance(j, int)
                        par, p = at(k)
                        b = 2 * j + par
                        if "m" in do:
                            maxima(U + 1, k + 1)
                        if L == 0 and (not known or U >= 3):
                            dve.wait_ge(s_OT, U - 2)
                            _, pl = at(k - 3)
                            r = rinv[:, 0:4].rearrange("p (j t) -> p j t", j=2)
                            link(nc.vector.reciprocal(r, OT[:, :, :, D]))
                            nc.vector.tensor_tensor(heads[:, 2 * pl:2 * pl + 2], OT[:, :, :, 0:D], bc(r.unsqueeze(3), [P, 2, 2, D]), ALU.mult).then_inc(s_norm, 1)
                            dve.wait_ge(s_norm, U - 2)
                            if p == 2 and (not known or b >= 1):
                                link(nc.vector.tensor_reduce(hsum, heads.rearrange("p h t d -> p t d h"), AX.X, ALU.add))
                                rs = res[:, span(2 * (b - 1), 2)]
                                link(nc.vector.tensor_tensor(rs, rs, hsum, ALU.add))
                        if L == 1:
                            if p == 2 and (not known or b >= 1):
                                dve.wait_ge(s_OT, b)
                                r = rinv.rearrange("p (t h) -> p t h", t=2)
                                l = OT[:, :, D:OW]
                                link(nc.vector.reciprocal(r, l))
                                link(nc.vector.tensor_tensor(rgate, r, bc(omg.unsqueeze(1), [P, 2, H]), ALU.mult))
                                link(nc.vector.tensor_tensor(asum, l, rgate, ALU.mult))
                                link(nc.vector.tensor_tensor(asum, asum, gsum, ALU.add))
                                link(nc.vector.reciprocal(asum, asum))
                                shape = [P, 2, H, D // H]
                                by_head = lambda a: a.rearrange("p t (h d) -> p t h d", h=H)
                                if not known or b >= 2:
                                    dve.wait_ge(s_oTp, b - 1)
                                link(nc.vector.tensor_tensor(by_head(blend), by_head(OT[:, :, 0:D]), bc(rgate.unsqueeze(3), shape), ALU.mult))
                                link(nc.vector.tensor_tensor(blend, blend, posv[:, :, b - 1], ALU.add))
                                nc.vector.tensor_tensor(by_head(blend), by_head(blend), bc(asum.unsqueeze(3), shape), ALU.mult).then_inc(s_bl, 1)
                                dve.wait_ge(s_bl, b)
                            if p == 0 and (not known or b >= 2):
                                dve.wait_ge(s_y, b - 1)
                                y = ps[:, 5:7, 0:D]
                                link(nc.vector.tensor_tensor(hsum, y, bc(bprojb[:].unsqueeze(1), [P, 2, D]), ALU.add))
                                rs = res[:, span(2 * (b - 2), 2)]
                                nc.vector.tensor_tensor(rs, rs, hsum, ALU.add).then_inc(s_fin, 1)
                                dve.wait_ge(s_fin, b - 1)
                        if "proj" in do:
                            if p == 1:
                                k_out(b + 1, (par + 1) % 2)
                            if p == 2 and L == 0:
                                v_out(b + 1, (par + 1) % 2)

                    k_out(0, 0)
                    for n in range(2):
                        link(nc.vector.memset(mhl[n][:], 0.0))
                    if L == 0:
                        for par in range(2):
                            for c in range(2):
                                nc.vector.memset(val[par][:, c, D:H * VW:VW], 1.0).then_inc(s_ones, 1)
                        v_out(0, 0)
                    maxima(0, 0)
                    for k in range(2 * PAIRS):
                        slot(0, k)
                    per = 2 * (4 * 2 + 4 + 2) if L == 0 else 2 * (4 * 2 + 7 + 1)
                    link.loop(lambda j: [slot(j, k) for k in range(2 * PAIRS)], 1, B // 2, per)
                    for k in range(5 if L else 3):
                        slot(B // 2, k, ("n",))

                @block.gpsimd
                def _(pool):
                    def fetch(b, par):
                        if not isinstance(b, int) or b >= 2:
                            pool.wait_ge(s_vp if L == 0 else s_qkp, b - 1)
                        nc.gpsimd.tensor_copy(xs[par], xT[:, b]).then_inc(s_xs, 1)
                        if L == 1:
                            if not isinstance(b, int) or b >= 2:
                                pool.wait_ge(s_PV, PAIRS * (b - 1))
                            for c in range(2):
                                last = nc.gpsimd.tensor_copy(v1own[par][:, c, :, 0:D // H],
                                                             vall[:, 2 * b + c].rearrange("p (h d) -> p h d", h=H))
                                if c == 1:
                                    last.then_inc(s_v_act, 1)

                    fetch(0, 0)
                    fetch(1, 1)
                    with pool.Fori(1, B // 2) as j:
                        fetch(2 * j, 0)
                        fetch(2 * j + 1, 1)
                    pool.wait_ge(s_vp if L == 0 else s_qkp, B - 1)
                    nc.gpsimd.tensor_copy(xs[0], xT[:, B]).then_inc(s_xs, 1)
                    if L == 0:
                        pool_setup(pool)

        mt_t = [[sb(f"mt{n}", [P, 256], BF16)[:] for n in range(2)]] * 2
        mhl_t = [[sb(f"mhl{n}", [P, 2, P], BF16) for n in range(2)]] * 2
        qr_t = [sb(f"qr{n}", [P, 2, 256], F32R) for n in range(2)]
        kr_t = [sb(f"kr{n}", [P, 2, 256], F32R) for n in range(2)]

        vall = xh
        v1flat = [mid[:, 0:1280].rearrange("p (c v) -> p c v", c=2), mid[:, 1280:2560].rearrange("p (c v) -> p c v", c=2)]
        v1pad = v1flat
        v1own = [v.rearrange("p c (h s) -> p c h s", h=H) for v in v1flat]
        posv = mid[:, 2560:2560 + 2048].rearrange("p (t b d) -> p t b d", t=2, b=B)
        gsum = mid[:, 4608:4624].rearrange("p (t h) -> p t h", t=2)
        omg = mid[:, 4624:4632]

        def pool_setup(pool):
            link = chain(pool, "setup_pool")
            s_in = sem("setup_in")
            stage = mid
            link(nc.gpsimd.memset(b2p[0][:], 0.0))
            link(nc.gpsimd.memset(b2p[1][:], 0.0))
            for L, (wsrc, n) in enumerate(((w1_0, 2048), (w1_1, 512))):
                E3 = 48 if L == 0 else 24
                raw, rest = stage[:, 0:n], stage[:, 2048:2048 + n]
                pool.dma_start(raw, wsrc).then_inc(s_in, 16)
                pool.dma_start(stage[0:E3, 4096:4096 + D], (b2_0, b2_1)[L]).then_inc(s_in, 16)
                pool.wait_ge(s_in, 32 * (L + 1))
                hi, md, lo = (wst[L][:, s] for s in range(3))
                link(nc.gpsimd.tensor_copy(hi, raw))
                link(nc.gpsimd.tensor_tensor(rest, raw, hi, ALU.subtract))
                link(nc.gpsimd.tensor_copy(md, rest))
                link(nc.gpsimd.tensor_tensor(lo[0:D], rest[0:D], md[0:D], ALU.subtract))
                link(nc.gpsimd.tensor_copy(lo[D:P], hi[D:P]))
                raw, rest = stage[0:E3, 4096:4096 + D], stage[0:E3, 4160:4160 + D]
                hi, md, lo = (b2p[L][0:E3, s] for s in range(3))
                link(nc.gpsimd.tensor_copy(hi, raw))
                link(nc.gpsimd.tensor_tensor(rest, raw, hi, ALU.subtract))
                link(nc.gpsimd.tensor_copy(md, rest))
                link(nc.gpsimd.tensor_tensor(lo, rest, md, ALU.subtract))

        xa = big[:, 0:2048].bitcast(BF16).rearrange("p (c q) -> p c q", c=CH)
        xb = big[:, 2048:4096].bitcast(BF16).rearrange("p (c q) -> p c q", c=CH)
        ct = big[:, 4096:6144].bitcast(BF16).rearrange("p (c q) -> p c q", c=CH)
        mo = big[:, 6144:16384]

        def experts_prep(L):
            E = 16 if L == 0 else 8
            t = f"m{L}_"
            rest = [mo[:, 512 * n:512 * n + 512] for n in range(2)]
            lt = [mo[0:E, 1024 + 512 * n:1536 + 512 * n] for n in range(2)]
            lg = mo[:, 2048:2048 + NT * E].rearrange("p (t e) -> p t e", t=NT)
            v8 = mo[:, 2560:2816].rearrange("p (t e) -> p t e", t=NT)
            i8 = mo[:, 2816:3072].bitcast(U32).rearrange("p (t e) -> p t e", t=NT)
            idx = mo[:, 3072:3136].rearrange("p (e t) -> p e t", e=2)
            wts = mo[:, 3136:3136 + 4 * NT].rearrange("p (e t) -> p e t", e=4)
            comb = mo[:, 3328:3328 + NT * E].rearrange("p (t e) -> p t e", t=NT)
            pick = mo[:, 3840:3840 + NT * E].rearrange("p (t e) -> p t e", t=NT)
            c3 = mo[:, 4352:4352 + NT * 3 * E // 2].bitcast(BF16).rearrange("p (t s e) -> p t s e", t=NT, s=3)

            x2 = mo[:, 5120:5120 + NT * 2 * D].rearrange("p (t a d) -> p t a d", t=NT, a=2)
            s_tr, s_x, s_xt, s_xr, s_xp = (sem(t + n) for n in ("turned", "x_hi", "x_full", "x_rest", "x_parts"))
            s_lg, s_lt, s_lp, s_lc = (sem(t + n) for n in ("logits", "logits_biased", "logits_turned", "logits_ready"))
            s_dv, s_ex, s_c3, s_ctp, s_ct, s_sel, s_rt = (sem(t + n) for n in ("gap", "gap_exp", "parts", "weights_turned", "weights_ready", "selectors", "retired"))
            n_sel = 16 if L == 0 else 4
            o_sel = o_sel0 if L == 0 else o_sel1
            E3 = 3 * E

            def pe_work(pe, s_xh):
                for c in range(CH + 2):
                    if c < CH:
                        pe.wait_ge(s_xh, c // (CH // 2) + 1)
                        if c >= 2:
                            pe.wait_ge(s_xt, 2 * (c - 1))
                            pe.wait_ge(s_xr, c - 1)
                        turned(c, c % 2, x2.rearrange("p t a d -> p t (a d)")).then_inc(s_tr, 1)
                    if 1 <= c <= CH:
                        d = c - 1
                        pe.wait_ge(s_xt, 2 * d + 2)
                        if d >= 2:
                            pe.wait_ge(s_lt, d - 1)
                        nc.tensor.matmul(ps[0:E, 2 + d % 2], gws[L][:], xT[:, 2 * d:2 * d + 2].rearrange("p b q -> p (b q)"), start=True, stop=True).then_inc(s_lg, 1)
                    if c >= 2:
                        d = c - 2
                        pe.wait_ge(s_lt, d + 1)
                        if d >= 2:
                            pe.wait_ge(s_lc, d - 1)
                        for k in range(TC):
                            last = nc.tensor.transpose(ps[:, 4 + d % 2, E * k:E * k + E], lt[d % 2][:, P * k:P * k + P], ident[0:E, 0:E])
                        last.then_inc(s_lp, 1)
                pe.wait_ge(s_c3, 1)
                for c in range(CH):
                    if c >= 2:
                        pe.wait_ge(s_ct, c - 1)
                    bank = ps[0:E3, 6 + c % 2, 0:256].bitcast(BF16)
                    for k in range(TC):
                        last = nc.tensor.transpose(bank[:, P * k:P * k + P], c3[:, TC * c + k].rearrange("p s e -> p (s e)"), ident_b[:])
                    last.then_inc(s_ctp, 1)

            def act_work(act):
                for c in range(CH + 1):
                    if c < CH:
                        act.wait_ge(s_tr, c + 1)
                        nc.scalar.activation(xa[:, c], ps[:, c % 2], ACT.Copy).then_inc(s_x, 1)
                        nc.scalar.activation(xb[0:D, c], ps[0:D, c % 2], ACT.Copy).then_inc(s_xt, 1)
                        nc.scalar.activation(xT[:, 2 * c:2 * c + 2], ps[0:D, c % 2].rearrange("p (b q) -> p b q", b=2), ACT.Copy).then_inc(s_xt, 1)
                    if c >= 1:
                        d = c - 1
                        act.wait_ge(s_lg, d + 1)
                        if d >= 2:
                            act.wait_ge(s_lp, d - 1)
                        if L == 0:
                            nc.scalar.activation(lt[d % 2], ps[0:E, 2 + d % 2], ACT.Identity, bias=gbs[0:E]).then_inc(s_lt, 1)
                        else:
                            nc.scalar.activation(lt[d % 2], ps[0:E, 2 + d % 2], ACT.Copy).then_inc(s_lt, 1)
                act.wait_ge(s_dv, 1)
                nc.scalar.activation(wts[:, 0], wts[:, 0], ACT.Exp).then_inc(s_ex, 1)
                for c in range(CH):
                    act.wait_ge(s_ctp, c + 1)
                    if c == 0:
                        act.wait_ge(s_sel, 1)
                    nc.scalar.activation(ct[0:E3, c], ps[0:E3, 6 + c % 2, 0:256].bitcast(BF16), ACT.Copy).then_inc(s_ct, 1)

            def dve_work(dve, link):
                nc.vector.memset(ct, 0.0).then_inc(s_sel, 1)
                for c in range(CH + 2):
                    if c < CH:
                        dve.wait_ge(s_xt, 2 * c + 2)
                        r = rest[c % 2][D:P]
                        nc.vector.tensor_tensor(r, ps[D:P, c % 2], xa[D:P, c], ALU.subtract).then_inc(s_xr, 1)
                        dve.wait_ge(s_xr, c + 1)
                        link(nc.vector.tensor_copy(xa[D:P, c], r))
                        link(nc.vector.tensor_tensor(xb[D:P, c], r, xa[D:P, c], ALU.subtract))
                    if c >= 2:
                        d = c - 2
                        dve.wait_ge(s_lp, d + 1)
                        nc.vector.tensor_copy(lg[:, TC * d:TC * d + TC], ps[:, 4 + d % 2, 0:TC * E].rearrange("p (t e) -> p t e", t=TC)).then_inc(s_lc, 1)
                dve.wait_ge(s_lc, CH)
                for n in range(NT):
                    last = nc.vector.max(v8[:, n], lg[:, n])
                link(last)
                for n in range(NT):
                    last = nc.vector.max_index(i8[:, n], v8[:, n], lg[:, n])
                link(last)
                nc.vector.tensor_tensor(wts[:, 0], v8[:, :, 1], v8[:, :, 0], ALU.subtract).then_inc(s_dv, 1)
                link(nc.vector.tensor_copy(idx.rearrange("p e t -> p t e"), i8[:, :, 0:2]))
                dve.wait_ge(s_ex, 1)
                link(nc.vector.tensor_scalar(wts[:, 1], wts[:, 0], 1.0, None, ALU.add))
                link(nc.vector.reciprocal(wts[:, 2], wts[:, 1]))
                link(nc.vector.tensor_tensor(wts[:, 3], wts[:, 0], wts[:, 2], ALU.mult))
                shape = [P, NT, E]
                for n, dst in ((0, comb), (1, pick)):
                    link(nc.vector.tensor_tensor(dst, bc(iota[:, 0:E].unsqueeze(1), shape), bc(idx[:, n].unsqueeze(2), shape), ALU.is_equal))
                    link(nc.vector.tensor_tensor(dst, dst, bc(wts[:, 2 + n].unsqueeze(2), shape), ALU.mult))
                link(nc.vector.tensor_tensor(comb, comb, pick, ALU.add))
                link(nc.vector.tensor_copy(c3[:, :, 0], comb))
                link(nc.vector.tensor_tensor(pick, comb, c3[:, :, 0], ALU.subtract))
                link(nc.vector.tensor_copy(c3[:, :, 1], pick))
                nc.vector.tensor_tensor(c3[:, :, 2], pick, c3[:, :, 1], ALU.subtract).then_inc(s_c3, 1)

            def pool_work(pool):
                link = chain(pool, t + "pool")
                link(nc.gpsimd.memset(selb[:], 0.0))
                link(nc.gpsimd.tensor_copy(selb[0:E3, 0:n_sel].rearrange("p e f -> p (e f)"), cst[0:E3, o_sel:o_sel + n_sel * P]))

            norm_all(t + "n", pe_work, act_work, dve_work, pool_work, doubled=x2)

        def experts(L):
            NS = 16 if L == 0 else 4
            t = f"e{L}_"
            func = ACT.Relu if L == 0 else ACT.Gelu
            DEEP = 4
            hid = [mo[:, 512 * n:512 * n + 512] for n in range(DEEP)]
            wgt = [mo[:, 2048 + 512 * n:2560 + 512 * n] for n in range(DEEP)]
            y_sb = mo[0:D, 4096:4608]
            yy = mo[:, 4608:4864].rearrange("p (t d) -> p t d", t=TC)
            yq = mo[:, 4864:5120].rearrange("p (t d) -> p t d", t=TC)
            st = mo[:, 5120:5136].rearrange("p (s t) -> p s t", s=4)
            nh = mo[:, 5136:5140]
            s_h, s_hid, s_cb, s_wgt, s_w2, s_y = (sem(t + n) for n in ("hidden", "activated", "weights_spread", "weighted", "second_done", "summed"))
            s_ysb, s_yt, s_fin, s_var, s_rs, s_out, s_nh = (sem(t + n) for n in ("sum_in_sbuf", "sum_turned", "added", "var", "rsd", "stored", "half"))
            H1, CB, Y, YT = (lambda e: ps[:, e % 2]), (lambda e: ps[:, 2 + e % 2]), ps[0:D, 4], ps[:, 5]
            LAG = 3
            read_at, turn_at, add_at = (3, 5, 6) if L == 0 else (2, 3, 3)

            with nc.Block() as block:
                @block.tensor
                def _(pe):
                    def second(c, e, s):
                        if e == 0:
                            if not isinstance(c, int) or c >= 1:
                                pe.wait_ge(s_ysb, c)
                        pe.wait_ge(s_wgt, s + 1)
                        last = nc.tensor.matmul(Y, w2s[L][:, e], wgt[e % DEEP], start=(e == 0), stop=(e == NS - 1))
                        if e == 0:
                            for n in range(3):
                                last = nc.tensor.matmul(Y, b2p[L][:, n], ct[:, c], start=False, stop=False)
                        last.then_inc(s_w2, 1)

                    def turn(c):
                        for k in range(TC):
                            last = nc.tensor.transpose(YT[:, D * k:D * k + D], y_sb[:, P * k:P * k + P], ident[0:D, 0:D])
                        last.then_inc(s_yt, 1)

                    def chunk(c):
                        known = isinstance(c, int)
                        for e in range(NS):
                            s = NS * c + e
                            if not known or s >= 2:
                                pe.wait_ge(s_hid, s - 1)
                            for n, src in enumerate((xa, xa, xb)):
                                last = nc.tensor.matmul(H1(e), wst[L][:, n, P * e:P * e + P], src[:, c], start=(n == 0), stop=(n == 2))
                            last.then_inc(s_h, 1)
                            if not known or s >= 2:
                                pe.wait_ge(s_wgt, s - 1)
                            nc.tensor.matmul(CB(e), selb[:, e], ct[:, c], start=True, stop=True).then_inc(s_cb, 1)
                            turning = e == turn_at and (not known or c >= 1)
                            if turning:
                                pe.wait_ge(s_ysb, c)
                                if not known or c >= 2:
                                    pe.wait_ge(s_fin, c - 1)
                            if not known or s >= LAG:
                                if e >= LAG:
                                    second(c, e - LAG, s - LAG)
                                else:
                                    second(c - 1, e - LAG + NS, s - LAG)
                            if turning:
                                turn(c - 1)

                    chunk(0)
                    with pe.Fori(1, CH) as c:
                        chunk(c)
                    for e in range(NS - LAG, NS):
                        second(CH - 1, e, NS * (CH - 1) + e)
                    pe.wait_ge(s_ysb, CH)
                    pe.wait_ge(s_fin, CH - 1)
                    turn(CH - 1)

                @block.scalar
                def _(act):
                    def y_out(c):
                        act.wait_ge(s_w2, NS * (c + 1))
                        if not isinstance(c, int) or c >= 1:
                            act.wait_ge(s_yt, c)
                        nc.scalar.activation(y_sb, Y, ACT.Copy).then_inc(s_ysb, 1)

                    def chunk(c):
                        known = isinstance(c, int)
                        for e in range(NS):
                            s = NS * c + e
                            act.wait_ge(s_h, s + 1)
                            if not known or s >= DEEP:
                                act.wait_ge(s_wgt, s + 1 - DEEP)
                            nc.scalar.activation(hid[e % DEEP], H1(e), func, bias=b1s[L][:, e:e + 1]).then_inc(s_hid, 1)
                            if e == read_at and (not known or c >= 1):
                                y_out(c - 1)

                    chunk(0)
                    with act.Fori(1, CH) as c:
                        chunk(c)
                    y_out(CH - 1)

                @block.vector
                def _(dve):
                    link = chain(dve, t + "dve")

                    def finish(c):
                        y = YT[:, 0:TC * D].rearrange("p (t d) -> p t d", t=TC)
                        tl = span(TC * c, TC)
                        shape = [P, TC, D]

                        def total():
                            dve.wait_ge(s_yt, c + 1)
                            link(nc.vector.tensor_tensor(yy, y, xh[:, tl], ALU.add))

                        def mean():
                            link(nc.vector.tensor_reduce(st[:, 0], yy, AX.X, ALU.add))
                            link(nc.vector.tensor_scalar(st[:, 0], st[:, 0], -1.0 / D, None, ALU.mult))

                        def centre():
                            link(nc.vector.tensor_tensor(yy, yy, bc(st[:, 0].unsqueeze(2), shape), ALU.add))

                        def square():
                            link(nc.vector.tensor_tensor(yq, yy, yy, ALU.mult))

                        def variance():
                            link(nc.vector.tensor_reduce(st[:, 1], yq, AX.X, ALU.add))
                            nc.vector.tensor_scalar(st[:, 2], st[:, 1], 1.0 / D, EPS, ALU.mult, ALU.add).then_inc(s_var, 1)

                        def scale():
                            dve.wait_ge(s_rs, c + 1)
                            link(nc.vector.tensor_tensor(yy, yy, bc(st[:, 3].unsqueeze(2), shape), ALU.mult))

                        def gain():
                            link(nc.vector.tensor_tensor(yy, yy, bc(gb[:, 0].unsqueeze(1), shape), ALU.mult))

                        def shift():
                            link(nc.vector.tensor_tensor(yy, yy, bc(gb[:, 1].unsqueeze(1), shape), ALU.add))

                        def add():
                            nc.vector.tensor_tensor(res[:, tl], res[:, tl], yy, ALU.add).then_inc(s_fin, 1)
                            dve.wait_ge(s_fin, c + 1)

                        if L == 1:
                            return [total, add]
                        return [total, mean, centre, square, variance, lambda: None, scale, gain, shift, add]

                    def chunk(c):
                        known = isinstance(c, int)
                        for e in range(NS):
                            s = NS * c + e
                            dve.wait_ge(s_hid, s + 1)
                            dve.wait_ge(s_cb, s + 1)
                            if not known or s >= DEEP:
                                dve.wait_ge(s_w2, s + 1 - DEEP)
                            nc.vector.tensor_tensor(wgt[e % DEEP], hid[e % DEEP], CB(e), ALU.mult).then_inc(s_wgt, 1)
                            if not known or c >= 1:
                                steps = finish(c - 1)
                                n = e - add_at
                                for step in (steps[n:n + 1] if L == 0 else steps) if n >= 0 else ():
                                    step()

                    nc.vector.memset(nh, -0.5).then_inc(s_nh, 1)
                    chunk(0)
                    link.loop(chunk, 1, CH, 9 if L == 0 else 1)
                    for step in finish(CH - 1):
                        step()

                if L == 0:
                    @block.gpsimd
                    def _(pool):
                        pool.wait_ge(s_nh, 1)

                        def rsd(c):
                            pool.wait_ge(s_var, c + 1)
                            nc.gpsimd.tensor_tensor(st[:, 3], st[:, 2], nh, ALU.pow).then_inc(s_rs, 1)

                        with pool.Fori(0, CH) as c:
                            rsd(c)
                else:
                    @block.sync
                    def _(sp):
                        def store(c):
                            sp.wait_ge(s_fin, c + 1)
                            for tq in range(2):
                                n = P - tq
                                src = res[0:n].rearrange("p (b t) d -> p b t d", t=2)
                                sp.dma_start(out[bass.ds(2 * c, 2), P * tq:P * tq + n].rearrange("b w d -> w b d"),
                                             src[:, bass.ds(2 * c, 2), tq]).then_inc(s_out, 16)

                        with sp.Fori(0, CH) as c:
                            store(c)
                        sp.wait_ge(s_out, 16 * 2 * CH)

        def attention_prep1():
            sco = big[:, 0:4096].rearrange("p (t h k) -> p t h k", t=2, h=H)
            d2 = big[:, 4096:4608].rearrange("p (t k) -> p t k", t=2)
            term = big[:, 4608:5120].rearrange("p (t k) -> p t k", t=2)
            posT = big[:, 5120:5120 + 4096].rearrange("p (h c q) -> p h c q", h=H, c=2)
            st = big[:, 9216:9216 + 128]
            pmax = st[:, 0:16].rearrange("p (t h) -> p t h", t=2)
            psum = st[:, 16:32].rearrange("p (t h) -> p t h", t=2)
            pinv = st[:, 32:48].rearrange("p (t h) -> p t h", t=2)
            zb = st[:, 48:56]
            gt = st[:, 56:64]
            s_tr, s_xT, s_v, s_vo = (sem("a1_" + n) for n in ("turned", "xT", "values", "values_out"))
            s_sco, s_max, s_exp, s_inv, s_g, s_g1 = (sem("a1_" + n) for n in ("pos_scores", "pos_max", "pos_exp", "pos_scale", "gate_exp", "gate"))
            s_pt, s_ptc, s_pv, s_pvo, s_pad = (sem("a1_" + n) for n in ("pos_turned", "pos_turned_out", "pos_values", "pos_values_out", "padded"))

            def pe_work(pe, s_xh):
                for c in range(CH + 1):
                    if c < CH:
                        pe.wait_ge(s_xh, c // (CH // 2) + 1)
                        if c >= 2:
                            pe.wait_ge(s_xT, c - 1)
                        turned(c, c % 2, xh[:]).then_inc(s_tr, 1)
                    if c >= 1:
                        d = c - 1
                        pe.wait_ge(s_xT, d + 1)
                        if d >= 2:
                            pe.wait_ge(s_vo, d - 1)
                        for k in range(TC):
                            last = nc.tensor.matmul(ps[:, 2 + d % 2, D * k:D * k + D], xT[:, 2 * d + k // 2, P * (k % 2):P * (k % 2) + P], wvs[:], start=True, stop=True)
                        last.then_inc(s_v, 1)
                for h in range(H):
                    pe.wait_ge(s_exp, 16)
                    if h >= 2:
                        pe.wait_ge(s_ptc, h - 1)
                    for c in range(2):
                        for tq in range(2):
                            last = nc.tensor.transpose(ps[:, h % 2, 256 * c + P * tq:256 * c + P * tq + P], sco[:, tq, h, P * c:P * c + P], ident)
                    last.then_inc(s_pt, 1)
                pe.wait_ge(s_ptc, H)
                pe.wait_ge(s_vo, CH)
                v = vall[:].rearrange("p (b c) (h d) -> p b c h d", c=2, h=H)
                for tq in range(2):
                    for g in range(2):
                        for hh in range(4):
                            h = 4 * g + hh
                            for c in range(2):
                                n = P - c
                                last = nc.tensor.matmul(ps[:, 4 + 2 * tq + g, P * hh:P * hh + P], posT[0:n, h, c, P * tq:P * tq + P], v[0:n, :, c, h],
                                                        start=(c == 0), stop=(c == 1))
                        last.then_inc(s_pv, 1)

            def act_work(act):
                for c in range(CH):
                    act.wait_ge(s_tr, c + 1)
                    nc.scalar.activation(xT[:, 2 * c:2 * c + 2], ps[0:D, c % 2].rearrange("p (b q) -> p b q", b=2), ACT.Copy).then_inc(s_xT, 1)
                nc.scalar.activation(gt, posw[:, 4], ACT.Exp, scale=-1.0).then_inc(s_g, 1)
                act.wait_ge(s_max, 1)
                for tq in range(2):
                    for h in range(H):
                        nc.scalar.activation(sco[:, tq, h], sco[:, tq, h], ACT.Exp, bias=pmax[:, tq, h:h + 1]).then_inc(s_exp, 1)
                for h in range(H):
                    act.wait_ge(s_pt, h + 1)
                    nc.scalar.activation(posT[:, h], ps[:, h % 2].rearrange("p (c q) -> p c q", c=2), ACT.Copy).then_inc(s_ptc, 1)

            def dve_work(dve, link):
                dve.wait_ge(s_sco, 1)
                link(nc.vector.tensor_reduce(pmax, sco[:, :, :, 0:NW], AX.X, ALU.max))
                nc.vector.tensor_scalar(pmax, pmax, -1.0, None, ALU.mult).then_inc(s_max, 1)
                for c in range(CH):
                    dve.wait_ge(s_v, c + 1)
                    nc.vector.tensor_copy(vall[:, TC * c:TC * c + TC], ps[:, 2 + c % 2, 0:TC * D].rearrange("p (t d) -> p t d", t=TC)).then_inc(s_vo, 1)
                dve.wait_ge(s_g, 1)
                link(nc.vector.tensor_scalar(gt, gt, 1.0, None, ALU.add))
                link(nc.vector.reciprocal(gt, gt))
                link(nc.vector.tensor_scalar(omg, gt, -1.0, 1.0, ALU.mult, ALU.add))
                dve.wait_ge(s_exp, 16)
                link(nc.vector.tensor_reduce(psum, sco[:, :, :, 0:NW], AX.X, ALU.add))
                link(nc.vector.reciprocal(pinv, psum))
                link(nc.vector.tensor_tensor(pinv, pinv, bc(gt.unsqueeze(1), [P, 2, H]), ALU.mult))
                link(nc.vector.tensor_tensor(gsum, psum, pinv, ALU.mult))
                for tq in range(2):
                    for g in range(2):
                        dve.wait_ge(s_pv, 2 * tq + g + 1)
                        for hh in range(4):
                            h = 4 * g + hh
                            link(nc.vector.tensor_scalar(posv[:, tq, :, 8 * h:8 * h + 8], ps[:, 4 + 2 * tq + g, P * hh:P * hh + P].rearrange("p (b d) -> p b d", b=B),
                                                         pinv[:, tq, h:h + 1], None, ALU.mult))

            def pool_work(pool):
                link = chain(pool, "a1_pool")
                link(nc.gpsimd.tensor_tensor(d2, dist, dist, ALU.mult))
                link(nc.gpsimd.tensor_scalar(zb, posw[:, 1], 0.0, None, ALU.mult))
                link(nc.gpsimd.tensor_tensor(zb, zb, posw[:, 3], ALU.add))
                for h in range(H):
                    link(nc.gpsimd.tensor_scalar(term, dist, posw[:, 0, h:h + 1], None, ALU.mult))
                    link(nc.gpsimd.tensor_scalar(sco[:, :, h], d2, posw[:, 2, h:h + 1], zb[:, h:h + 1], ALU.mult, ALU.add))
                    link(nc.gpsimd.tensor_tensor(sco[:, :, h], sco[:, :, h], term, ALU.add))
                nc.gpsimd.memset(sco[:, :, :, NW:NW + 1], -1e30).then_inc(s_sco, 1)

            norm_all("a1", pe_work, act_work, dve_work, pool_work)

            with nc.Block() as block:
                @block.gpsimd
                def _(pool):
                    link = chain(pool, "a1_pad")
                    for n in range(2):
                        link(nc.gpsimd.memset(v1flat[n], 0.0))
                        link(nc.gpsimd.memset(v1flat[n][:, :, D:H * OW:OW + 1], 1.0))

        phase(tokens)
        phase(attention_prep0)
        phase(attention, 0)
        phase(experts_prep, 0)
        phase(experts, 0)
        phase(attention_prep1)
        phase(attention, 1)
        phase(experts_prep, 1)
        phase(experts, 1)


def tap_table():
    f = np.float32
    n = (SIG - 1) * UP + 1
    pos = (np.arange(n, dtype=f) / f(n - 1)) * f(SIG - 1)
    i0 = np.floor(pos)
    frac = (pos - i0).astype(f)
    A = f(-0.75)
    table = np.zeros((2 * P, TAPS, WIN), f)
    for k in range(-1, 3):
        at = np.abs(frac - f(k)).astype(f)
        near = ((A + f(2)) * at - (A + f(3))) * at * at + f(1)
        far = ((A * at - f(5) * A) * at + f(8) * A) * at - f(4) * A
        wk = np.where(at <= 1, near, np.where(at < 2, far, f(0))).astype(f)
        for p in range(NW * WIN):
            w, j = divmod(p, WIN)
            o = int(i0[p]) + k - (HOP * w + j // UP)
            assert -2 <= o <= 2 and (o > -2 or j % UP == 0)
            table[w, o + 2, j] += wk[p]
    table[NW] = table[NW - 1]
    return np.ascontiguousarray(table.reshape(2, P, TAPS, WIN).transpose(1, 0, 2, 3))


def constant_table():
    f = np.float32
    ident = np.eye(P, dtype=f)
    n, k = np.arange(WIN)[:, None], np.arange(WIN)[None, :]
    ang = 2 * np.pi * n / WIN
    cols = np.where(k < NB, np.cos(ang * k), np.sin(ang * (k - NB + 1)))
    dft = np.zeros((P, P))
    dft[:WIN, :WIN] = dft[WIN:, WIN:] = cols
    iota = np.tile(np.arange(16), (P, 1))
    q = np.arange(P)[:, None, None] + P * np.arange(2)[None, :, None]
    dist = (np.arange(256)[None, None, :] - q).reshape(P, 512)
    selm = np.zeros((P, P))
    for i in range(4):
        selm[32 * i:32 * i + 2] = -1
    sel0 = np.zeros((P, 16, P))
    sel1 = np.zeros((P, 4, 2, 64))
    for part in range(3):
        for e in range(16):
            sel0[16 * part + e, e] = 1
        for e in range(8):
            sel1[8 * part + e, e // 2, e % 2] = 1
    return np.concatenate([a.reshape(P, -1).astype(f) for a in (ident, dft, iota, dist, selm, sel0, sel1)], axis=1)


def kernel(**inputs):
    import concourse.bacc as _bacc
    from concourse.bass_utils import run_bass_kernel_spmd as _run

    a = {k: np.asarray(v) for k, v in inputs.items()}

    def heads(w):
        return w.transpose(2, 0, 1).reshape(D, -1)

    wqk = a["L1_attn_Wqk"].reshape(2, 2, 4, D // H, D).transpose(0, 4, 1, 2, 3)
    gamma_beta = np.stack([a["L0_ffn_gamma"], a["L0_ffn_beta"]])
    wpos = np.concatenate([a["L1_attn_Wpos"].T, a["L1_attn_bpos"][None], a["L1_attn_gating"][None]])
    twice = lambda w: np.concatenate([w, w])
    w1_0 = a["L0_ffn_w1"].transpose(1, 0, 2).reshape(D, -1)
    w1_1 = a["L1_ffn_w1"].transpose(1, 0, 2).reshape(D, -1)
    feeds = {
        "x": a["x"], "taps": tap_table(), "consts": constant_table(),
        "wq0": heads(a["L0_attn_Q"]), "wk0": heads(a["L0_attn_K"]),
        "vo": a["L0_attn_VO"].transpose(1, 0, 2).reshape(D, -1),
        "gate_w0": a["L0_ffn_gate_w"], "gate_b0": a["L0_ffn_gate_b"][:, None],
        "w1_0": twice(w1_0), "b1_0": a["L0_ffn_b1"].T, "w2_0": a["L0_ffn_w2"].transpose(1, 0, 2),
        "b2_0": np.concatenate([a["L0_ffn_b2"]] * 3), "gamma": gamma_beta,
        "wq1": wqk[0], "wk1": wqk[1], "wv1": a["L1_attn_Wv"].T, "wpos": wpos,
        "wproj": twice(a["L1_attn_Wproj"].T), "bproj": a["L1_attn_bproj"][None],
        "router": a["L1_ffn_router_w"].T, "w1_1": twice(w1_1),
        "b1_1": a["L1_ffn_b1"].reshape(4, P).T,
        "w2_1": a["L1_ffn_w2"].reshape(4, P, D).transpose(1, 0, 2),
        "b2_1": np.concatenate([a["L1_ffn_b2"]] * 3),
    }
    nc = _bacc.Bacc("TRN2", target_bir_lowering=False, num_devices=1)
    arrays, args = {}, []
    for name, v in feeds.items():
        v = np.ascontiguousarray(v)
        arrays[f"in_{name}"] = v
        args.append(nc.dram_tensor(f"in_{name}", v.shape, mybir.dt.from_np(v.dtype), kind="ExternalInput").ap())
    args.append(nc.dram_tensor("out_tokens", (B, NW, D), F32, kind="ExternalOutput").ap())
    tower(nc, *args)
    r = _run(nc, [arrays], core_ids=[0])
    return r.results[0]["out_tokens"]
```

```python
from contextlib import ExitStack

import numpy as np

import concourse.bass as bass
from concourse import mybir

ALU = mybir.AluOpType
ACT = mybir.ActivationFunctionType
AX = mybir.AxisListType
F32 = mybir.dt.float32
F32R = mybir.dt.float32r
BF16 = mybir.dt.bfloat16
U32 = mybir.dt.uint32

P = 128
B, SIG = 16, 4096
UP = 4
WIN = 64
NW = 255
HOP = WIN // UP
TAPS = 5
REACH = HOP + TAPS - 1
NB = WIN // 2 + 1
D = WIN
NT = 2 * B
H = 8
PAIRS = H // 2
UNITS = B * PAIRS
CH = 8
TC = NT // CH
EPS = 1e-5
ALPHA, BETA = 0.12, 0.9
VW = D + 1
OW = D + H
VS = OW + D // H
ROWS = 6 * (D // H)
Q_PART = (0, 0, 1, 0, 2, 1)
K_PART = (0, 1, 0, 2, 0, 1)


def bc(ap, shape):
    return ap.broadcast_to(shape)


def span(start, n):
    return slice(start, start + n) if isinstance(start, int) else bass.ds(start, n)


class Chain:

    def __init__(self, eng, sem):
        self.eng, self.sem, self.n, self.base = eng, sem, 0, 0

    def __call__(self, ins):
        self.n += 1
        ins.then_inc(self.sem, 1)
        self.eng.wait_ge(self.sem, self.base + self.n)

    def loop(self, body, first, end, per):
        start = self.n
        with self.eng.Fori(first, end) as j:
            self.base = j * per - first * per
            body(j)
            assert self.n - start == per, (self.n - start, per)
            self.base = 0
        self.n = start + per * (end - first)


def tower(nc, x, taps, consts, wq0, wk0, vo, gate_w0, gate_b0, w1_0, b1_0, w2_0, b2_0, gamma,
          wqk, split_sel, wv1, wpos, wproj, bproj, router, w1_1, b1_1, w2_1, b2_1, out):
    with ExitStack() as ctx:
        def sb(name, shape, dt=F32):
            return ctx.enter_context(nc.sbuf_tensor(name, shape, dt))

        ps = ctx.enter_context(nc.psum_tensor("ps", [P, 8, 512], F32))
        res = sb("res", [P, NT, D])
        xh = sb("xh", [P, NT, D])
        xT = sb("xT", [D, B + 1, 2 * P])
        cst = sb("cst", [P, consts.shape[1]])
        ident_b = sb("ident_b", [P, P], BF16)
        selm = sb("selm", [P, P], BF16)
        small = sb("small", [P, 4])
        rowsc = sb("rowsc", [P, 3, NT])
        w0 = {"q": sb("wq0s", [D, 2 * P]), "k": sb("wk0s", [D, 2 * P])}
        wqk1 = sb("wqk1s", [D, P])
        vos = sb("vos", [D, H * D])
        wvs, wps = sb("wvs", [D, D]), sb("wps", [P, P])
        bprojb = sb("bprojb", [P, D])
        gb = sb("gb", [P, 2, D])
        posw = sb("posw", [P, 5, H])
        gws = [sb("gws0", [D, 16]), sb("gws1", [D, 8])]
        gbs = sb("gbs", [16, 1])
        b1s = [sb("b1s0", [P, 16]), sb("b1s1", [P, 4])]
        w2s = [sb("w2s0", [P, 16, D]), sb("w2s1", [P, 4, D])]
        wst = [sb("wst0", [P, 3, 16 * P], BF16), sb("wst1", [P, 3, 4 * P], BF16)]
        b2p = [sb("b2p0", [P, 3, D], BF16), sb("b2p1", [P, 3, D], BF16)]
        selb = sb("selb", [P, 16, P], BF16)
        big = sb("big", [P, 8 * 2048])
        mid = sb("mid", [P, 6 * 1024])

        o_id = 0
        o_dft = o_id + P
        o_iota = o_dft + P
        o_dist = o_iota + 16
        o_selm = o_dist + 2 * 256
        o_sel0 = o_selm + P
        o_sel1 = o_sel0 + 16 * P
        o_neg = o_sel1 + 4 * 2 * 64
        ident = cst[:, o_id:o_id + P]
        dft = cst[:, o_dft:o_dft + P]
        iota = cst[:, o_iota:o_iota + 16]
        dist = cst[:, o_dist:o_dist + 512].rearrange("p (t k) -> p t k", t=2)

        held = []

        def sem(name):
            held.append(nc.alloc_semaphore(name))
            return held[-1]

        def phase(program, *args):
            program(*args)
            nc.clear_and_free_semaphores(held)
            held.clear()
            nc.all_engine_barrier()

        def chain(eng, name):
            return Chain(eng, sem(name))

        def tokens():
            sig = mid[:, 0:2 * B * REACH].rearrange("p (t b s) -> p t b s", t=2, b=B)
            tw = mid[:, 640:640 + 2 * TAPS * WIN].rearrange("p (t k j) -> p t k j", t=2, k=TAPS)
            tmp = mid[:, 1280:1280 + 2048].rearrange("p (t b j) -> p t b j", t=2, b=B)
            area = lambda n: big[:, 2048 * n:2048 * (n + 1)].rearrange("p (t b j) -> p t b j", t=2, b=B)
            z, poly, gauss, power = area(0), area(1), area(2), area(3)
            kT = big[:, 8192:8192 + 2048].rearrange("p (g k) -> p g k", g=4)
            spec = lambda n: big[:, 10240 + 1056 * n:10240 + 1056 * (n + 1)].rearrange(
                "p (t b k) -> p t b k", t=2, b=B)
            mag, arg, mask, mt = spec(0), spec(1), spec(2), spec(3)
            low = spec(4)
            top, cap = rowsc[:, 0, :], rowsc[:, 1, :]

            s_sig, s_cst, s_w, s_wz = sem("tok_signal_in"), sem("tok_consts_in"), sem("weights_in"), sem("w_zeroed")
            s_z, s_sq, s_kw = [sem("tok_interp0"), sem("tok_interp1")], sem("tok_window_parts"), sem("tok_kernelled")
            s_tr, s_kT, s_ft, s_pw = sem("tok_turned"), sem("tok_turned_out"), sem("tok_ft"), sem("tok_power")
            s_m2, s_mag, s_arg, s_mask = sem("tok_power_sum"), sem("tok_mag"), sem("tok_arg"), sem("tok_mask")
            s_abs, s_log, s_sm = sem("tok_abs"), sem("tok_log"), sem("tok_small")

            with nc.Block() as block:
                def squares(act, g):
                    nc.scalar.activation(power[:, g // 2, 8 * (g % 2):8 * (g % 2) + 8],
                                         ps[:, 2 + g % 2].rearrange("p (b k) -> p b k", b=8), ACT.Square).then_inc(s_pw, 1)

                def interpolate(eng, ch, t):
                    ch.eng.wait_ge(s_cst, 32)
                    shape = [P, B, HOP, UP]
                    first = lambda k: bc(sig[:, t, :, k:k + HOP].unsqueeze(3), shape)
                    weight = lambda k: bc(tw[:, t, k].rearrange("p (m r) -> p m r", r=UP).unsqueeze(1), shape)
                    zz = z[:, t].rearrange("p b (m r) -> p b m r", r=UP)
                    tt = tmp[:, t].rearrange("p b (m r) -> p b m r", r=UP)
                    ch(eng.tensor_tensor(zz, first(1), weight(1), ALU.mult))
                    for k in range(2, TAPS):
                        ch(eng.tensor_tensor(tt, first(k), weight(k), ALU.mult))
                        ch(eng.tensor_tensor(zz, zz, tt, ALU.add))
                    w = bc(tw[:, t, 0, 0:WIN:UP].unsqueeze(1), [P, B, HOP])
                    ch(eng.tensor_tensor(tt[:, :, :, 0], sig[:, t, :, 0:HOP], w, ALU.mult))
                    return eng.tensor_tensor(zz[:, :, :, 0], zz[:, :, :, 0], tt[:, :, :, 0], ALU.add)

                @block.sync
                def _(sp):
                    sp.dma_start(cst[:], consts).then_inc(s_cst, 16)
                    sp.dma_start(tw, taps).then_inc(s_cst, 16)
                    t0 = x.tensor
                    for b in range(B):
                        sp.dma_start(sig[1:P, 0, b], bass.AP(tensor=t0, offset=b * SIG + HOP - 2,
                                                              ap=[[HOP, P - 1], [1, REACH]])).then_inc(s_sig, 16)
                    sp.dma_start(sig[0:1, 0, :, 2:REACH], bass.AP(tensor=t0, offset=0, ap=[[SIG, 1], [SIG, B], [1, REACH - 2]])).then_inc(s_sig, 16)
                    sp.wait_ge(s_wz, 1)
                    for dst, src in ((w0["q"][:], wq0), (w0["k"][:], wk0), (vos[:], vo), (wvs[:], wv1), (wqk1[:], wqk),
                                     (wps[0:D, 0:D], wproj), (wps[D:P, D:P], wproj),
                                     (gws[0][:], gate_w0), (gws[1][:], router), (gbs[:], gate_b0),
                                     (b1s[0][:], b1_0), (b1s[1][:], b1_1)):
                        sp.dma_start(dst, src).then_inc(s_w, 16)
                    sp.wait_ge(s_w, 16 * 12)
                    sp.wait_ge(s_cst, 32)

                @block.scalar
                def _(act):
                    act.dma_start(sig[P - 1:P, 1], bass.AP(tensor=x.tensor, offset=HOP * (NW - 1) - 2, ap=[[SIG, 1], [SIG, B], [1, REACH]])).then_inc(s_sig, 16)
                    for b in range(B):
                        act.dma_start(sig[0:P - 1, 1, b], bass.AP(tensor=x.tensor, offset=b * SIG + HOP * P - 2,
                                                                   ap=[[HOP, P - 1], [1, REACH]])).then_inc(s_sig, 16)
                    act.wait_ge(s_sm, 3)
                    for t in (0, 1):
                        act.wait_ge(s_z[t], 1)
                        nc.scalar.activation(poly[:, t], z[:, t], ACT.Square, bias=small[:, 0:1], scale=float(np.sqrt(0.5))).then_inc(s_sq, 1)
                        nc.scalar.activation(gauss[:, t], z[:, t], ACT.Square, bias=small[:, 1:2]).then_inc(s_sq, 1)
                        act.wait_ge(s_sq, 3 * t + 2)
                        nc.scalar.activation(gauss[:, t], gauss[:, t], ACT.Exp, scale=-0.5).then_inc(s_sq, 1)
                    for g in range(4):
                        act.wait_ge(s_tr, g + 1)
                        nc.scalar.activation(kT[:, g], ps[:, g % 2], ACT.Copy).then_inc(s_kT, 1)
                        if g:
                            act.wait_ge(s_ft, g)
                            squares(act, g - 1)
                    act.wait_ge(s_ft, 4)
                    squares(act, 3)
                    act.wait_ge(s_m2, 1)
                    nc.scalar.activation(mag, power[:, :, :, 0:NB], ACT.Sqrt).then_inc(s_mag, 1)
                    act.wait_ge(s_arg, 1)
                    nc.scalar.activation(mask, arg, ACT.Sigmoid).then_inc(s_mask, 1)
                    act.wait_ge(s_abs, 1)
                    nc.scalar.activation(arg, arg, ACT.Abs).then_inc(s_log, 1)
                    act.wait_ge(s_log, 1)
                    nc.scalar.activation(arg, arg, ACT.Exp, scale=-1.0).then_inc(s_log, 1)
                    act.wait_ge(s_log, 2)
                    nc.scalar.activation(arg, arg, ACT.Ln, bias=small[:, 2:3]).then_inc(s_log, 1)

                @block.vector
                def _(dve):
                    link = chain(dve, "tok_dve")
                    nc.vector.memset(small[:, 0:1], 1.3 * float(np.sqrt(0.5))).then_inc(s_sm, 1)
                    nc.vector.memset(small[:, 1:2], -0.7).then_inc(s_sm, 1)
                    nc.vector.memset(small[:, 2:3], 1.0).then_inc(s_sm, 1)
                    dve.wait_ge(s_sig, 16 * (2 * B + 2))
                    link(nc.vector.tensor_copy(sig[0:1, 0, :, 0:2], bc(sig[0:1, 0, :, 2:3], [1, B, 2])))
                    interpolate(nc.vector, link, 0).then_inc(s_z[0], 1)
                    for t in (0, 1):
                        dve.wait_ge(s_sq, 3 * t + 3)
                        nc.vector.scalar_tensor_tensor(out=z[:, t].rearrange("p b j -> p (b j)"), in0=gauss[:, t].rearrange("p b j -> p (b j)"), scalar=0.5,
                                                       in1=poly[:, t].rearrange("p b j -> p (b j)"), op0=ALU.mult, op1=ALU.add).then_inc(s_kw, 1)
                    dve.wait_ge(s_pw, 4)
                    nc.vector.tensor_tensor(power[:, :, :, 1:32], power[:, :, :, 1:32], power[:, :, :, 33:64], ALU.add).then_inc(s_m2, 1)
                    dve.wait_ge(s_mag, 1)
                    flat = lambda a: a.rearrange("p t b k -> p (t b) k")
                    over = lambda a: bc(a.unsqueeze(2), [P, NT, NB])
                    link(nc.vector.tensor_reduce(top, flat(mag), AX.X, ALU.max))
                    link(nc.vector.tensor_scalar(cap, top, -ALPHA, None, ALU.mult))
                    nc.vector.tensor_tensor(flat(arg), flat(mag), over(cap), ALU.add).then_inc(s_arg, 1)
                    dve.wait_ge(s_arg, 1)
                    link(nc.vector.tensor_scalar(cap, top, BETA, None, ALU.mult))
                    dve.wait_ge(s_mask, 1)
                    link(nc.vector.tensor_tensor(flat(mt), flat(mag), flat(mask), ALU.mult))
                    nc.vector.tensor_tensor(flat(arg), flat(mt), over(cap), ALU.subtract).then_inc(s_abs, 1)
                    link(nc.vector.tensor_tensor(flat(low), flat(mt), over(cap), ALU.min))
                    dve.wait_ge(s_log, 3)
                    rows = res[:].rearrange("p (b t) d -> p t b d", t=2)
                    for t in (0, 1):
                        link(nc.vector.tensor_tensor(rows[:, t, :, 0:NB], low[:, t], arg[:, t], ALU.subtract))
                        link(nc.vector.tensor_tensor(rows[:, t, :, NB:WIN], low[:, t, :, NB - 2:0:-1], arg[:, t, :, NB - 2:0:-1], ALU.subtract))

                @block.gpsimd
                def _(pool):
                    link = chain(pool, "tok_pool")
                    nc.gpsimd.memset(wps[:], 0.0).then_inc(s_wz, 1)
                    pool.wait_ge(s_sig, 16 * (2 * B + 2))
                    interpolate(nc.gpsimd, link, 1).then_inc(s_z[1], 1)
                    link(nc.gpsimd.memset(xT[:, B], 0.0))
                    link(nc.gpsimd.tensor_copy(ident_b[:], ident))
                    link(nc.gpsimd.tensor_copy(selm[:], cst[:, o_selm:o_selm + P]))

                @block.tensor
                def _(pe):
                    pe.wait_ge(s_cst, 32)
                    for g in range(5):
                        if g < 4:
                            pe.wait_ge(s_kw, g // 2 + 1)
                            if g >= 2:
                                pe.wait_ge(s_kT, g - 1)
                            for c in range(4):
                                pair = z[:, g // 2, 8 * (g % 2) + 2 * c:8 * (g % 2) + 2 * c + 2].rearrange("p b j -> p (b j)")
                                last = nc.tensor.transpose(ps[:, g % 2, P * c:P * c + P], pair, ident)
                            last.then_inc(s_tr, 1)
                        if g:
                            pe.wait_ge(s_kT, g)
                            if g >= 3:
                                pe.wait_ge(s_pw, g - 2)
                            for c in range(4):
                                last = nc.tensor.matmul(ps[:, 2 + (g - 1) % 2, P * c:P * c + P], kT[:, g - 1, P * c:P * c + P], dft, start=True, stop=True)
                            last.then_inc(s_ft, 1)

        def norm_all(tag, after_norm_pe, after_norm_act, after_norm_dve, pool_work=None, sp_work=None, doubled=None):
            sq = mid[:, 0:2048].rearrange("p (t d) -> p t d", t=NT)
            s_xc, s_sq, s_var, s_sd, s_xh = (sem(f"{tag}_{n}") for n in ("centred", "squared", "var", "sd", "normed"))
            half = NT // 2
            mean, var, sd = rowsc[:, 0], rowsc[:, 1], rowsc[:, 2]
            with nc.Block() as block:
                @block.vector
                def _(dve):
                    link = chain(dve, f"{tag}_dve")
                    for n in (0, 1):
                        s = slice(half * n, half * n + half)
                        link(nc.vector.tensor_reduce(mean[:, s], res[:, s], AX.X, ALU.add))
                        link(nc.vector.tensor_scalar(mean[:, s], mean[:, s], -1.0 / D, None, ALU.mult))
                        nc.vector.tensor_tensor(xh[:, s], res[:, s], bc(mean[:, s].unsqueeze(2), [P, half, D]), ALU.add).then_inc(s_xc, 1)
                    for n in (0, 1):
                        s = slice(half * n, half * n + half)
                        dve.wait_ge(s_sq, n + 1)
                        link(nc.vector.tensor_reduce(var[:, s], sq[:, s], AX.X, ALU.add))
                        nc.vector.tensor_scalar(var[:, s], var[:, s], 1.0 / D, EPS, ALU.mult, ALU.add).then_inc(s_var, 1)
                    for n in (0, 1):
                        s = slice(half * n, half * n + half)
                        dve.wait_ge(s_sd, n + 1)
                        link(nc.vector.reciprocal(sd[:, s], sd[:, s]))
                        last = nc.vector.tensor_tensor(xh[:, s], xh[:, s], bc(sd[:, s].unsqueeze(2), [P, half, D]), ALU.mult)
                        if doubled is not None:
                            link(last)
                            last = nc.vector.tensor_copy(doubled[:, s], bc(xh[:, s].unsqueeze(2), [P, half, 2, D]))
                        last.then_inc(s_xh, 1)
                    after_norm_dve(dve, link)

                @block.scalar
                def _(act):
                    for n in (0, 1):
                        act.wait_ge(s_xc, n + 1)
                        s = slice(half * n, half * n + half)
                        nc.scalar.activation(sq[:, s], xh[:, s], ACT.Square).then_inc(s_sq, 1)
                    for n in (0, 1):
                        s = slice(half * n, half * n + half)
                        act.wait_ge(s_var, n + 1)
                        nc.scalar.activation(sd[:, s], var[:, s], ACT.Sqrt).then_inc(s_sd, 1)
                    after_norm_act(act)

                @block.tensor
                def _(pe):
                    after_norm_pe(pe, s_xh)

                if pool_work:
                    @block.gpsimd
                    def _(pool):
                        pool_work(pool)

                if sp_work:
                    @block.sync
                    def _(sp):
                        sp_work(sp)

        def turned(c, bank, src):
            width = src.shape[2]
            for k in range(TC):
                last = nc.tensor.transpose(ps[0:width, bank, P * k:P * k + P], src[:, TC * c + k], ident)
            return last

        def attention_prep0():
            s_tr, s_xT = sem("a0_turned"), sem("a0_xT")
            s_w, s_rest = sem("a0_weights_in"), sem("a0_rest")

            def pe_work(pe, s_xh):
                for c in range(CH):
                    pe.wait_ge(s_xh, c // (CH // 2) + 1)
                    if c >= 2:
                        pe.wait_ge(s_xT, c - 1)
                    turned(c, c % 2, xh[:]).then_inc(s_tr, 1)

            def act_work(act):
                for c in range(CH):
                    act.wait_ge(s_tr, c + 1)
                    nc.scalar.activation(xT[:, 2 * c:2 * c + 2], ps[0:D, c % 2].rearrange("p (b q) -> p b q", b=2), ACT.Copy).then_inc(s_xT, 1)

            def sp_work(sp):
                n = 0
                for dst, src in ((w2s[0][:], w2_0), (w2s[1][:], w2_1), (bprojb[:], bproj), (gb[:], gamma_beta),
                                 (posw[:], pos_in)):
                    sp.dma_start(dst, src).then_inc(s_w, 16)
                    n += 16
                sp.wait_ge(s_w, n)

            norm_all("a0", pe_work, act_work, lambda dve, link: None, None, sp_work)

        gamma_beta = bass.AP(tensor=gamma.tensor, offset=0, ap=[[0, P], [D, 2], [1, D]])
        pos_in = bass.AP(tensor=wpos.tensor, offset=0, ap=[[0, P], [H, 5], [1, H]])
        bproj = bass.AP(tensor=bproj.tensor, offset=0, ap=[[0, P], [1, D]])

        def attention0():
            L = 0
            scale = D ** -0.5 if L == 0 else (D // H) ** -0.5
            w = w0
            wl = {n: (w[n][:] if L == 0 else w[n][:].rearrange("p g h d -> p (g h d)")) for n in "qk"}

            pos = [0]
            def take(n, dt=F32):
                a = big[:, pos[0]:pos[0] + n] if pos[0] + n <= 16384 else None
                assert a is not None
                pos[0] += n
                return a
            q32 = [take(512).rearrange("p (g q) -> p g q", g=2) for _ in range(2)]
            k32 = [take(512).rearrange("p (g q) -> p g q", g=2) for _ in range(2)]
            e_sb = [take(1024).rearrange("p (j c q) -> p j c q", j=2, c=2) for _ in range(2)]
            if L == 0:
                val = [take(2 * H * VW).rearrange("p (c v) -> p c v", c=2) for _ in range(2)]
                heads = take(H * 2 * D).rearrange("p (h t d) -> p h t d", h=H, t=2)
            else:
                val = v1pad
            xs = [take(256)[0:D] for _ in range(2)]
            o_rows = VW if L == 0 else OW
            o_sb = [take(512)[0:o_rows] for _ in range(2)]
            work = take(1024)
            mx = work[:, 0:4].rearrange("p (j t) -> p j t", j=2)
            hsum = work[:, 16:16 + 2 * D].rearrange("p (t d) -> p t d", t=2)
            rinv = work[:, 144:160]
            rgate = work[:, 160:176].rearrange("p (t h) -> p t h", t=2)
            asum = work[:, 176:192].rearrange("p (t h) -> p t h", t=2)
            blend = work[:, 192:192 + 2 * D].rearrange("p (t d) -> p t d", t=2)
            oT_sb = work[:, 320:320 + P]
            mt_sb, mhl, q_r, k_r = mt_t[L], mhl_t[L], qr_t, kr_t

            S = ps[:, 0:2].rearrange("p j (t k) -> p j t k", t=2)
            T = ps[:, 2:4].rearrange("p j (c q) -> p j c q", c=2)
            O = ps[:, 4].rearrange("p (j q) -> p j q", j=2)
            PQ, PK = ps[:, 5], ps[:, 6]
            MT = ps[:, 7, 0:P].bitcast(BF16)
            if L == 0:
                OT = ps[:, 7, P:P + 4 * VW].rearrange("p (j t d) -> p j t d", j=2, t=2)
            else:
                OT = ps[:, 7, P:P + 2 * OW].rearrange("p (t d) -> p t d", t=2)

            t = f"L{L}_"
            s_xs, s_qkp, s_qk_act, s_qk_dve = (sem(t + n) for n in ("xs_ready", "qk_projected", "q_in_sbuf", "k_in_sbuf"))
            s_vp, s_v_act, s_v_dve = (sem(t + n) for n in ("v_projected", "v_even", "v_odd"))
            s_S, s_mhl, s_mtp, s_mt = (sem(t + n) for n in ("scores", "max_parts", "max_turned", "max_ready"))
            s_T, s_E, s_PV, s_O, s_OT, s_norm = (sem(t + n) for n in ("turned_scores", "exps", "outputs", "outputs_in_sbuf", "outputs_turned", "normed"))
            s_bl, s_oTp, s_oT, s_y, s_fin = (sem(t + n) for n in ("blended", "blended_turned", "blended_ready", "projected", "added"))
            s_ones = sem(t + "ones")

            def rows(p, j):
                r = 32 * (2 * (p % 2) + j)
                return slice(r, r + 32)

            def at(k):
                return (k // PAIRS) % 2, k % PAIRS

            with nc.Block() as block:
                @block.tensor
                def _(pe):
                    def project(b, par):
                        pe.wait_ge(s_xs, b + 1)
                        if L == 0:
                            if not isinstance(b, int) or b >= 1:
                                pe.wait_ge(s_v_act, b)
                                pe.wait_ge(s_v_dve, b)
                        elif not isinstance(b, int) or b >= 3:
                            pe.wait_ge(s_fin, b - 2)
                        for bank, n in ((PQ, "q"), (PK, "k")):
                            for g in range(2):
                                last = nc.tensor.matmul(bank[:, 256 * g:256 * g + 256], wl[n][:, P * g:P * g + P], xs[par], start=True, stop=True)
                        last.then_inc(s_qkp, 1)

                    def values(b, par):
                        pe.wait_ge(s_qk_act, 2 * (b + 1))
                        pe.wait_ge(s_qk_dve, 2 * (b + 1))
                        for c, bank in ((0, PQ), (1, PK)):
                            last = nc.tensor.matmul(bank, xs[par][:, P * c:P * c + P], vos[:], start=True, stop=True)
                        last.then_inc(s_vp, 1)

                    def scores(par, p):
                        for tq in range(2):
                            for j in range(2):
                                r = rows(p, j)
                                last = nc.tensor.matmul(S[:, j, tq], q_r[par][r, p // 2, P * tq:P * tq + P], k_r[par][r, p // 2], start=True, stop=True)
                        last.then_inc(s_S, 1)

                    def max_turn(k):
                        for tq in range(2):
                            last = nc.tensor.transpose(MT[:, P * tq:P * tq + P], mhl[k % 2][:, tq], ident_b[:])
                        last.then_inc(s_mtp, 1)

                    def turned_scores(k):
                        par, p = at(k)
                        for c in range(2):
                            for j in range(2):
                                r = rows(p, j)
                                nc.tensor.matmul(T[:, j, c], k32[par][r, p // 2, P * c:P * c + P], q32[par][r, p // 2], start=True, stop=False)
                                last = nc.tensor.matmul(T[:, j, c], selm[r], mt_sb[k % 2][r], start=False, stop=True)
                        last.then_inc(s_T, 1)

                    def outputs(k):
                        par, p = at(k)
                        for j in range(2):
                            h = 2 * p + j
                            for c in range(2):
                                n = P - c
                                if L == 0:
                                    last = nc.tensor.matmul(O[0:VW, j], val[par][0:n, c, VW * h:VW * h + VW], e_sb[k % 2][0:n, j, c], start=(c == 0), stop=(c == 1))
                                else:
                                    last = nc.tensor.matmul(O[0:OW, par], val[par][0:n, c, OW * h:OW * h + OW], e_sb[k % 2][0:n, j, c],
                                                            start=(h == 0 and c == 0), stop=(h == H - 1 and c == 1))
                        last.then_inc(s_PV, 1)

                    def slot(j, k, do=("mt", "s", "pv", "turn", "t", "tail", "proj")):
                        U = 2 * PAIRS * j + k
                        known = isinstance(j, int)
                        par, p = at(k)
                        b = 2 * j + par
                        if "mt" in do:
                            pe.wait_ge(s_mhl, U + 1)
                            if not known or U >= 1:
                                pe.wait_ge(s_mt, U)
                            if L == 0 and (not known or U >= 4):
                                pe.wait_ge(s_norm, U - 3)
                            if L == 1 and p == 3 and (not known or b >= 1):
                                pe.wait_ge(s_bl, b)
                            max_turn(k)
                        if "s" in do:
                            par1, p1 = at(k + 1)
                            if p1 == 0:
                                pe.wait_ge(s_qk_act, 2 * (b + 2))
                                pe.wait_ge(s_qk_dve, 2 * (b + 2))
                            scores(par1, p1)
                        if "pv" in do and (not known or U >= 2):
                            pe.wait_ge(s_E, U - 1)
                            bl = b - 1 if p < 2 else b
                            if L == 0:
                                if p == 2:
                                    pe.wait_ge(s_v_act, bl + 1)
                                    pe.wait_ge(s_v_dve, bl + 1)
                                if not known or U >= 3:
                                    pe.wait_ge(s_O, U - 2)
                            elif p == 2:
                                pe.wait_ge(s_v_act, bl + 1)
                                if not known or bl >= 1:
                                    pe.wait_ge(s_O, bl)
                            outputs(k - 2)
                        if "turn" in do and (not known or U >= 3) and (L == 0 or p == 2) and (L == 0 or not known or b >= 1):
                            if "mt" in do:
                                pe.wait_ge(s_mt, U + 1)
                            if L == 0:
                                if "mt" not in do:
                                    pe.wait_ge(s_norm, U - 3)
                                pe.wait_ge(s_O, U - 2)
                                for jj in range(2):
                                    for tq in range(2):
                                        last = nc.tensor.transpose(OT[:, jj, tq], o_sb[(k + 1) % 2][:, 256 * jj + P * tq:256 * jj + P * tq + P], ident[0:VW, 0:VW])
                            else:
                                pe.wait_ge(s_O, b)
                                for tq in range(2):
                                    last = nc.tensor.transpose(OT[:, tq], o_sb[(par + 1) % 2][:, P * tq:P * tq + P], ident[0:OW, 0:OW])
                            last.then_inc(s_OT, 1)
                        if "t" in do:
                            pe.wait_ge(s_mt, U + 1)
                            if not known or U >= 1:
                                pe.wait_ge(s_E, U)
                            turned_scores(k)
                        if "tail" in do and L == 1:
                            if p == 3 and (not known or b >= 1):
                                pe.wait_ge(s_bl, b)
                                if "proj" in do:
                                    pe.wait_ge(s_qk_act, 2 * (b + 2))
                                    pe.wait_ge(s_qk_dve, 2 * (b + 2))
                                nc.tensor.transpose(PQ[:, 0:P], blend.rearrange("p t d -> p (t d)"), ident).then_inc(s_oTp, 1)
                            if p == 0 and (not known or b >= 2):
                                pe.wait_ge(s_oT, b - 1)
                                for tq in range(2):
                                    r = slice(D * tq, D * tq + D)
                                    last = nc.tensor.matmul(ps[:, 5 + tq, 0:D], oT_sb[r], wps[r], start=True, stop=True)
                                last.then_inc(s_y, 1)
                        if "proj" in do:
                            if p == 1:
                                project(b + 1, (par + 1) % 2)
                            if p == 2 and L == 0:
                                values(b + 1, (par + 1) % 2)

                    project(0, 0)
                    if L == 0:
                        values(0, 0)
                    pe.wait_ge(s_qk_act, 2)
                    pe.wait_ge(s_qk_dve, 2)
                    scores(0, 0)
                    for k in range(2 * PAIRS):
                        slot(0, k)
                    with pe.Fori(1, B // 2) as j:
                        for k in range(2 * PAIRS):
                            slot(j, k)
                    for k in range(5 if L else 3):
                        slot(B // 2, k, ("pv", "turn", "tail") if k < 2 else ("turn", "tail"))

                @block.scalar
                def _(act):
                    def q_out(b, par):
                        act.wait_ge(s_qkp, b + 1)
                        if not isinstance(b, int) or b >= 2:
                            act.wait_ge(s_T, PAIRS * (b - 1))
                        nc.scalar.activation(q32[par].rearrange("p g q -> p (g q)"), PQ, ACT.Copy).then_inc(s_qk_act, 1)
                        nc.scalar.activation(q_r[par][:].rearrange("p g q -> p (g q)"), PQ, ACT.Copy).then_inc(s_qk_act, 1)

                    def v_out(b, par):
                        act.wait_ge(s_vp, b + 1)
                        if not isinstance(b, int) or b >= 2:
                            act.wait_ge(s_PV, PAIRS * (b - 1))
                        nc.scalar.activation(val[par][:, 0].rearrange("p (h d) -> p h d", h=H)[:, :, 0:D],
                                             PQ.rearrange("p (h d) -> p h d", h=H), ACT.Copy).then_inc(s_v_act, 1)

                    def slot(j, k, do=("mt", "e", "o", "proj")):
                        U = 2 * PAIRS * j + k
                        known = isinstance(j, int)
                        par, p = at(k)
                        b = 2 * j + par
                        if "mt" in do:
                            act.wait_ge(s_mtp, U + 1)
                            if not known or U >= 2:
                                act.wait_ge(s_T, U - 1)
                            nc.scalar.activation(mt_sb[k % 2], MT, ACT.Copy).then_inc(s_mt, 1)
                        if "o" in do and L == 0 and (not known or U >= 2):
                            act.wait_ge(s_PV, U - 1)
                            if not known or U >= 4:
                                act.wait_ge(s_OT, U - 3)
                            nc.scalar.activation(o_sb[k % 2], ps[0:VW, 4], ACT.Copy).then_inc(s_O, 1)
                        if "o" in do and L == 1 and p == 1 and (not known or b >= 1):
                            act.wait_ge(s_PV, U - 1)
                            pl = (par + 1) % 2
                            if not known or b >= 3:
                                act.wait_ge(s_OT, b - 2)
                            nc.scalar.activation(o_sb[pl][:, 0:256], O[0:OW, pl], ACT.Copy).then_inc(s_O, 1)
                        if "e" in do:
                            act.wait_ge(s_T, U + 1)
                            if not known or U >= 2:
                                act.wait_ge(s_PV, U - 1)
                            nc.scalar.activation(e_sb[k % 2], T, ACT.Exp, scale=scale).then_inc(s_E, 1)
                        if "o" in do and L == 1 and p == 3 and (not known or b >= 1):
                            act.wait_ge(s_oTp, b)
                            if not known or b >= 2:
                                act.wait_ge(s_y, b - 1)
                            nc.scalar.activation(oT_sb, PQ[:, 0:P], ACT.Copy).then_inc(s_oT, 1)
                        if "proj" in do:
                            if p == 1:
                                q_out(b + 1, (par + 1) % 2)
                            if p == 2 and L == 0:
                                v_out(b + 1, (par + 1) % 2)

                    q_out(0, 0)
                    if L == 0:
                        act.wait_ge(s_ones, 4)
                        v_out(0, 0)
                    for k in range(2 * PAIRS):
                        slot(0, k)
                    with act.Fori(1, B // 2) as j:
                        for k in range(2 * PAIRS):
                            slot(j, k)
                    for k in range(4 if L else 2):
                        slot(B // 2, k, ("o",))

                @block.vector
                def _(dve):
                    link = chain(dve, t + "dve")

                    def k_out(b, par):
                        dve.wait_ge(s_qkp, b + 1)
                        if not isinstance(b, int) or b >= 2:
                            dve.wait_ge(s_T, PAIRS * (b - 1))
                        nc.vector.tensor_copy(k32[par].rearrange("p g q -> p (g q)"), PK).then_inc(s_qk_dve, 1)
                        nc.vector.tensor_copy(k_r[par][:].rearrange("p g q -> p (g q)"), PK).then_inc(s_qk_dve, 1)

                    def v_out(b, par):
                        dve.wait_ge(s_vp, b + 1)
                        if not isinstance(b, int) or b >= 2:
                            dve.wait_ge(s_PV, PAIRS * (b - 1))
                        nc.vector.tensor_copy(val[par][:, 1].rearrange("p (h d) -> p h d", h=H)[:, :, 0:D],
                                              PK.rearrange("p (h d) -> p h d", h=H)).then_inc(s_v_dve, 1)

                    def maxima(U, k):
                        dve.wait_ge(s_S, U + 1)
                        link(nc.vector.tensor_reduce(mx, S[:, :, :, 0:NW], AX.X, ALU.max))
                        if not isinstance(U, int) or U >= 2:
                            dve.wait_ge(s_mtp, U - 1)
                        i = 2 * (k % 2)
                        m = mhl[k % 2][:].rearrange("p t (i c) -> p t i c", i=4)[:, :, i:i + 2]
                        mt = mx.rearrange("p j t -> p t j")
                        link(nc.vector.tensor_copy(m[:, :, :, 0], mt))
                        nc.vector.tensor_tensor(m[:, :, :, 1], mt, m[:, :, :, 0], ALU.subtract).then_inc(s_mhl, 1)
                        dve.wait_ge(s_mhl, U + 1)

                    def slot(j, k, do=("m", "n", "proj")):
                        U = 2 * PAIRS * j + k
                        known = isinstance(j, int)
                        par, p = at(k)
                        b = 2 * j + par
                        if "m" in do:
                            maxima(U + 1, k + 1)
                        if L == 0 and (not known or U >= 3):
                            dve.wait_ge(s_OT, U - 2)
                            _, pl = at(k - 3)
                            r = rinv[:, 0:4].rearrange("p (j t) -> p j t", j=2)
                            link(nc.vector.reciprocal(r, OT[:, :, :, D]))
                            nc.vector.tensor_tensor(heads[:, 2 * pl:2 * pl + 2], OT[:, :, :, 0:D], bc(r.unsqueeze(3), [P, 2, 2, D]), ALU.mult).then_inc(s_norm, 1)
                            dve.wait_ge(s_norm, U - 2)
                            if p == 2 and (not known or b >= 1):
                                link(nc.vector.tensor_reduce(hsum, heads.rearrange("p h t d -> p t d h"), AX.X, ALU.add))
                                rs = res[:, span(2 * (b - 1), 2)]
                                link(nc.vector.tensor_tensor(rs, rs, hsum, ALU.add))
                        if L == 1:
                            if p == 2 and (not known or b >= 1):
                                dve.wait_ge(s_OT, b)
                                r = rinv.rearrange("p (t h) -> p t h", t=2)
                                l = OT[:, :, D:OW]
                                link(nc.vector.reciprocal(r, l))
                                link(nc.vector.tensor_tensor(rgate, r, bc(omg.unsqueeze(1), [P, 2, H]), ALU.mult))
                                link(nc.vector.tensor_tensor(asum, l, rgate, ALU.mult))
                                link(nc.vector.tensor_tensor(asum, asum, gsum, ALU.add))
                                link(nc.vector.reciprocal(asum, asum))
                                shape = [P, 2, H, D // H]
                                by_head = lambda a: a.rearrange("p t (h d) -> p t h d", h=H)
                                if not known or b >= 2:
                                    dve.wait_ge(s_oTp, b - 1)
                                link(nc.vector.tensor_tensor(by_head(blend), by_head(OT[:, :, 0:D]), bc(rgate.unsqueeze(3), shape), ALU.mult))
                                link(nc.vector.tensor_tensor(blend, blend, posv[:, :, b - 1], ALU.add))
                                nc.vector.tensor_tensor(by_head(blend), by_head(blend), bc(asum.unsqueeze(3), shape), ALU.mult).then_inc(s_bl, 1)
                                dve.wait_ge(s_bl, b)
                            if p == 0 and (not known or b >= 2):
                                dve.wait_ge(s_y, b - 1)
                                y = ps[:, 5:7, 0:D]
                                link(nc.vector.tensor_tensor(hsum, y, bc(bprojb[:].unsqueeze(1), [P, 2, D]), ALU.add))
                                rs = res[:, span(2 * (b - 2), 2)]
                                nc.vector.tensor_tensor(rs, rs, hsum, ALU.add).then_inc(s_fin, 1)
                                dve.wait_ge(s_fin, b - 1)
                        if "proj" in do:
                            if p == 1:
                                k_out(b + 1, (par + 1) % 2)
                            if p == 2 and L == 0:
                                v_out(b + 1, (par + 1) % 2)

                    k_out(0, 0)
                    for n in range(2):
                        link(nc.vector.memset(mhl[n][:], 0.0))
                    if L == 0:
                        for par in range(2):
                            for c in range(2):
                                nc.vector.memset(val[par][:, c, D:H * VW:VW], 1.0).then_inc(s_ones, 1)
                        v_out(0, 0)
                    maxima(0, 0)
                    for k in range(2 * PAIRS):
                        slot(0, k)
                    per = 2 * (4 * 2 + 4 + 2) if L == 0 else 2 * (4 * 2 + 7 + 1)
                    link.loop(lambda j: [slot(j, k) for k in range(2 * PAIRS)], 1, B // 2, per)
                    for k in range(5 if L else 3):
                        slot(B // 2, k, ("n",))

                @block.gpsimd
                def _(pool):
                    def fetch(b, par):
                        if not isinstance(b, int) or b >= 2:
                            pool.wait_ge(s_vp if L == 0 else s_qkp, b - 1)
                        nc.gpsimd.tensor_copy(xs[par], xT[:, b]).then_inc(s_xs, 1)
                        if L == 1:
                            if not isinstance(b, int) or b >= 2:
                                pool.wait_ge(s_PV, PAIRS * (b - 1))
                            for c in range(2):
                                last = nc.gpsimd.tensor_copy(v1own[par][:, c, :, 0:D // H],
                                                             vall[:, 2 * b + c].rearrange("p (h d) -> p h d", h=H))
                                if c == 1:
                                    last.then_inc(s_v_act, 1)

                    fetch(0, 0)
                    fetch(1, 1)
                    with pool.Fori(1, B // 2) as j:
                        fetch(2 * j, 0)
                        fetch(2 * j + 1, 1)
                    pool.wait_ge(s_vp if L == 0 else s_qkp, B - 1)
                    nc.gpsimd.tensor_copy(xs[0], xT[:, B]).then_inc(s_xs, 1)
                    if L == 0:
                        pool_setup(pool)

        mt_t = [[sb(f"mt{n}", [P, 256], BF16)[:] for n in range(2)]] * 2
        mhl_t = [[sb(f"mhl{n}", [P, 2, P], BF16) for n in range(2)]] * 2
        qr_t = [sb(f"qr{n}", [P, 2, 256], F32R) for n in range(2)]
        kr_t = [sb(f"kr{n}", [P, 2, 256], F32R) for n in range(2)]

        vall = xh
        v1flat = [mid[:, 0:1280].rearrange("p (c v) -> p c v", c=2), mid[:, 1280:2560].rearrange("p (c v) -> p c v", c=2)]
        v1pad = v1flat
        v1own = [v.rearrange("p c (h s) -> p c h s", h=H) for v in v1flat]
        posv = mid[:, 2560:2560 + 2048].rearrange("p (t b d) -> p t b d", t=2, b=B)
        selqk = big[:, 12800:12800 + 1536].bitcast(BF16).rearrange("p (a s m) -> p a s m", a=H, s=3)
        gsum = mid[:, 4608:4624].rearrange("p (t h) -> p t h", t=2)
        omg = mid[:, 4624:4632]

        def pool_setup(pool):
            link = chain(pool, "setup_pool")
            s_in = sem("setup_in")
            stage = mid
            link(nc.gpsimd.memset(b2p[0][:], 0.0))
            link(nc.gpsimd.memset(b2p[1][:], 0.0))
            for L, (wsrc, n) in enumerate(((w1_0, 2048), (w1_1, 512))):
                E3 = 48 if L == 0 else 24
                raw, rest = stage[:, 0:n], stage[:, 2048:2048 + n]
                pool.dma_start(raw, wsrc).then_inc(s_in, 16)
                pool.dma_start(stage[0:E3, 4096:4096 + D], (b2_0, b2_1)[L]).then_inc(s_in, 16)
                pool.wait_ge(s_in, 32 * (L + 1))
                hi, md, lo = (wst[L][:, s] for s in range(3))
                link(nc.gpsimd.tensor_copy(hi, raw))
                link(nc.gpsimd.tensor_tensor(rest, raw, hi, ALU.subtract))
                link(nc.gpsimd.tensor_copy(md, rest))
                link(nc.gpsimd.tensor_tensor(lo[0:D], rest[0:D], md[0:D], ALU.subtract))
                link(nc.gpsimd.tensor_copy(lo[D:P], hi[D:P]))
                raw, rest = stage[0:E3, 4096:4096 + D], stage[0:E3, 4160:4160 + D]
                hi, md, lo = (b2p[L][0:E3, s] for s in range(3))
                link(nc.gpsimd.tensor_copy(hi, raw))
                link(nc.gpsimd.tensor_tensor(rest, raw, hi, ALU.subtract))
                link(nc.gpsimd.tensor_copy(md, rest))
                link(nc.gpsimd.tensor_tensor(lo, rest, md, ALU.subtract))

        xa = big[:, 0:2048].bitcast(BF16).rearrange("p (c q) -> p c q", c=CH)
        xb = big[:, 2048:4096].bitcast(BF16).rearrange("p (c q) -> p c q", c=CH)
        ct = big[:, 4096:6144].bitcast(BF16).rearrange("p (c q) -> p c q", c=CH)
        mo = big[:, 6144:16384]

        def experts_prep(L):
            E = 16 if L == 0 else 8
            t = f"m{L}_"
            rest = [mo[:, 512 * n:512 * n + 512] for n in range(2)]
            lt = [mo[0:E, 1024 + 512 * n:1536 + 512 * n] for n in range(2)]
            lg = mo[:, 2048:2048 + NT * E].rearrange("p (t e) -> p t e", t=NT)
            v8 = mo[:, 2560:2816].rearrange("p (t e) -> p t e", t=NT)
            i8 = mo[:, 2816:3072].bitcast(U32).rearrange("p (t e) -> p t e", t=NT)
            idx = mo[:, 3072:3136].rearrange("p (e t) -> p e t", e=2)
            wts = mo[:, 3136:3136 + 4 * NT].rearrange("p (e t) -> p e t", e=4)
            comb = mo[:, 3328:3328 + NT * E].rearrange("p (t e) -> p t e", t=NT)
            pick = mo[:, 3840:3840 + NT * E].rearrange("p (t e) -> p t e", t=NT)
            c3 = mo[:, 4352:4352 + NT * 3 * E // 2].bitcast(BF16).rearrange("p (t s e) -> p t s e", t=NT, s=3)

            x2 = mo[:, 5120:5120 + NT * 2 * D].rearrange("p (t a d) -> p t a d", t=NT, a=2)
            s_tr, s_x, s_xt, s_xr, s_xp = (sem(t + n) for n in ("turned", "x_hi", "x_full", "x_rest", "x_parts"))
            s_lg, s_lt, s_lp, s_lc = (sem(t + n) for n in ("logits", "logits_biased", "logits_turned", "logits_ready"))
            s_dv, s_ex, s_c3, s_ctp, s_ct, s_sel, s_rt = (sem(t + n) for n in ("gap", "gap_exp", "parts", "weights_turned", "weights_ready", "selectors", "retired"))
            n_sel = 16 if L == 0 else 4
            o_sel = o_sel0 if L == 0 else o_sel1
            E3 = 3 * E

            def pe_work(pe, s_xh):
                for c in range(CH + 2):
                    if c < CH:
                        pe.wait_ge(s_xh, c // (CH // 2) + 1)
                        if c >= 2:
                            pe.wait_ge(s_xt, 2 * (c - 1))
                            pe.wait_ge(s_xr, c - 1)
                        turned(c, c % 2, x2.rearrange("p t a d -> p t (a d)")).then_inc(s_tr, 1)
                    if 1 <= c <= CH:
                        d = c - 1
                        pe.wait_ge(s_xt, 2 * d + 2)
                        if d >= 2:
                            pe.wait_ge(s_lt, d - 1)
                        nc.tensor.matmul(ps[0:E, 2 + d % 2], gws[L][:], xT[:, 2 * d:2 * d + 2].rearrange("p b q -> p (b q)"), start=True, stop=True).then_inc(s_lg, 1)
                    if c >= 2:
                        d = c - 2
                        pe.wait_ge(s_lt, d + 1)
                        if d >= 2:
                            pe.wait_ge(s_lc, d - 1)
                        for k in range(TC):
                            last = nc.tensor.transpose(ps[:, 4 + d % 2, E * k:E * k + E], lt[d % 2][:, P * k:P * k + P], ident[0:E, 0:E])
                        last.then_inc(s_lp, 1)
                pe.wait_ge(s_c3, 1)
                for c in range(CH):
                    if c >= 2:
                        pe.wait_ge(s_ct, c - 1)
                    bank = ps[0:E3, 6 + c % 2, 0:256].bitcast(BF16)
                    for k in range(TC):
                        last = nc.tensor.transpose(bank[:, P * k:P * k + P], c3[:, TC * c + k].rearrange("p s e -> p (s e)"), ident_b[:])
                    last.then_inc(s_ctp, 1)

            def act_work(act):
                for c in range(CH + 1):
                    if c < CH:
                        act.wait_ge(s_tr, c + 1)
                        nc.scalar.activation(xa[:, c], ps[:, c % 2], ACT.Copy).then_inc(s_x, 1)
                        nc.scalar.activation(xb[0:D, c], ps[0:D, c % 2], ACT.Copy).then_inc(s_xt, 1)
                        nc.scalar.activation(xT[:, 2 * c:2 * c + 2], ps[0:D, c % 2].rearrange("p (b q) -> p b q", b=2), ACT.Copy).then_inc(s_xt, 1)
                    if c >= 1:
                        d = c - 1
                        act.wait_ge(s_lg, d + 1)
                        if d >= 2:
                            act.wait_ge(s_lp, d - 1)
                        if L == 0:
                            nc.scalar.activation(lt[d % 2], ps[0:E, 2 + d % 2], ACT.Identity, bias=gbs[0:E]).then_inc(s_lt, 1)
                        else:
                            nc.scalar.activation(lt[d % 2], ps[0:E, 2 + d % 2], ACT.Copy).then_inc(s_lt, 1)
                act.wait_ge(s_dv, 1)
                nc.scalar.activation(wts[:, 0], wts[:, 0], ACT.Exp).then_inc(s_ex, 1)
                for c in range(CH):
                    act.wait_ge(s_ctp, c + 1)
                    if c == 0:
                        act.wait_ge(s_sel, 1)
                    nc.scalar.activation(ct[0:E3, c], ps[0:E3, 6 + c % 2, 0:256].bitcast(BF16), ACT.Copy).then_inc(s_ct, 1)

            def dve_work(dve, link):
                nc.vector.memset(ct, 0.0).then_inc(s_sel, 1)
                for c in range(CH + 2):
                    if c < CH:
                        dve.wait_ge(s_xt, 2 * c + 2)
                        r = rest[c % 2][D:P]
                        nc.vector.tensor_tensor(r, ps[D:P, c % 2], xa[D:P, c], ALU.subtract).then_inc(s_xr, 1)
                        dve.wait_ge(s_xr, c + 1)
                        link(nc.vector.tensor_copy(xa[D:P, c], r))
                        link(nc.vector.tensor_tensor(xb[D:P, c], r, xa[D:P, c], ALU.subtract))
                    if c >= 2:
                        d = c - 2
                        dve.wait_ge(s_lp, d + 1)
                        nc.vector.tensor_copy(lg[:, TC * d:TC * d + TC], ps[:, 4 + d % 2, 0:TC * E].rearrange("p (t e) -> p t e", t=TC)).then_inc(s_lc, 1)
                dve.wait_ge(s_lc, CH)
                for n in range(NT):
                    last = nc.vector.max(v8[:, n], lg[:, n])
                link(last)
                for n in range(NT):
                    last = nc.vector.max_index(i8[:, n], v8[:, n], lg[:, n])
                link(last)
                nc.vector.tensor_tensor(wts[:, 0], v8[:, :, 1], v8[:, :, 0], ALU.subtract).then_inc(s_dv, 1)
                link(nc.vector.tensor_copy(idx.rearrange("p e t -> p t e"), i8[:, :, 0:2]))
                dve.wait_ge(s_ex, 1)
                link(nc.vector.tensor_scalar(wts[:, 1], wts[:, 0], 1.0, None, ALU.add))
                link(nc.vector.reciprocal(wts[:, 2], wts[:, 1]))
                link(nc.vector.tensor_tensor(wts[:, 3], wts[:, 0], wts[:, 2], ALU.mult))
                shape = [P, NT, E]
                for n, dst in ((0, comb), (1, pick)):
                    link(nc.vector.tensor_tensor(dst, bc(iota[:, 0:E].unsqueeze(1), shape), bc(idx[:, n].unsqueeze(2), shape), ALU.is_equal))
                    link(nc.vector.tensor_tensor(dst, dst, bc(wts[:, 2 + n].unsqueeze(2), shape), ALU.mult))
                link(nc.vector.tensor_tensor(comb, comb, pick, ALU.add))
                link(nc.vector.tensor_copy(c3[:, :, 0], comb))
                link(nc.vector.tensor_tensor(pick, comb, c3[:, :, 0], ALU.subtract))
                link(nc.vector.tensor_copy(c3[:, :, 1], pick))
                nc.vector.tensor_tensor(c3[:, :, 2], pick, c3[:, :, 1], ALU.subtract).then_inc(s_c3, 1)

            def pool_work(pool):
                link = chain(pool, t + "pool")
                link(nc.gpsimd.memset(selb[:], 0.0))
                link(nc.gpsimd.tensor_copy(selb[0:E3, 0:n_sel].rearrange("p e f -> p (e f)"), cst[0:E3, o_sel:o_sel + n_sel * P]))

            norm_all(t + "n", pe_work, act_work, dve_work, pool_work, doubled=x2)

        def experts(L):
            NS = 16 if L == 0 else 4
            t = f"e{L}_"
            func = ACT.Relu if L == 0 else ACT.Gelu
            DEEP = 4
            hid = [mo[:, 512 * n:512 * n + 512] for n in range(DEEP)]
            wgt = [mo[:, 2048 + 512 * n:2560 + 512 * n] for n in range(DEEP)]
            y_sb = mo[0:D, 4096:4608]
            yy = mo[:, 4608:4864].rearrange("p (t d) -> p t d", t=TC)
            yq = mo[:, 4864:5120].rearrange("p (t d) -> p t d", t=TC)
            st = mo[:, 5120:5136].rearrange("p (s t) -> p s t", s=4)
            nh = mo[:, 5136:5140]
            s_h, s_hid, s_cb, s_wgt, s_w2, s_y = (sem(t + n) for n in ("hidden", "activated", "weights_spread", "weighted", "second_done", "summed"))
            s_ysb, s_yt, s_fin, s_var, s_rs, s_out, s_nh = (sem(t + n) for n in ("sum_in_sbuf", "sum_turned", "added", "var", "rsd", "stored", "half"))
            H1, CB, Y, YT = (lambda e: ps[:, e % 2]), (lambda e: ps[:, 2 + e % 2]), ps[0:D, 4], ps[:, 5]
            LAG = 3
            read_at, turn_at, add_at = (3, 5, 6) if L == 0 else (2, 3, 3)

            with nc.Block() as block:
                @block.tensor
                def _(pe):
                    def second(c, e, s):
                        if e == 0:
                            if not isinstance(c, int) or c >= 1:
                                pe.wait_ge(s_ysb, c)
                        pe.wait_ge(s_wgt, s + 1)
                        last = nc.tensor.matmul(Y, w2s[L][:, e], wgt[e % DEEP], start=(e == 0), stop=(e == NS - 1))
                        if e == 0:
                            for n in range(3):
                                last = nc.tensor.matmul(Y, b2p[L][:, n], ct[:, c], start=False, stop=False)
                        last.then_inc(s_w2, 1)

                    def turn(c):
                        for k in range(TC):
                            last = nc.tensor.transpose(YT[:, D * k:D * k + D], y_sb[:, P * k:P * k + P], ident[0:D, 0:D])
                        last.then_inc(s_yt, 1)

                    def chunk(c):
                        known = isinstance(c, int)
                        for e in range(NS):
                            s = NS * c + e
                            if not known or s >= 2:
                                pe.wait_ge(s_hid, s - 1)
                            for n, src in enumerate((xa, xa, xb)):
                                last = nc.tensor.matmul(H1(e), wst[L][:, n, P * e:P * e + P], src[:, c], start=(n == 0), stop=(n == 2))
                            last.then_inc(s_h, 1)
                            if not known or s >= 2:
                                pe.wait_ge(s_wgt, s - 1)
                            nc.tensor.matmul(CB(e), selb[:, e], ct[:, c], start=True, stop=True).then_inc(s_cb, 1)
                            turning = e == turn_at and (not known or c >= 1)
                            if turning:
                                pe.wait_ge(s_ysb, c)
                                if not known or c >= 2:
                                    pe.wait_ge(s_fin, c - 1)
                            if not known or s >= LAG:
                                if e >= LAG:
                                    second(c, e - LAG, s - LAG)
                                else:
                                    second(c - 1, e - LAG + NS, s - LAG)
                            if turning:
                                turn(c - 1)

                    chunk(0)
                    with pe.Fori(1, CH) as c:
                        chunk(c)
                    for e in range(NS - LAG, NS):
                        second(CH - 1, e, NS * (CH - 1) + e)
                    pe.wait_ge(s_ysb, CH)
                    pe.wait_ge(s_fin, CH - 1)
                    turn(CH - 1)

                @block.scalar
                def _(act):
                    def y_out(c):
                        act.wait_ge(s_w2, NS * (c + 1))
                        if not isinstance(c, int) or c >= 1:
                            act.wait_ge(s_yt, c)
                        nc.scalar.activation(y_sb, Y, ACT.Copy).then_inc(s_ysb, 1)

                    def chunk(c):
                        known = isinstance(c, int)
                        for e in range(NS):
                            s = NS * c + e
                            act.wait_ge(s_h, s + 1)
                            if not known or s >= DEEP:
                                act.wait_ge(s_wgt, s + 1 - DEEP)
                            nc.scalar.activation(hid[e % DEEP], H1(e), func, bias=b1s[L][:, e:e + 1]).then_inc(s_hid, 1)
                            if e == read_at and (not known or c >= 1):
                                y_out(c - 1)

                    chunk(0)
                    with act.Fori(1, CH) as c:
                        chunk(c)
                    y_out(CH - 1)

                @block.vector
                def _(dve):
                    link = chain(dve, t + "dve")

                    def finish(c):
                        y = YT[:, 0:TC * D].rearrange("p (t d) -> p t d", t=TC)
                        tl = span(TC * c, TC)
                        shape = [P, TC, D]

                        def total():
                            dve.wait_ge(s_yt, c + 1)
                            link(nc.vector.tensor_tensor(yy, y, xh[:, tl], ALU.add))

                        def mean():
                            link(nc.vector.tensor_reduce(st[:, 0], yy, AX.X, ALU.add))
                            link(nc.vector.tensor_scalar(st[:, 0], st[:, 0], -1.0 / D, None, ALU.mult))

                        def centre():
                            link(nc.vector.tensor_tensor(yy, yy, bc(st[:, 0].unsqueeze(2), shape), ALU.add))

                        def square():
                            link(nc.vector.tensor_tensor(yq, yy, yy, ALU.mult))

                        def variance():
                            link(nc.vector.tensor_reduce(st[:, 1], yq, AX.X, ALU.add))
                            nc.vector.tensor_scalar(st[:, 2], st[:, 1], 1.0 / D, EPS, ALU.mult, ALU.add).then_inc(s_var, 1)

                        def scale():
                            dve.wait_ge(s_rs, c + 1)
                            link(nc.vector.tensor_tensor(yy, yy, bc(st[:, 3].unsqueeze(2), shape), ALU.mult))

                        def gain():
                            link(nc.vector.tensor_tensor(yy, yy, bc(gb[:, 0].unsqueeze(1), shape), ALU.mult))

                        def shift():
                            link(nc.vector.tensor_tensor(yy, yy, bc(gb[:, 1].unsqueeze(1), shape), ALU.add))

                        def add():
                            nc.vector.tensor_tensor(res[:, tl], res[:, tl], yy, ALU.add).then_inc(s_fin, 1)
                            dve.wait_ge(s_fin, c + 1)

                        if L == 1:
                            return [total, add]
                        return [total, mean, centre, square, variance, lambda: None, scale, gain, shift, add]

                    def chunk(c):
                        known = isinstance(c, int)
                        for e in range(NS):
                            s = NS * c + e
                            dve.wait_ge(s_hid, s + 1)
                            dve.wait_ge(s_cb, s + 1)
                            if not known or s >= DEEP:
                                dve.wait_ge(s_w2, s + 1 - DEEP)
                            nc.vector.tensor_tensor(wgt[e % DEEP], hid[e % DEEP], CB(e), ALU.mult).then_inc(s_wgt, 1)
                            if not known or c >= 1:
                                steps = finish(c - 1)
                                n = e - add_at
                                for step in (steps[n:n + 1] if L == 0 else steps) if n >= 0 else ():
                                    step()

                    nc.vector.memset(nh, -0.5).then_inc(s_nh, 1)
                    chunk(0)
                    link.loop(chunk, 1, CH, 9 if L == 0 else 1)
                    for step in finish(CH - 1):
                        step()

                if L == 0:
                    @block.gpsimd
                    def _(pool):
                        pool.wait_ge(s_nh, 1)

                        def rsd(c):
                            pool.wait_ge(s_var, c + 1)
                            nc.gpsimd.tensor_tensor(st[:, 3], st[:, 2], nh, ALU.pow).then_inc(s_rs, 1)

                        with pool.Fori(0, CH) as c:
                            rsd(c)
                else:
                    @block.sync
                    def _(sp):
                        def store(c):
                            sp.wait_ge(s_fin, c + 1)
                            for tq in range(2):
                                n = P - tq
                                src = res[0:n].rearrange("p (b t) d -> p b t d", t=2)
                                sp.dma_start(out[bass.ds(2 * c, 2), P * tq:P * tq + n].rearrange("b w d -> w b d"),
                                             src[:, bass.ds(2 * c, 2), tq]).then_inc(s_out, 16)

                        with sp.Fori(0, CH) as c:
                            store(c)
                        sp.wait_ge(s_out, 16 * 2 * CH)

        def attention1():
            scale = (D // H) ** -0.5
            pos = [0]
            def take(n, dt=F32):
                a = big[:, pos[0]:pos[0] + n]
                pos[0] += n
                assert pos[0] <= 8192
                return a if dt == F32 else a.bitcast(dt)
            parts = [take(384, BF16).rearrange("p (s q) -> p s q", s=3) for _ in range(2)]
            qs = [take(128, BF16) for _ in range(4)]
            ks = [take(128, BF16) for _ in range(4)]
            qm = [take(128, BF16) for _ in range(2)]
            mhl = [take(128, BF16).rearrange("p (t m) -> p t m", t=2) for _ in range(2)]
            e_sb = [take(1024).rearrange("p (j c q) -> p j c q", j=2, c=2) for _ in range(2)]
            xs = [take(256)[0:D] for _ in range(2)]
            o_sb = [take(256)[0:OW] for _ in range(2)]
            rest = take(256)
            work = take(512)
            mx = work[:, 0:4].rearrange("p (j t) -> p j t", j=2)
            rinv = work[:, 8:24].rearrange("p (t h) -> p t h", t=2)
            rgate = work[:, 24:40].rearrange("p (t h) -> p t h", t=2)
            asum = work[:, 40:56].rearrange("p (t h) -> p t h", t=2)
            hsum = work[:, 64:64 + 2 * D].rearrange("p (t d) -> p t d", t=2)
            blend = work[:, 192:192 + 2 * D].rearrange("p (t d) -> p t d", t=2)
            oT_sb = work[:, 320:320 + P]

            S = ps[:, 0:2].rearrange("p j (t k) -> p j t k", t=2)
            T = ps[:, 2:4].rearrange("p j (c q) -> p j c q", c=2)
            O = ps[:, 4].rearrange("p (b q) -> p b q", b=2)
            QS, KS = ps[:, 5, 0:256], ps[:, 5, 256:512]
            QK, BT = ps[:, 6, 0:256], ps[:, 6, 256:384]
            MT = ps[:, 7, 0:P].bitcast(BF16)
            OT = ps[:, 7, P:P + 2 * OW].rearrange("p (t d) -> p t d", t=2)
            Y = ps[:, 7, 288:288 + P].rearrange("p (t d) -> p t d", t=2)

            s_xs, s_qkp, s_parts, s_st, s_q, s_k = (sem("L1_" + n) for n in ("xs_ready", "qk_projected", "parts_ready", "stacked", "q_in_sbuf", "k_in_sbuf"))
            s_S, s_mhl, s_mtp, s_qm = (sem("L1_" + n) for n in ("scores", "max_parts", "max_turned", "q_with_max"))
            s_T, s_E, s_v, s_PV, s_O = (sem("L1_" + n) for n in ("turned_scores", "exps", "values_padded", "outputs", "outputs_in_sbuf"))
            s_OT, s_otr, s_bl, s_oTp, s_oT, s_y, s_fin = (sem("L1_" + n) for n in (
                "outputs_turned", "turned_outputs_read", "blended", "blend_turned", "blend_in_sbuf", "projected", "added"))
            s_zero = sem("L1_max_zeroed")

            def at(k):
                return (k // PAIRS) % 2, k % PAIRS

            def head(j):
                return slice(64 * j, 64 * j + 64)

            with nc.Block() as block:
                @block.tensor
                def _(pe):
                    def project(b, par):
                        pe.wait_ge(s_xs, b + 1)
                        if not isinstance(b, int) or b >= 1:
                            pe.wait_ge(s_parts, b)
                        nc.tensor.matmul(QK, wqk1[:], xs[par], start=True, stop=True).then_inc(s_qkp, 1)

                    def stack(par, p):
                        for n, out_ in enumerate((QS, KS)):
                            for part in range(3):
                                last = nc.tensor.matmul(out_, selqk[:, 2 * p + n, part], parts[par][:, part], start=(part == 0), stop=(part == 2))
                        last.then_inc(s_st, 1)

                    def scores(k):
                        for j in range(2):
                            for tq in range(2):
                                last = nc.tensor.matmul(S[:, j, tq], qs[k % 4][head(j), P * tq:P * tq + P], ks[k % 4][head(j)], start=True, stop=True)
                        last.then_inc(s_S, 1)

                    def turned_scores(k):
                        for j in range(2):
                            for c in range(2):
                                last = nc.tensor.matmul(T[:, j, c], ks[k % 4][head(j), P * c:P * c + P], qm[k % 2][head(j)], start=True, stop=True)
                        last.then_inc(s_T, 1)

                    def outputs(k):
                        par, p = at(k)
                        for j in range(2):
                            h = 2 * p + j
                            for c in range(2):
                                n = P - c
                                last = nc.tensor.matmul(O[0:OW, par], v1pad[par][0:n, c, OW * h:OW * h + OW], e_sb[k % 2][0:n, j, c],
                                                        start=(h == 0 and c == 0), stop=(h == H - 1 and c == 1))
                        last.then_inc(s_PV, 1)

                    def slot(j, k, do=("unit", "pv", "tail")):
                        U = 2 * PAIRS * j + k
                        known = isinstance(j, int)
                        par, p = at(k)
                        b = 2 * j + par
                        if "unit" in do:
                            pe.wait_ge(s_mhl, U + 1)
                            if not known or U >= 1:
                                pe.wait_ge(s_qm, U)
                            if p == 3 and (not known or b >= 1):
                                pe.wait_ge(s_otr, b)
                            if p == 1 and (not known or b >= 2):
                                pe.wait_ge(s_fin, b - 1)
                            for tq in range(2):
                                last = nc.tensor.transpose(MT[:, P * tq:P * tq + P], mhl[k % 2][:, tq], ident_b[:])
                            last.then_inc(s_mtp, 1)
                            pe.wait_ge(s_q, U + 2)
                            pe.wait_ge(s_k, U + 2)
                            scores(k + 1)
                            if p == 2:
                                pe.wait_ge(s_parts, b + 2)
                            stack(at(k + 2)[0], at(k + 2)[1])
                        if "tail" in do:
                            if "unit" in do and p in (0, 2) and (not known or b >= (1 if p else 2)):
                                pe.wait_ge(s_qm, U + 1)
                            if p == 2 and "unit" not in do:
                                pe.wait_ge(s_fin, b - 1)
                            if p == 2 and (not known or b >= 1):
                                pe.wait_ge(s_O, b)
                                for tq in range(2):
                                    last = nc.tensor.transpose(OT[:, tq], o_sb[(par + 1) % 2][:, P * tq:P * tq + P], ident[0:OW, 0:OW])
                                last.then_inc(s_OT, 1)
                            if p == 3 and (not known or b >= 1):
                                pe.wait_ge(s_bl, b)
                                if "unit" in do:
                                    pe.wait_ge(s_parts, b + 2)
                                nc.tensor.transpose(BT, blend.rearrange("p t d -> p (t d)"), ident).then_inc(s_oTp, 1)
                            if p == 0 and (not known or b >= 2):
                                pe.wait_ge(s_oT, b - 1)
                                nc.tensor.matmul(Y.rearrange("p t d -> p (t d)"), oT_sb, wps[:], start=True, stop=True).then_inc(s_y, 1)
                            if p == 0 and "unit" in do:
                                project(b + 1, (par + 1) % 2)
                        if "pv" in do and (not known or U >= 2):
                            pe.wait_ge(s_E, U - 1)
                            if p == 2:
                                pe.wait_ge(s_v, b + 1)
                                if not known or b >= 1:
                                    pe.wait_ge(s_O, b)
                            outputs(k - 2)
                        if "unit" in do:
                            pe.wait_ge(s_qm, U + 1)
                            if not known or U >= 1:
                                pe.wait_ge(s_E, U)
                            turned_scores(k)

                    project(0, 0)
                    pe.wait_ge(s_parts, 1)
                    stack(0, 0)
                    pe.wait_ge(s_q, 1)
                    pe.wait_ge(s_k, 1)
                    stack(0, 1)
                    scores(0)
                    for k in range(2 * PAIRS):
                        slot(0, k)
                    with pe.Fori(1, B // 2) as j:
                        for k in range(2 * PAIRS):
                            slot(j, k)
                    for k in range(5):
                        slot(B // 2, k, ("pv", "tail") if k < 2 else ("tail",))

                @block.scalar
                def _(act):
                    def stack_out(U, k):
                        act.wait_ge(s_st, U + 1)
                        if not isinstance(U, int) or U >= 4:
                            act.wait_ge(s_T, U - 3)
                        nc.scalar.activation(qs[k % 4], QS, ACT.Copy).then_inc(s_q, 1)
                        nc.scalar.activation(ks[k % 4], KS, ACT.Identity, bias=cst[:, o_neg:o_neg + 1]).then_inc(s_k, 1)

                    def slot(j, k, do=("unit", "o")):
                        U = 2 * PAIRS * j + k
                        known = isinstance(j, int)
                        par, p = at(k)
                        b = 2 * j + par
                        if "unit" in do:
                            stack_out(U + 2, k + 2)
                        if p == 1 and (not known or b >= 1):
                            act.wait_ge(s_PV, U - 1)
                            pl = (par + 1) % 2
                            if not known or b >= 3:
                                act.wait_ge(s_OT, b - 2)
                            nc.scalar.activation(o_sb[pl], O[0:OW, pl], ACT.Copy).then_inc(s_O, 1)
                        if p == 3 and (not known or b >= 1):
                            act.wait_ge(s_oTp, b)
                            if not known or b >= 2:
                                act.wait_ge(s_y, b - 1)
                            nc.scalar.activation(oT_sb, BT, ACT.Copy).then_inc(s_oT, 1)
                        if "unit" in do:
                            act.wait_ge(s_T, U + 1)
                            if not known or U >= 2:
                                act.wait_ge(s_PV, U - 1)
                            nc.scalar.activation(e_sb[k % 2], T, ACT.Exp, scale=scale).then_inc(s_E, 1)

                    stack_out(0, 0)
                    stack_out(1, 1)
                    for k in range(2 * PAIRS):
                        slot(0, k)
                    with act.Fori(1, B // 2) as j:
                        for k in range(2 * PAIRS):
                            slot(j, k)
                    for k in range(4):
                        slot(B // 2, k, ("o",))

                @block.vector
                def _(dve):
                    link = chain(dve, "L1_dve")

                    def split(b, par):
                        dve.wait_ge(s_qkp, b + 1)
                        if not isinstance(b, int) or b >= 2:
                            dve.wait_ge(s_st, PAIRS * (b - 1))
                        hi, md, lo = (parts[par][:, n] for n in range(3))
                        link(nc.vector.tensor_copy(hi, QK))
                        link(nc.vector.tensor_tensor(rest, QK, hi, ALU.subtract))
                        link(nc.vector.tensor_copy(md, rest))
                        nc.vector.tensor_tensor(lo, rest, md, ALU.subtract).then_inc(s_parts, 1)

                    def maxima(U, k):
                        dve.wait_ge(s_S, U + 1)
                        link(nc.vector.tensor_reduce(mx, S[:, :, :, 0:NW], AX.X, ALU.max))
                        if not isinstance(U, int) or U >= 2:
                            dve.wait_ge(s_mtp, U - 1)
                        m = mhl[k % 2].rearrange("p t (j c) -> p t j c", j=2)[:, :, :, ROWS:ROWS + 2]
                        mt = mx.rearrange("p j t -> p t j")
                        link(nc.vector.tensor_copy(m[:, :, :, 0], mt))
                        nc.vector.tensor_tensor(m[:, :, :, 1], mt, m[:, :, :, 0], ALU.subtract).then_inc(s_mhl, 1)

                    def slot(j, k, do=("unit",)):
                        U = 2 * PAIRS * j + k
                        known = isinstance(j, int)
                        par, p = at(k)
                        b = 2 * j + par
                        if "unit" in do:
                            dve.wait_ge(s_mtp, U + 1)
                            if not known or U >= 2:
                                dve.wait_ge(s_T, U - 1)
                            nc.vector.tensor_tensor(qm[k % 2], qs[k % 4], MT, ALU.add).then_inc(s_qm, 1)
                            maxima(U + 1, k + 1)
                        if p == 2 and (not known or b >= 1):
                            dve.wait_ge(s_OT, b)
                            l = OT[:, :, D:OW]
                            link(nc.vector.reciprocal(rinv, l))
                            link(nc.vector.tensor_tensor(rgate, rinv, bc(omg.unsqueeze(1), [P, 2, H]), ALU.mult))
                            link(nc.vector.tensor_tensor(asum, l, rgate, ALU.mult))
                            shape = [P, 2, H, D // H]
                            by_head = lambda a: a.rearrange("p t (h d) -> p t h d", h=H)
                            if not known or b >= 2:
                                dve.wait_ge(s_oTp, b - 1)
                            nc.vector.tensor_tensor(by_head(blend), by_head(OT[:, :, 0:D]), bc(rgate.unsqueeze(3), shape), ALU.mult).then_inc(s_otr, 1)
                            link(nc.vector.tensor_tensor(asum, asum, gsum, ALU.add))
                            link(nc.vector.reciprocal(asum, asum))
                            dve.wait_ge(s_otr, b)
                            link(nc.vector.tensor_tensor(blend, blend, posv[:, :, b - 1], ALU.add))
                            nc.vector.tensor_tensor(by_head(blend), by_head(blend), bc(asum.unsqueeze(3), shape), ALU.mult).then_inc(s_bl, 1)
                        if p == 0 and (not known or b >= 2):
                            dve.wait_ge(s_y, b - 1)
                            link(nc.vector.tensor_tensor(hsum, Y, bc(bprojb[:].unsqueeze(1), [P, 2, D]), ALU.add))
                            rs = res[:, span(2 * (b - 2), 2)]
                            nc.vector.tensor_tensor(rs, rs, hsum, ALU.add).then_inc(s_fin, 1)
                            dve.wait_ge(s_fin, b - 1)
                        if p == 0 and "unit" in do:
                            split(b + 1, (par + 1) % 2)

                    for n in range(2):
                        nc.vector.memset(mhl[n], 0.0).then_inc(s_zero, 1)
                    dve.wait_ge(s_zero, 2)
                    split(0, 0)
                    maxima(0, 0)
                    for k in range(2 * PAIRS):
                        slot(0, k)
                    per = 2 * (4 * 2 + 6 + 1 + 3)
                    link.loop(lambda j: [slot(j, k) for k in range(2 * PAIRS)], 1, B // 2, per)
                    for k in range(5):
                        slot(B // 2, k, ())

                @block.gpsimd
                def _(pool):
                    def fetch(b, par):
                        if not isinstance(b, int) or b >= 2:
                            pool.wait_ge(s_qkp, b - 1)
                        nc.gpsimd.tensor_copy(xs[par], xT[:, b]).then_inc(s_xs, 1)

                    def pad(b, par):
                        if not isinstance(b, int) or b >= 2:
                            pool.wait_ge(s_PV, PAIRS * (b - 1))
                        for c in range(2):
                            last = nc.gpsimd.tensor_copy(v1own[par][:, c, :, 0:D // H],
                                                         vall[:, 2 * b + c].rearrange("p (h d) -> p h d", h=H))
                        last.then_inc(s_v, 1)

                    for b in range(2):
                        fetch(b, b)
                        pad(b, b)
                    with pool.Fori(1, B // 2) as j:
                        for par in range(2):
                            fetch(2 * j + par, par)
                            pad(2 * j + par, par)
                    fetch(B, 0)

        def attention_prep1():
            sco = big[:, 0:4096].rearrange("p (t h k) -> p t h k", t=2, h=H)
            d2 = big[:, 4096:4608].rearrange("p (t k) -> p t k", t=2)
            term = big[:, 4608:5120].rearrange("p (t k) -> p t k", t=2)
            posT = big[:, 5120:5120 + 4096].rearrange("p (h c q) -> p h c q", h=H, c=2)
            st = big[:, 9216:9216 + 128]
            pmax = st[:, 0:16].rearrange("p (t h) -> p t h", t=2)
            psum = st[:, 16:32].rearrange("p (t h) -> p t h", t=2)
            pinv = st[:, 32:48].rearrange("p (t h) -> p t h", t=2)
            zb = st[:, 48:56]
            gt = st[:, 56:64]
            raw_sel = big[:, 9728:9728 + 3072]
            s_rs, s_rsb = sem("a1_selectors_in"), sem("a1_selectors")
            s_tr, s_xT, s_v, s_vo = (sem("a1_" + n) for n in ("turned", "xT", "values", "values_out"))
            s_sco, s_max, s_exp, s_inv, s_g, s_g1 = (sem("a1_" + n) for n in ("pos_scores", "pos_max", "pos_exp", "pos_scale", "gate_exp", "gate"))
            s_pt, s_ptc, s_pv, s_pvo, s_pad = (sem("a1_" + n) for n in ("pos_turned", "pos_turned_out", "pos_values", "pos_values_out", "padded"))

            def pe_work(pe, s_xh):
                for c in range(CH + 1):
                    if c < CH:
                        pe.wait_ge(s_xh, c // (CH // 2) + 1)
                        if c >= 2:
                            pe.wait_ge(s_xT, c - 1)
                        turned(c, c % 2, xh[:]).then_inc(s_tr, 1)
                    if c >= 1:
                        d = c - 1
                        pe.wait_ge(s_xT, d + 1)
                        if d >= 2:
                            pe.wait_ge(s_vo, d - 1)
                        for k in range(TC):
                            last = nc.tensor.matmul(ps[:, 2 + d % 2, D * k:D * k + D], xT[:, 2 * d + k // 2, P * (k % 2):P * (k % 2) + P], wvs[:], start=True, stop=True)
                        last.then_inc(s_v, 1)
                for h in range(H):
                    pe.wait_ge(s_exp, 16)
                    if h >= 2:
                        pe.wait_ge(s_ptc, h - 1)
                    for c in range(2):
                        for tq in range(2):
                            last = nc.tensor.transpose(ps[:, h % 2, 256 * c + P * tq:256 * c + P * tq + P], sco[:, tq, h, P * c:P * c + P], ident)
                    last.then_inc(s_pt, 1)
                pe.wait_ge(s_ptc, H)
                pe.wait_ge(s_vo, CH)
                v = vall[:].rearrange("p (b c) (h d) -> p b c h d", c=2, h=H)
                for tq in range(2):
                    for g in range(2):
                        for hh in range(4):
                            h = 4 * g + hh
                            for c in range(2):
                                n = P - c
                                last = nc.tensor.matmul(ps[:, 4 + 2 * tq + g, P * hh:P * hh + P], posT[0:n, h, c, P * tq:P * tq + P], v[0:n, :, c, h],
                                                        start=(c == 0), stop=(c == 1))
                        last.then_inc(s_pv, 1)

            def act_work(act):
                for c in range(CH):
                    act.wait_ge(s_tr, c + 1)
                    nc.scalar.activation(xT[:, 2 * c:2 * c + 2], ps[0:D, c % 2].rearrange("p (b q) -> p b q", b=2), ACT.Copy).then_inc(s_xT, 1)
                act.wait_ge(s_rs, 16)
                nc.scalar.activation(selqk.rearrange("p a s m -> p (a s m)"), raw_sel, ACT.Copy).then_inc(s_rsb, 1)
                nc.scalar.activation(gt, posw[:, 4], ACT.Exp, scale=-1.0).then_inc(s_g, 1)
                act.wait_ge(s_max, 1)
                for tq in range(2):
                    for h in range(H):
                        nc.scalar.activation(sco[:, tq, h], sco[:, tq, h], ACT.Exp, bias=pmax[:, tq, h:h + 1]).then_inc(s_exp, 1)
                for h in range(H):
                    act.wait_ge(s_pt, h + 1)
                    nc.scalar.activation(posT[:, h], ps[:, h % 2].rearrange("p (c q) -> p c q", c=2), ACT.Copy).then_inc(s_ptc, 1)

            def dve_work(dve, link):
                dve.wait_ge(s_sco, 1)
                link(nc.vector.tensor_reduce(pmax, sco[:, :, :, 0:NW], AX.X, ALU.max))
                nc.vector.tensor_scalar(pmax, pmax, -1.0, None, ALU.mult).then_inc(s_max, 1)
                for c in range(CH):
                    dve.wait_ge(s_v, c + 1)
                    nc.vector.tensor_copy(vall[:, TC * c:TC * c + TC], ps[:, 2 + c % 2, 0:TC * D].rearrange("p (t d) -> p t d", t=TC)).then_inc(s_vo, 1)
                dve.wait_ge(s_g, 1)
                link(nc.vector.tensor_scalar(gt, gt, 1.0, None, ALU.add))
                link(nc.vector.reciprocal(gt, gt))
                link(nc.vector.tensor_scalar(omg, gt, -1.0, 1.0, ALU.mult, ALU.add))
                dve.wait_ge(s_exp, 16)
                link(nc.vector.tensor_reduce(psum, sco[:, :, :, 0:NW], AX.X, ALU.add))
                link(nc.vector.reciprocal(pinv, psum))
                link(nc.vector.tensor_tensor(pinv, pinv, bc(gt.unsqueeze(1), [P, 2, H]), ALU.mult))
                link(nc.vector.tensor_tensor(gsum, psum, pinv, ALU.mult))
                for tq in range(2):
                    for g in range(2):
                        dve.wait_ge(s_pv, 2 * tq + g + 1)
                        for hh in range(4):
                            h = 4 * g + hh
                            link(nc.vector.tensor_scalar(posv[:, tq, :, 8 * h:8 * h + 8], ps[:, 4 + 2 * tq + g, P * hh:P * hh + P].rearrange("p (b d) -> p b d", b=B),
                                                         pinv[:, tq, h:h + 1], None, ALU.mult))

            def pool_work(pool):
                link = chain(pool, "a1_pool")
                link(nc.gpsimd.tensor_tensor(d2, dist, dist, ALU.mult))
                link(nc.gpsimd.tensor_scalar(zb, posw[:, 1], 0.0, None, ALU.mult))
                link(nc.gpsimd.tensor_tensor(zb, zb, posw[:, 3], ALU.add))
                for h in range(H):
                    link(nc.gpsimd.tensor_scalar(term, dist, posw[:, 0, h:h + 1], None, ALU.mult))
                    link(nc.gpsimd.tensor_scalar(sco[:, :, h], d2, posw[:, 2, h:h + 1], zb[:, h:h + 1], ALU.mult, ALU.add))
                    link(nc.gpsimd.tensor_tensor(sco[:, :, h], sco[:, :, h], term, ALU.add))
                nc.gpsimd.memset(sco[:, :, :, NW:NW + 1], -1e30).then_inc(s_sco, 1)

            def sp_work(sp):
                sp.dma_start(raw_sel, split_sel).then_inc(s_rs, 16)
                sp.wait_ge(s_rs, 16)

            norm_all("a1", pe_work, act_work, dve_work, pool_work, sp_work)

            with nc.Block() as block:
                @block.gpsimd
                def _(pool):
                    link = chain(pool, "a1_pad")
                    for n in range(2):
                        link(nc.gpsimd.memset(v1flat[n], 0.0))
                        link(nc.gpsimd.memset(v1flat[n][:, :, D:H * OW:OW + 1], 1.0))

        phase(tokens)
        phase(attention_prep0)
        phase(attention0)
        phase(experts_prep, 0)
        phase(experts, 0)
        phase(attention_prep1)
        phase(attention1)
        phase(experts_prep, 1)
        phase(experts, 1)


def tap_table():
    f = np.float32
    n = (SIG - 1) * UP + 1
    pos = (np.arange(n, dtype=f) / f(n - 1)) * f(SIG - 1)
    i0 = np.floor(pos)
    frac = (pos - i0).astype(f)
    A = f(-0.75)
    table = np.zeros((2 * P, TAPS, WIN), f)
    for k in range(-1, 3):
        at = np.abs(frac - f(k)).astype(f)
        near = ((A + f(2)) * at - (A + f(3))) * at * at + f(1)
        far = ((A * at - f(5) * A) * at + f(8) * A) * at - f(4) * A
        wk = np.where(at <= 1, near, np.where(at < 2, far, f(0))).astype(f)
        for p in range(NW * WIN):
            w, j = divmod(p, WIN)
            o = int(i0[p]) + k - (HOP * w + j // UP)
            assert -2 <= o <= 2 and (o > -2 or j % UP == 0)
            table[w, o + 2, j] += wk[p]
    table[NW] = table[NW - 1]
    return np.ascontiguousarray(table.reshape(2, P, TAPS, WIN).transpose(1, 0, 2, 3))


def constant_table():
    f = np.float32
    ident = np.eye(P, dtype=f)
    n, k = np.arange(WIN)[:, None], np.arange(WIN)[None, :]
    ang = 2 * np.pi * n / WIN
    cols = np.where(k < NB, np.cos(ang * k), np.sin(ang * (k - NB + 1)))
    dft = np.zeros((P, P))
    dft[:WIN, :WIN] = dft[WIN:, WIN:] = cols
    iota = np.tile(np.arange(16), (P, 1))
    q = np.arange(P)[:, None, None] + P * np.arange(2)[None, :, None]
    dist = (np.arange(256)[None, None, :] - q).reshape(P, 512)
    selm = np.zeros((P, P))
    for i in range(4):
        selm[32 * i:32 * i + 2] = -1
    sel0 = np.zeros((P, 16, P))
    sel1 = np.zeros((P, 4, 2, 64))
    for part in range(3):
        for e in range(16):
            sel0[16 * part + e, e] = 1
        for e in range(8):
            sel1[8 * part + e, e // 2, e % 2] = 1
    neg = np.zeros((P, 1))
    for j in range(2):
        neg[64 * j + ROWS:64 * j + ROWS + 2] = -1
    return np.concatenate([a.reshape(P, -1).astype(f) for a in (ident, dft, iota, dist, selm, sel0, sel1, neg)], axis=1)


def stack_table():
    hd = D // H
    sel = np.zeros((P, H, 3, P), np.float32)
    for p in range(PAIRS):
        for n, takes in enumerate((Q_PART, K_PART)):
            for j in range(2):
                for product, part in enumerate(takes):
                    for d in range(hd):
                        sel[D * n + hd * (2 * p + j) + d, 2 * p + n, part, 64 * j + hd * product + d] = 1
    return sel


def kernel(**inputs):
    import concourse.bacc as _bacc
    from concourse.bass_utils import run_bass_kernel_spmd as _run

    a = {k: np.asarray(v) for k, v in inputs.items()}

    def heads(w):
        return w.transpose(2, 0, 1).reshape(D, -1)

    gamma_beta = np.stack([a["L0_ffn_gamma"], a["L0_ffn_beta"]])
    wpos = np.concatenate([a["L1_attn_Wpos"].T, a["L1_attn_bpos"][None], a["L1_attn_gating"][None]])
    twice = lambda w: np.concatenate([w, w])
    w1_0 = a["L0_ffn_w1"].transpose(1, 0, 2).reshape(D, -1)
    w1_1 = a["L1_ffn_w1"].transpose(1, 0, 2).reshape(D, -1)
    feeds = {
        "x": a["x"], "taps": tap_table(), "consts": constant_table(),
        "wq0": heads(a["L0_attn_Q"]), "wk0": heads(a["L0_attn_K"]),
        "vo": a["L0_attn_VO"].transpose(1, 0, 2).reshape(D, -1),
        "gate_w0": a["L0_ffn_gate_w"], "gate_b0": a["L0_ffn_gate_b"][:, None],
        "w1_0": twice(w1_0), "b1_0": a["L0_ffn_b1"].T, "w2_0": a["L0_ffn_w2"].transpose(1, 0, 2),
        "b2_0": np.concatenate([a["L0_ffn_b2"]] * 3), "gamma": gamma_beta,
        "wqk": a["L1_attn_Wqk"].T, "split_sel": stack_table(), "wv1": a["L1_attn_Wv"].T, "wpos": wpos,
        "wproj": a["L1_attn_Wproj"].T, "bproj": a["L1_attn_bproj"][None],
        "router": a["L1_ffn_router_w"].T, "w1_1": twice(w1_1),
        "b1_1": a["L1_ffn_b1"].reshape(4, P).T,
        "w2_1": a["L1_ffn_w2"].reshape(4, P, D).transpose(1, 0, 2),
        "b2_1": np.concatenate([a["L1_ffn_b2"]] * 3),
    }
    nc = _bacc.Bacc("TRN2", target_bir_lowering=False, num_devices=1)
    arrays, args = {}, []
    for name, v in feeds.items():
        v = np.ascontiguousarray(v)
        arrays[f"in_{name}"] = v
        args.append(nc.dram_tensor(f"in_{name}", v.shape, mybir.dt.from_np(v.dtype), kind="ExternalInput").ap())
    args.append(nc.dram_tensor("out_tokens", (B, NW, D), F32, kind="ExternalOutput").ap())
    tower(nc, *args)
    r = _run(nc, [arrays], core_ids=[0])
    return r.results[0]["out_tokens"]
```

```python
from contextlib import ExitStack

import numpy as np

import concourse.bass as bass
from concourse import mybir

ALU = mybir.AluOpType
ACT = mybir.ActivationFunctionType
AX = mybir.AxisListType
F32 = mybir.dt.float32
F32R = mybir.dt.float32r
BF16 = mybir.dt.bfloat16
U32 = mybir.dt.uint32

P = 128
B, SIG = 16, 4096
UP = 4
WIN = 64
NW = 255
HOP = WIN // UP
TAPS = 5
REACH = HOP + TAPS - 1
NB = WIN // 2 + 1
D = WIN
WALL = 16 * P + 4 * P
Q0, K0, V0 = 0, 256, 512
GATE, ROUTER = slice(1024, 1040), slice(1040, 1048)
QK1, V1 = slice(1048, 1176), slice(1176, 1240)
W64 = 1240
NT = 2 * B
H = 8
PAIRS = H // 2
UNITS = B * PAIRS
CH = 8
TC = NT // CH
EPS = 1e-5
ALPHA, BETA = 0.12, 0.9
VW = D + 1
OW = D + H
VS = OW + D // H
ROWS = 6 * (D // H)
Q_PART = (0, 0, 1, 0, 2, 1)
K_PART = (0, 1, 0, 2, 0, 1)


def bc(ap, shape):
    return ap.broadcast_to(shape)


def span(start, n):
    return slice(start, start + n) if isinstance(start, int) else bass.ds(start, n)


class Chain:

    def __init__(self, eng, sem):
        self.eng, self.sem, self.n, self.base = eng, sem, 0, 0

    def __call__(self, ins):
        self.n += 1
        ins.then_inc(self.sem, 1)
        self.eng.wait_ge(self.sem, self.base + self.n)

    def loop(self, body, first, end, per):
        start = self.n
        with self.eng.Fori(first, end) as j:
            self.base = j * per - first * per
            body(j)
            assert self.n - start == per, (self.n - start, per)
            self.base = 0
        self.n = start + per * (end - first)


def tower(nc, x, taps, consts, w_raw, gate_b0, w1_01, b1_0, w2_0, b2_0, gamma,
          split_sel, wpos, wproj, bproj, b1_1, w2_1, b2_1, out):
    with ExitStack() as ctx:
        def sb(name, shape, dt=F32):
            return ctx.enter_context(nc.sbuf_tensor(name, shape, dt))

        ps = ctx.enter_context(nc.psum_tensor("ps", [P, 8, 512], F32))
        res = sb("res", [P, NT, D])
        vall = sb("vall", [P, 2, H, B, D // H])
        cols_area = sb("cols_area", [P, B + 1, 2 * P])
        xab = cols_area[:].rearrange("p b q -> p (b q)").bitcast(BF16).rearrange("p (k b q) -> p k b q", k=2, b=B + 1)
        columns = [xab[:, k, 0:B].rearrange("p b q -> p (b q)").rearrange("p (c q) -> p c q", c=CH) for k in range(2)]
        cst = sb("cst", [P, consts.shape[1]])
        ident_b = sb("ident_b", [P, P], BF16)
        small = sb("small", [P, 4 + H])
        rowsc = sb("rowsc", [P, 3, NT])
        w64 = sb("w64", [P, 3, W64], BF16)
        selqk = sb("selqk", [P, H, 3, P], BF16)
        pexp = sb("pexp", [P, 2, H, 256])
        pmax = sb("pmax", [P, 2, H])
        psum = sb("psum", [P, 2, H])
        wps = sb("wps", [P, P])
        bprojb = sb("bprojb", [P, D])
        gb = sb("gb", [P, 2, D])
        posw = sb("posw", [P, 5, H])
        gbs = sb("gbs", [P, 16])
        b1s = [sb("b1s0", [P, 16]), sb("b1s1", [P, 4])]
        w2s = [sb("w2s0", [P, 16, D]), sb("w2s1", [P, 4, D])]
        wall = sb("wall", [P, 3, WALL], BF16)
        wst = [wall[:, :, 0:16 * P], wall[:, :, 16 * P:WALL]]
        b2p = [sb("b2p0", [P, 3, D], BF16), sb("b2p1", [P, 3, D], BF16)]
        selb = sb("selb", [P, 16, P], BF16)
        big = sb("big", [P, 8 * 2048])
        mid = sb("mid", [P, 6 * 1024])
        x2 = big[:, 11264:15872].rearrange("p (t a d) -> p t a d", t=NT + TC, a=2)
        column_rest = [big[:, 6144 + 512 * n:6144 + 512 * n + 512] for n in range(2)]

        o_id = 0
        o_dft = o_id + P
        o_iota = o_dft + P
        o_dist = o_iota + 16
        o_sel0 = o_dist + 2 * 256
        o_sel1 = o_sel0 + 16 * P
        o_neg = o_sel1 + 4 * 2 * 64
        ident = cst[:, o_id:o_id + P]
        dft = cst[:, o_dft:o_dft + P]
        iota = cst[:, o_iota:o_iota + 16]
        dist = cst[:, o_dist:o_dist + 512].rearrange("p (t k) -> p t k", t=2)

        held = []

        def sem(name):
            held.append(nc.alloc_semaphore(name))
            return held[-1]

        def phase(program):
            program()
            nc.clear_and_free_semaphores(held)
            held.clear()
            nc.all_engine_barrier()

        def chain(eng, name):
            return Chain(eng, sem(name))

        def tokens():
            sig = mid[:, 0:2 * B * REACH].rearrange("p (t b s) -> p t b s", t=2, b=B)
            tw = mid[:, 640:640 + 2 * TAPS * WIN].rearrange("p (t k j) -> p t k j", t=2, k=TAPS)
            tmp = mid[:, 1280:1280 + 2048].rearrange("p (t b j) -> p t b j", t=2, b=B)
            area = lambda n: big[:, 2048 * n:2048 * (n + 1)].rearrange("p (t b j) -> p t b j", t=2, b=B)
            z, poly, gauss, power = area(0), area(1), area(2), area(3)
            kT = big[:, 8192:8192 + 2048].rearrange("p (g k) -> p g k", g=4)
            spec = lambda n: big[:, 10240 + 1056 * n:10240 + 1056 * (n + 1)].rearrange(
                "p (t b k) -> p t b k", t=2, b=B)
            mag, arg, mask, mt = spec(0), spec(1), spec(2), spec(3)
            low = spec(4)
            raw, raw_rest = mid[:, 3328:3328 + W64], big[:, 13408:13408 + W64]
            s_raw, s_pw_in, s_z2 = sem("tok_raw_weights_in"), sem("tok_pos_weights_in"), sem("tok_interp1_rest")
            d2 = big[:, 15520:16032].rearrange("p (t k) -> p t k", t=2)
            term = mid[:, 5424:5936].rearrange("p (t k) -> p t k", t=2)
            zb = small[:, 4:4 + H]
            top, cap, thr = (rowsc[:, n].rearrange("p (t b) -> p t b", t=2) for n in range(3))

            s_sig, s_tw, s_cst, s_w, s_wz = sem("tok_signal_in"), sem("tok_taps_in"), sem("tok_consts_in"), sem("weights_in"), sem("w_zeroed")
            s_z, s_sq, s_kw = [sem("tok_interp0"), sem("tok_interp1")], sem("tok_window_parts"), sem("tok_kernelled")
            s_tr, s_kT, s_ft, s_pw = sem("tok_turned"), sem("tok_turned_out"), sem("tok_ft"), sem("tok_power")
            s_m2, s_mag, s_arg, s_mask = sem("tok_power_sum"), sem("tok_mag"), sem("tok_arg"), sem("tok_mask")
            s_abs, s_log, s_sm = sem("tok_abs"), sem("tok_log"), sem("tok_small")

            with nc.Block() as block:
                def squares(act, g):
                    nc.scalar.activation(power[:, g // 2, 8 * (g % 2):8 * (g % 2) + 8],
                                         ps[:, 2 + g % 2].rearrange("p (b k) -> p b k", b=8), ACT.Square).then_inc(s_pw, 1)

                def interpolate(eng, ch, t, first_b, n):
                    ch.eng.wait_ge(s_tw, 16)
                    bs = slice(first_b, first_b + n)
                    shape = [P, n, HOP, UP]
                    first = lambda k: bc(sig[:, t, bs, k:k + HOP].unsqueeze(3), shape)
                    weight = lambda k: bc(tw[:, t, k].rearrange("p (m r) -> p m r", r=UP).unsqueeze(1), shape)
                    zz = z[:, t, bs].rearrange("p b (m r) -> p b m r", r=UP)
                    tt = tmp[:, t, bs].rearrange("p b (m r) -> p b m r", r=UP)
                    ch(eng.tensor_tensor(zz, first(1), weight(1), ALU.mult))
                    for k in range(2, TAPS):
                        ch(eng.tensor_tensor(tt, first(k), weight(k), ALU.mult))
                        ch(eng.tensor_tensor(zz, zz, tt, ALU.add))
                    w = bc(tw[:, t, 0, 0:WIN:UP].unsqueeze(1), [P, n, HOP])
                    ch(eng.tensor_tensor(tt[:, :, :, 0], sig[:, t, bs, 0:HOP], w, ALU.mult))
                    return eng.tensor_tensor(zz[:, :, :, 0], zz[:, :, :, 0], tt[:, :, :, 0], ALU.add)

                @block.sync
                def _(sp):
                    t0 = x.tensor
                    sp.dma_start(sig[1:P, 0], bass.AP(tensor=t0, offset=HOP - 2,
                                                      ap=[[HOP, P - 1], [SIG, B], [1, REACH]])).then_inc(s_sig, 16)
                    sp.dma_start(sig[0:1, 0, :, 2:REACH], bass.AP(tensor=t0, offset=0, ap=[[SIG, 1], [SIG, B], [1, REACH - 2]])).then_inc(s_sig, 16)
                    sp.dma_start(posw[:], pos_in).then_inc(s_pw_in, 16)
                    sp.dma_start(cst[:], consts).then_inc(s_cst, 16)
                    sp.dma_start(raw, w_raw).then_inc(s_raw, 16)
                    sp.wait_ge(s_wz, 1)
                    for dst, src in ((gbs[:], gate_bias),
                                     (wps[0:D, 0:D], wproj), (wps[D:P, D:P], wproj),
                                     (b1s[0][:], b1_0), (b1s[1][:], b1_1)):
                        sp.dma_start(dst, src).then_inc(s_w, 16)
                    sp.wait_ge(s_w, 16 * 5)
                    sp.wait_ge(s_cst, 16)
                    sp.wait_ge(s_tw, 16)

                @block.scalar
                def _(act):
                    act.dma_start(sig[P - 1:P, 1], bass.AP(tensor=x.tensor, offset=HOP * (NW - 1) - 2, ap=[[SIG, 1], [SIG, B], [1, REACH]])).then_inc(s_sig, 16)
                    act.dma_start(sig[0:P - 1, 1], bass.AP(tensor=x.tensor, offset=HOP * P - 2,
                                                           ap=[[HOP, P - 1], [SIG, B], [1, REACH]])).then_inc(s_sig, 16)
                    act.dma_start(tw, taps).then_inc(s_tw, 16)
                    act.wait_ge(s_sm, 3)
                    for t in (0, 1):
                        act.wait_ge(s_z[t], 1)
                        if t == 1:
                            act.wait_ge(s_z2, 1)
                        nc.scalar.activation(poly[:, t], z[:, t], ACT.Square, bias=small[:, 0:1], scale=float(np.sqrt(0.5))).then_inc(s_sq, 1)
                        nc.scalar.activation(gauss[:, t], z[:, t], ACT.Square, bias=small[:, 1:2]).then_inc(s_sq, 1)
                        act.wait_ge(s_sq, 3 * t + 2)
                        nc.scalar.activation(gauss[:, t], gauss[:, t], ACT.Exp, scale=-0.5).then_inc(s_sq, 1)
                    for g in range(4):
                        act.wait_ge(s_tr, g + 1)
                        nc.scalar.activation(kT[:, g], ps[:, g % 2], ACT.Copy).then_inc(s_kT, 1)
                        if g:
                            act.wait_ge(s_ft, g)
                            squares(act, g - 1)
                    act.wait_ge(s_ft, 4)
                    squares(act, 3)
                    for t in (0, 1):
                        act.wait_ge(s_m2, t + 1)
                        nc.scalar.activation(mag[:, t], power[:, t, :, 0:NB], ACT.Sqrt).then_inc(s_mag, 1)
                    for t in (0, 1):
                        act.wait_ge(s_arg, t + 1)
                        nc.scalar.activation(mask[:, t], arg[:, t], ACT.Sigmoid).then_inc(s_mask, 1)
                    nc.scalar.activation(small[:, 3:4], small[:, 2:3], ACT.Exp).then_inc(s_sm, 1)
                    for t in (0, 1):
                        act.wait_ge(s_abs, t + 1)
                        nc.scalar.activation(arg[:, t], arg[:, t], ACT.Abs).then_inc(s_log, 1)
                        act.wait_ge(s_log, 2 * t + 1)
                        nc.scalar.activation(arg[:, t], arg[:, t], ACT.Exp, scale=-1.0).then_inc(s_log, 1)
                    for t in (0, 1):
                        act.wait_ge(s_log, 4)
                        nc.scalar.activation(arg[:, t], arg[:, t], ACT.Ln, bias=small[:, 2:3]).then_inc(s_log, 1)

                @block.vector
                def _(dve):
                    link = chain(dve, "tok_dve")
                    nc.vector.memset(small[:, 0:1], 1.3 * float(np.sqrt(0.5))).then_inc(s_sm, 1)
                    nc.vector.memset(small[:, 1:2], -0.7).then_inc(s_sm, 1)
                    nc.vector.memset(small[:, 2:3], 1.0).then_inc(s_sm, 1)
                    dve.wait_ge(s_sig, 16 * 4)
                    link(nc.vector.tensor_copy(sig[0:1, 0, :, 0:2], bc(sig[0:1, 0, :, 2:3], [1, B, 2])))
                    interpolate(nc.vector, link, 0, 0, B).then_inc(s_z[0], 1)
                    interpolate(nc.vector, link, 1, B - 6, 6).then_inc(s_z2, 1)
                    for t in (0, 1):
                        dve.wait_ge(s_sq, 3 * t + 3)
                        nc.vector.scalar_tensor_tensor(out=z[:, t].rearrange("p b j -> p (b j)"), in0=gauss[:, t].rearrange("p b j -> p (b j)"), scalar=0.5,
                                                       in1=poly[:, t].rearrange("p b j -> p (b j)"), op0=ALU.mult, op1=ALU.add).then_inc(s_kw, 1)
                    dve.wait_ge(s_raw, 16)
                    hi, md, lo = (w64[:, s] for s in range(3))
                    link(nc.vector.tensor_copy(hi, raw))
                    link(nc.vector.tensor_tensor(raw_rest, raw, hi, ALU.subtract))
                    link(nc.vector.tensor_copy(md, raw_rest))
                    link(nc.vector.tensor_tensor(lo[0:D], raw_rest[0:D], md[0:D], ALU.subtract))
                    link(nc.vector.tensor_copy(lo[D:P], hi[D:P]))
                    dve.wait_ge(s_pw, 4)
                    over = lambda a, t: bc(a[:, t].unsqueeze(2), [P, B, NB])
                    for t in (0, 1):
                        nc.vector.tensor_tensor(power[:, t, :, 1:32], power[:, t, :, 1:32], power[:, t, :, 33:64], ALU.add).then_inc(s_m2, 1)
                    for t in (0, 1):
                        dve.wait_ge(s_mag, t + 1)
                        link(nc.vector.tensor_reduce(top[:, t], mag[:, t], AX.X, ALU.max))
                        link(nc.vector.tensor_scalar(thr[:, t], top[:, t], -ALPHA, None, ALU.mult))
                        nc.vector.tensor_tensor(arg[:, t], mag[:, t], over(thr, t), ALU.add).then_inc(s_arg, 1)
                    link(nc.vector.tensor_scalar(cap, top, BETA, None, ALU.mult))
                    for t in (0, 1):
                        dve.wait_ge(s_mask, t + 1)
                        link(nc.vector.tensor_tensor(mt[:, t], mag[:, t], mask[:, t], ALU.mult))
                        nc.vector.tensor_tensor(arg[:, t], mt[:, t], over(cap, t), ALU.subtract).then_inc(s_abs, 1)
                    for t in (0, 1):
                        link(nc.vector.tensor_tensor(low[:, t], mt[:, t], over(cap, t), ALU.min))
                    rows = res[:].rearrange("p (b t) d -> p t b d", t=2)
                    for t in (0, 1):
                        dve.wait_ge(s_log, 5 + t)
                        link(nc.vector.tensor_tensor(rows[:, t, :, 0:NB], low[:, t], arg[:, t], ALU.subtract))
                        link(nc.vector.tensor_tensor(rows[:, t, :, NB:WIN], low[:, t, :, NB - 2:0:-1], arg[:, t, :, NB - 2:0:-1], ALU.subtract))

                @block.gpsimd
                def _(pool):
                    link = chain(pool, "tok_pool")
                    nc.gpsimd.memset(wps[:], 0.0).then_inc(s_wz, 1)
                    pool.wait_ge(s_sig, 16 * 4)
                    interpolate(nc.gpsimd, link, 1, 0, B - 6).then_inc(s_z[1], 1)
                    link(nc.gpsimd.memset(xab[:, :, B], 0.0))
                    pool.wait_ge(s_cst, 16)
                    link(nc.gpsimd.tensor_copy(ident_b[:], ident))
                    pool.wait_ge(s_pw_in, 16)
                    link(nc.gpsimd.tensor_tensor(d2, dist, dist, ALU.mult))
                    link(nc.gpsimd.tensor_scalar(zb, posw[:, 1], 0.0, None, ALU.mult))
                    link(nc.gpsimd.tensor_tensor(zb, zb, posw[:, 3], ALU.add))
                    for h in range(H):
                        link(nc.gpsimd.tensor_scalar(term, dist, posw[:, 0, h:h + 1], zb[:, h:h + 1], ALU.mult, ALU.add))
                        link(nc.gpsimd.tensor_scalar(pexp[:, :, h], d2, posw[:, 2, h:h + 1], 0.0, ALU.mult, ALU.add))
                        link(nc.gpsimd.tensor_tensor(pexp[:, :, h], pexp[:, :, h], term, ALU.add))
                    link(nc.gpsimd.memset(pexp[:, :, :, NW:NW + 1], -1e30))

                @block.tensor
                def _(pe):
                    pe.wait_ge(s_cst, 16)
                    for g in range(5):
                        if g < 4:
                            pe.wait_ge(s_kw, g // 2 + 1)
                            if g >= 2:
                                pe.wait_ge(s_kT, g - 1)
                            for c in range(4):
                                pair = z[:, g // 2, 8 * (g % 2) + 2 * c:8 * (g % 2) + 2 * c + 2].rearrange("p b j -> p (b j)")
                                last = nc.tensor.transpose(ps[:, g % 2, P * c:P * c + P], pair, ident)
                            last.then_inc(s_tr, 1)
                        if g:
                            pe.wait_ge(s_kT, g)
                            if g >= 3:
                                pe.wait_ge(s_pw, g - 2)
                            for c in range(4):
                                last = nc.tensor.matmul(ps[:, 2 + (g - 1) % 2, P * c:P * c + P], kT[:, g - 1, P * c:P * c + P], dft, start=True, stop=True)
                            last.then_inc(s_ft, 1)

        class ColumnParts:

            def __init__(self, tag, xa, xb, copy_on_dve):
                self.xa, self.xb, self.copy_on_dve = xa, xb, copy_on_dve
                self.s_tr, self.s_hi, self.s_h2, self.s_r, self.s_md, self.s_lo = (
                    sem(f"{tag}_{n}") for n in ("turned", "x_hi", "x_hi_again", "x_rest", "x_mid", "x_lo"))

            def turn(self, pe, c):
                if c >= 2:
                    pe.wait_ge(self.s_r, c - 1)
                for k in range(TC):
                    last = nc.tensor.transpose(ps[:, c % 2, P * k:P * k + P], x2[:, TC * c + k].rearrange("p a d -> p (a d)"), ident)
                last.then_inc(self.s_tr, 1)

            def high(self, act, c):
                act.wait_ge(self.s_tr, c + 1)
                nc.scalar.activation(self.xa[:, c], ps[:, c % 2], ACT.Copy).then_inc(self.s_hi, 1)
                if not self.copy_on_dve:
                    nc.scalar.activation(self.xb[0:D, c], ps[0:D, c % 2], ACT.Copy).then_inc(self.s_h2, 1)

            def middle(self, act, c):
                act.wait_ge(self.s_r, c + 1)
                nc.scalar.activation(self.xa[D:P, c], column_rest[c % 2][D:P], ACT.Copy).then_inc(self.s_md, 1)

            def rest(self, dve, c):
                dve.wait_ge(self.s_hi, c + 1)
                if not self.copy_on_dve:
                    dve.wait_ge(self.s_h2, c + 1)
                if c >= 2:
                    dve.wait_ge(self.s_lo, c - 1)
                nc.vector.tensor_tensor(column_rest[c % 2][D:P], ps[D:P, c % 2], self.xa[D:P, c], ALU.subtract).then_inc(self.s_r, 1)
                if self.copy_on_dve:
                    nc.vector.tensor_copy(self.xb[0:D, c], self.xa[0:D, c]).then_inc(self.s_h2, 1)

            def low(self, pool, c):
                pool.wait_ge(self.s_md, c + 1)
                nc.gpsimd.tensor_tensor(self.xb[D:P, c], column_rest[c % 2][D:P], self.xa[D:P, c], ALU.subtract).then_inc(self.s_lo, 1)

        def attention_prep0():
            sq = mid[:, 0:2048].rearrange("p (t d) -> p t d", t=NT)
            xc = mid[:, 2048:4096].rearrange("p (t d) -> p t d", t=NT)
            s_xc, s_sq, s_var, s_sd, s_x2 = (sem(f"a0_{n}") for n in ("centred", "squared", "var", "sd", "normed"))
            s_w, s_b2 = sem("a0_weights_in"), sem("a0_output_biases_in")
            s_selb, s_sel = sem("a0_selectors_zeroed"), sem("a0_selectors")
            cols = ColumnParts("a0", *columns, copy_on_dve=True)
            half = NT // 2
            halves = [slice(0, half), slice(half, NT)]
            mean, var, sd = rowsc[:, 0], rowsc[:, 1], rowsc[:, 2]

            with nc.Block() as block:
                @block.vector
                def _(dve):
                    link = chain(dve, "a0_dve")
                    for s in halves:
                        link(nc.vector.tensor_reduce(mean[:, s], res[:, s], AX.X, ALU.add))
                        link(nc.vector.tensor_scalar(mean[:, s], mean[:, s], -1.0 / D, None, ALU.mult))
                        nc.vector.tensor_tensor(xc[:, s], res[:, s], bc(mean[:, s].unsqueeze(2), [P, half, D]), ALU.add).then_inc(s_xc, 1)
                    for n, s in enumerate(halves):
                        dve.wait_ge(s_sq, n + 1)
                        link(nc.vector.tensor_reduce(var[:, s], sq[:, s], AX.X, ALU.add))
                        nc.vector.tensor_scalar(var[:, s], var[:, s], 1.0 / D, EPS, ALU.mult, ALU.add).then_inc(s_var, 1)
                    for n, s in enumerate(halves):
                        dve.wait_ge(s_sd, n + 1)
                        dve.wait_ge(s_xc, 2)
                        link(nc.vector.reciprocal(sd[:, s], sd[:, s]))
                        for c in range(CH // 2 * n, CH // 2 * (n + 1), 2):
                            q = slice(TC * c, TC * c + 2 * TC)
                            shape = [P, 2 * TC, 2, D]
                            nc.vector.tensor_tensor(x2[:, q], bc(xc[:, q].unsqueeze(2), shape), bc(sd[:, q].unsqueeze(2).unsqueeze(3), shape), ALU.mult).then_inc(s_x2, 1)
                            for d in (c - 2, c - 1):
                                if d >= 0:
                                    cols.rest(dve, d)
                    for d in (CH - 2, CH - 1):
                        cols.rest(dve, d)

                @block.scalar
                def _(act):
                    for n, s in enumerate(halves):
                        act.wait_ge(s_xc, n + 1)
                        nc.scalar.activation(sq[:, s], xc[:, s], ACT.Square).then_inc(s_sq, 1)
                    for n, s in enumerate(halves):
                        act.wait_ge(s_var, n + 1)
                        nc.scalar.activation(sd[:, s], var[:, s], ACT.Sqrt).then_inc(s_sd, 1)
                    act.wait_ge(s_selb, 1)
                    nc.scalar.activation(selb[0:48].rearrange("p e f -> p (e f)"), cst[0:48, o_sel0:o_sel0 + 16 * P], ACT.Copy).then_inc(s_sel, 1)
                    for c in range(CH + 1):
                        if c < CH:
                            cols.high(act, c)
                        if c >= 1:
                            cols.middle(act, c - 1)

                @block.tensor
                def _(pe):
                    for c in range(CH):
                        pe.wait_ge(s_x2, c // 2 + 1)
                        cols.turn(pe, c)

                @block.gpsimd
                def _(pool):
                    link = chain(pool, "a0_pool")
                    link(nc.gpsimd.memset(b2p[0][:], 0.0))
                    link(nc.gpsimd.memset(b2p[1][:], 0.0))
                    nc.gpsimd.memset(selb[:], 0.0).then_inc(s_selb, 1)
                    pool.wait_ge(s_selb, 1)
                    for L, E3 in ((0, 48), (1, 24)):
                        pool.wait_ge(s_b2, 32)
                        raw_b, rest_b = (mid[0:E3, 4096 + 128 * L + D * n:4096 + 128 * L + D * n + D] for n in range(2))
                        hi, md, lo = (b2p[L][0:E3, n] for n in range(3))
                        link(nc.gpsimd.tensor_copy(hi, raw_b))
                        link(nc.gpsimd.tensor_tensor(rest_b, raw_b, hi, ALU.subtract))
                        link(nc.gpsimd.tensor_copy(md, rest_b))
                        link(nc.gpsimd.tensor_tensor(lo, rest_b, md, ALU.subtract))
                    for c in range(CH):
                        cols.low(pool, c)

                @block.sync
                def _(sp):
                    for L, (E3, src) in enumerate(((48, b2_0), (24, b2_1))):
                        sp.dma_start(mid[0:E3, 4096 + 128 * L:4096 + 128 * L + D], src).then_inc(s_b2, 16)
                    sp.wait_ge(s_b2, 32)
                    n = 0
                    for dst, src in ((w2s[0][:], w2_0), (w2s[1][:], w2_1), (bprojb[:], bproj), (gb[:], gamma_beta)):
                        sp.dma_start(dst, src).then_inc(s_w, 16)
                        n += 16
                    sp.wait_ge(s_w, n)

        class TileNorm:

            def __init__(self, tag, link, work, n):
                self.link, self.n = link, n
                self.xc = work[:, 0:n * D].rearrange("p (t d) -> p t d", t=n)
                self.sq = work[:, n * D:2 * n * D].rearrange("p (t d) -> p t d", t=n)
                st = work[:, 2 * n * D:2 * n * D + 4 * n].rearrange("p (s t) -> p s t", s=4)
                self.sum, self.var, self.rs, self.nh = (st[:, s] for s in range(4))
                self.s_var, self.s_rs, self.s_nh = sem(tag + "_norm_var"), sem(tag + "_norm_rsd"), sem(tag + "_minus_half")

            def start(self):
                nc.vector.memset(self.nh, -0.5).then_inc(self.s_nh, 1)

            def mean(self, tiles):
                self.link(nc.vector.tensor_reduce(self.sum, tiles, AX.X, ALU.add))
                self.link(nc.vector.tensor_scalar(self.sum, self.sum, -1.0 / D, None, ALU.mult))

            def centre(self, tiles):
                self.link(nc.vector.tensor_tensor(self.xc, tiles, bc(self.sum.unsqueeze(2), [P, self.n, D]), ALU.add))

            def square(self):
                self.link(nc.vector.tensor_tensor(self.sq, self.xc, self.xc, ALU.mult))

            def variance(self):
                self.link(nc.vector.tensor_reduce(self.var, self.sq, AX.X, ALU.add))
                nc.vector.tensor_scalar(self.var, self.var, 1.0 / D, EPS, ALU.mult, ALU.add).then_inc(self.s_var, 1)

            def root(self, pool, i):
                pool.wait_ge(self.s_var, i + 1)
                nc.gpsimd.tensor_tensor(self.rs, self.var, self.nh, ALU.pow).then_inc(self.s_rs, 1)

            def scale_twice(self, dve, i, out_):
                dve.wait_ge(self.s_rs, i + 1)
                shape = [P, self.n, 2, D]
                self.link(nc.vector.tensor_tensor(out_, bc(self.xc.unsqueeze(2), shape), bc(self.rs.unsqueeze(2).unsqueeze(3), shape), ALU.mult))

        gamma_beta = bass.AP(tensor=gamma.tensor, offset=0, ap=[[0, P], [D, 2], [1, D]])
        pos_in = bass.AP(tensor=wpos.tensor, offset=0, ap=[[0, P], [H, 5], [1, H]])
        bproj = bass.AP(tensor=bproj.tensor, offset=0, ap=[[0, P], [1, D]])
        gate_bias = bass.AP(tensor=gate_b0.tensor, offset=0, ap=[[0, P], [1, 16]])

        def attention0():
            scale = D ** -0.5
            pos = [0]
            def take(n):
                a = big[:, pos[0]:pos[0] + n]
                pos[0] += n
                assert pos[0] <= 11264
                return a
            q32 = [take(512).rearrange("p (g q) -> p g q", g=2) for _ in range(2)]
            k32 = [take(512).rearrange("p (g q) -> p g q", g=2) for _ in range(2)]
            e_sb = [take(1024).rearrange("p (j t k) -> p j t k", j=2, t=2) for _ in range(2)]
            a_sb = [take(1024).rearrange("p (j c q) -> p j c q", j=2, c=2) for _ in range(2)]
            val = [take(2 * H * D).rearrange("p (c v) -> p c v", c=2) for _ in range(2)]
            xs = [take(256).bitcast(BF16).rearrange("p (k q) -> p k q", k=2) for _ in range(2)]
            o_sb = [take(256)[0:D] for _ in range(2)]
            new = take(2 * D).rearrange("p (t d) -> p t d", t=2)
            norm_work = take(512)
            work = take(64)
            quad = lambda n: work[:, 4 * n:4 * n + 4].rearrange("p (j t) -> p j t", j=2)
            mx, minus, total, inverse = quad(0), [quad(1), quad(2)], [quad(3), quad(4)], [quad(5), quad(6)]
            raw = mid[:, 0:WALL]
            rest = mid[:, WALL:2 * WALL]

            S = [ps[:, 2 * n:2 * n + 2].rearrange("p j (t k) -> p j t k", t=2) for n in range(2)]
            AT = ps[:, 4:6].rearrange("p j (c q) -> p j c q", c=2)
            O = ps[0:D, 6].rearrange("p (b q) -> p b q", b=2)
            M = ps[:, 7]
            OT = ps[:, 7, 0:2 * D].rearrange("p (t d) -> p t d", t=2)

            s_xs, s_pr, s_out = (sem("L0_" + n) for n in ("xs_ready", "projected", "projection_in_sbuf"))
            s_S, s_mx, s_E, s_inv, s_A, s_AT, s_at = (sem("L0_" + n) for n in (
                "scores", "minus_max", "exps", "inverse_sums", "probabilities", "probabilities_turned", "turned_in_sbuf"))
            s_PV, s_O, s_OT, s_add = (sem("L0_" + n) for n in ("outputs", "outputs_in_sbuf", "outputs_turned", "added"))
            s_pad, s_pmax, s_pexp = sem("L0_padded"), sem("L0_pos_max"), sem("L0_pos_exp")
            s_raw, s_whi, s_wrest, s_wmd = (sem("L0_" + n) for n in ("expert_w_in", "expert_w_hi", "expert_w_rest", "expert_w_mid"))
            link = chain(nc.vector, "L0_dve")
            norm = TileNorm("L0", link, norm_work, 2)
            part = lambda k: slice(512 * k, 512 * k + 512)
            PARTS = WALL // 512

            def rows(p, j):
                r = 32 * (2 * (p % 2) + j)
                return slice(r, r + 32)

            def at(k):
                return (k // PAIRS) % 2, k % PAIRS

            with nc.Block() as block:
                @block.tensor
                def _(pe):
                    def project(n, b, par):
                        if n == 0:
                            pe.wait_ge(s_xs, b + 1)
                        if not isinstance(b, int) or b >= 1 or n >= 1:
                            pe.wait_ge(s_out, 4 * b + n)
                        if n == 2 and (not isinstance(b, int) or b >= 2):
                            pe.wait_ge(s_add, b - 1)
                        kinds = ((0, True, False), (0, False, False), (1, False, True))
                        if n < 2:
                            for g in range(2):
                                w = (Q0, K0)[n] + P * g
                                for i, (kind, start, stop) in enumerate(kinds):
                                    last = nc.tensor.matmul(M[:, 256 * g:256 * g + 256], w64[:, i, w:w + P], xs[par][:, kind], start=start, stop=stop)
                        else:
                            c = n - 2
                            for i, (kind, start, stop) in enumerate(kinds):
                                last = nc.tensor.matmul(M, xs[par][:, kind, P * c:P * c + P], w64[:, i, V0:V0 + H * D], start=start, stop=stop)
                        last.then_inc(s_pr, 1)

                    def scores(k):
                        par, p = at(k)
                        for tq in range(2):
                            for j in range(2):
                                r = rows(p, j)
                                last = nc.tensor.matmul(S[k % 2][:, j, tq], q32[par][r, p // 2, P * tq:P * tq + P], k32[par][r, p // 2], start=True, stop=True)
                        last.then_inc(s_S, 1)

                    def turn(k, done, par, projections):
                        for j in range(2):
                            for c in range(2):
                                for tq in range(2):
                                    if done is not None and (j, c, tq) == (1, 1, 1):
                                        pe.wait_ge(s_O, done)
                                        pe.wait_ge(s_out, projections)
                                    last = nc.tensor.transpose(AT[:, j, c, P * tq:P * tq + P], e_sb[k % 2][:, j, tq, P * c:P * c + P], ident)
                        last.then_inc(s_AT, 1)
                        if done is not None:
                            outputs_turn(par)

                    def outputs_turn(par):
                        for tq in range(2):
                            last = nc.tensor.transpose(OT[:, tq], o_sb[par][:, P * tq:P * tq + P], ident[0:D, 0:D])
                        last.then_inc(s_OT, 1)

                    def outputs(k):
                        par, p = at(k)
                        for j in range(2):
                            h = 2 * p + j
                            for c in range(2):
                                n = P - c
                                last = nc.tensor.matmul(O[:, par], val[par][0:n, c, D * h:D * h + D], a_sb[k % 2][0:n, j, c],
                                                        start=(h == 0 and c == 0), stop=(h == H - 1 and c == 1))
                        last.then_inc(s_PV, 1)

                    def slot(j, k, do=("unit", "turn", "pv")):
                        U = 2 * PAIRS * j + k
                        known = isinstance(j, int)
                        par, p = at(k)
                        b = 2 * j + par
                        if "unit" in do:
                            if not known or U >= 1:
                                pe.wait_ge(s_E, U)
                            if p == 3:
                                pe.wait_ge(s_out, 4 * (b + 1) + 2)
                            scores(k + 1)
                        if "turn" in do and (not known or U >= 1):
                            pe.wait_ge(s_A, U)
                            if not known or U >= 2:
                                pe.wait_ge(s_at, U - 1)
                            turning = p == 2 and (not known or b >= 1)
                            turn(k - 1, b if turning else None, (par + 1) % 2, 4 * (b + 1) + 2)
                        if "pv" in do and (not known or U >= 2):
                            pe.wait_ge(s_at, U - 1)
                            if p == 2:
                                pe.wait_ge(s_out, 4 * (b + 1))
                                if not known or b >= 1:
                                    pe.wait_ge(s_O, b)
                            outputs(k - 2)
                        if "unit" in do:
                            project(p, b + 1, (par + 1) % 2)

                    for n in range(4):
                        project(n, 0, 0)
                    scores(0)
                    for k in range(2 * PAIRS):
                        slot(0, k)
                    with pe.Fori(1, B // 2) as j:
                        for k in range(2 * PAIRS):
                            slot(j, k)
                    slot(B // 2, 0, ("turn", "pv"))
                    slot(B // 2, 1, ("pv",))
                    pe.wait_ge(s_O, B)
                    pe.wait_ge(s_out, 4 * (B + 1))
                    outputs_turn((B - 1) % 2)

                @block.scalar
                def _(act):
                    def project_out(n, b, par):
                        act.wait_ge(s_pr, 4 * b + n + 1)
                        if n == 0 and (not isinstance(b, int) or b >= 2):
                            act.wait_ge(s_S, PAIRS * (b - 1))
                        if n == 2 and (not isinstance(b, int) or b >= 2):
                            act.wait_ge(s_PV, PAIRS * (b - 1))
                        dst = (q32, k32)[n][par].rearrange("p g q -> p (g q)") if n < 2 else val[par][:, n - 2]
                        nc.scalar.activation(dst, M, ACT.Copy).then_inc(s_out, 1)

                    def slot(j, k, do=("unit",)):
                        U = 2 * PAIRS * j + k
                        known = isinstance(j, int)
                        par, p = at(k)
                        b = 2 * j + par
                        if p == 2 and (not known or b >= 1):
                            act.wait_ge(s_PV, PAIRS * b)
                            if not known or b >= 3:
                                act.wait_ge(s_OT, b - 2)
                            nc.scalar.activation(o_sb[(par + 1) % 2], O[:, (par + 1) % 2], ACT.Copy).then_inc(s_O, 1)
                        if p == 2 and "unit" in do:
                            project_out(1, b + 1, (par + 1) % 2)
                        if "unit" in do:
                            act.wait_ge(s_mx, U + 1)
                            if not known or U >= 2:
                                act.wait_ge(s_AT, U - 1)
                            for jj in range(2):
                                for tq in range(2):
                                    last = nc.scalar.activation(e_sb[k % 2][:, jj, tq, 0:NW], S[k % 2][:, jj, tq, 0:NW], ACT.Exp, scale=scale,
                                                                bias=minus[k % 2][:, jj, tq:tq + 1], accum_out=total[k % 2][:, jj, tq:tq + 1])
                            last.then_inc(s_E, 1)
                        if p in (1, 3) and "unit" in do:
                            project_out(p - 1, b + 1, (par + 1) % 2)
                        if p == 0 and (not known or b >= 1):
                            project_out(3, b, par)
                        if known and j == 0:
                            act.wait_ge(s_pmax, k + 1)
                            for tq in range(2):
                                nc.scalar.activation(pexp[:, tq, k], pexp[:, tq, k], ACT.Exp, bias=pmax[:, tq, k:k + 1],
                                                     accum_out=psum[:, tq, k:k + 1]).then_inc(s_pexp, 1)
                            if k < PARTS:
                                act.wait_ge(s_raw, 16)
                                nc.scalar.activation(wall[:, 0, part(k)], raw[:, part(k)], ACT.Copy).then_inc(s_whi, 1)
                            if 0 <= k - 2 < PARTS:
                                act.wait_ge(s_wrest, k - 1)
                                nc.scalar.activation(wall[:, 1, part(k - 2)], rest[:, part(k - 2)], ACT.Copy).then_inc(s_wmd, 1)

                    act.wait_ge(s_pad, 2)
                    for n in range(4):
                        project_out(n, 0, 0)
                    for j in range(2):
                        for k in range(2 * PAIRS):
                            slot(j, k)
                    with act.Fori(2, B // 2) as j:
                        for k in range(2 * PAIRS):
                            slot(j, k)
                    for k in range(3):
                        slot(B // 2, k, ())

                @block.vector
                def _(dve):
                    link.eng = dve

                    def maxima(U, k):
                        dve.wait_ge(s_S, U + 1)
                        link(nc.vector.tensor_reduce(mx, S[k % 2][:, :, :, 0:NW], AX.X, ALU.max))
                        nc.vector.tensor_scalar(minus[k % 2], mx, -scale, None, ALU.mult).then_inc(s_mx, 1)

                    def slot(j, k, do=("unit",)):
                        U = 2 * PAIRS * j + k
                        known = isinstance(j, int)
                        par, p = at(k)
                        b = 2 * j + par
                        if "unit" in do:
                            dve.wait_ge(s_E, U + 1)
                            if not known or U >= 2:
                                dve.wait_ge(s_A, U - 1)
                            nc.vector.reciprocal(inverse[k % 2], total[k % 2]).then_inc(s_inv, 1)
                        if p == 2 and (not known or 1 <= b <= B):
                            dve.wait_ge(s_OT, b)
                            rs = res[:, span(2 * (b - 1), 2)]
                            link(nc.vector.tensor_tensor(new, rs, OT, ALU.add))
                            nc.vector.tensor_tensor(rs, rs, OT, ALU.add).then_inc(s_add, 1)
                        if "unit" in do:
                            maxima(U + 1, k + 1)
                        if ("unit" in do or k == 0) and (not known or U >= 1):
                            dve.wait_ge(s_AT, U)
                            if not known or U >= 3:
                                dve.wait_ge(s_PV, U - 2)
                            nc.vector.tensor_copy(a_sb[(k - 1) % 2], AT).then_inc(s_at, 1)
                        if p == 3 and (not known or b >= 1):
                            norm.mean(new)
                            norm.centre(new)
                            norm.square()
                            norm.variance()
                        if p == 0 and (not known or b >= 2):
                            norm.scale_twice(dve, b - 2, x2[:, span(2 * (b - 2), 2)])
                        if known and j == 0:
                            if k < 2 * PAIRS - 1:
                                pos_max(k + 1)
                            if 0 <= k - 1 < PARTS:
                                dve.wait_ge(s_whi, k)
                                nc.vector.tensor_tensor(rest[:, part(k - 1)], raw[:, part(k - 1)], wall[:, 0, part(k - 1)], ALU.subtract).then_inc(s_wrest, 1)
                            if 0 <= k - 3 < PARTS:
                                dve.wait_ge(s_wmd, k - 2)
                                s = part(k - 3)
                                link(nc.vector.tensor_tensor(wall[0:D, 2, s], rest[0:D, s], wall[0:D, 1, s], ALU.subtract))
                                link(nc.vector.tensor_copy(wall[D:P, 2, s], wall[D:P, 0, s]))

                    def pos_max(h):
                        link(nc.vector.tensor_reduce(pmax[:, :, h], pexp[:, :, h, 0:NW], AX.X, ALU.max))
                        nc.vector.tensor_scalar(pmax[:, :, h], pmax[:, :, h], -1.0, None, ALU.mult).then_inc(s_pmax, 1)

                    for n in range(2):
                        nc.vector.memset(e_sb[n][:, :, :, NW:NW + 1], 0.0).then_inc(s_pad, 1)
                    norm.start()
                    pos_max(0)
                    maxima(0, 0)
                    for k in range(2 * PAIRS):
                        slot(0, k)
                    per = 2 * (4 + 1 + 5 + 1)
                    link.loop(lambda j: [slot(j, k) for k in range(2 * PAIRS)], 1, B // 2, per)
                    for k in range(5):
                        slot(B // 2, k, ())

                @block.gpsimd
                def _(pool):
                    def fetch(b, par):
                        if not isinstance(b, int) or b >= 2:
                            pool.wait_ge(s_pr, 4 * (b - 1))
                        nc.gpsimd.tensor_copy(xs[par], xab[:, :, b]).then_inc(s_xs, 1)

                    def slot(j, k):
                        U = 2 * PAIRS * j + k
                        par, p = at(k)
                        b = 2 * j + par
                        pool.wait_ge(s_inv, U + 1)
                        nc.gpsimd.tensor_tensor(e_sb[k % 2], e_sb[k % 2], bc(inverse[k % 2].unsqueeze(3), [P, 2, 2, 256]), ALU.mult).then_inc(s_A, 1)
                        if p == 0 and (not isinstance(j, int) or b + 2 <= B):
                            fetch(b + 2, par)
                        if p == 3 and (not isinstance(j, int) or b >= 1):
                            norm.root(pool, b - 1)

                    for b in range(2):
                        fetch(b, b)
                    pool.wait_ge(norm.s_nh, 1)
                    pool.wait_ge(s_pad, 2)
                    for k in range(2 * PAIRS):
                        slot(0, k)
                    with pool.Fori(1, B // 2 - 1) as j:
                        for k in range(2 * PAIRS):
                            slot(j, k)
                    for k in range(2 * PAIRS):
                        slot(B // 2 - 1, k)
                    norm.root(pool, B - 1)

                @block.sync
                def _(sp):
                    sp.dma_start(raw, w1_01).then_inc(s_raw, 16)
                    sp.wait_ge(s_raw, 16)

        v1flat = [mid[:, 0:1280].rearrange("p (c v) -> p c v", c=2), mid[:, 1280:2560].rearrange("p (c v) -> p c v", c=2)]
        v1pad = v1flat
        v1own = [v.rearrange("p c (h s) -> p c h s", h=H) for v in v1flat]
        posv = mid[:, 2560:2560 + 2048].rearrange("p (t b d) -> p t b d", t=2, b=B)
        gsum = mid[:, 4608:4624].rearrange("p (t h) -> p t h", t=2)
        omg = mid[:, 4624:4632]

        xa = big[:, 0:2048].bitcast(BF16).rearrange("p (c q) -> p c q", c=CH)
        xb = big[:, 2048:4096].bitcast(BF16).rearrange("p (c q) -> p c q", c=CH)
        ct = big[:, 4096:6144].bitcast(BF16).rearrange("p (c q) -> p c q", c=CH)
        mo = big[:, 6144:16384]

        def experts_prep1():
            E = 8
            E3 = 3 * E
            t = "m1_"
            lg = mo[:, 1024:1024 + NT * E].rearrange("p (t e) -> p t e", t=NT)
            v8 = mo[:, 1536:1792].rearrange("p (t e) -> p t e", t=NT)
            i8 = mo[:, 1792:2048].bitcast(U32).rearrange("p (t e) -> p t e", t=NT)
            idx = mo[:, 2048:2112].rearrange("p (t e) -> p t e", t=NT)
            wts = mo[:, 2112:2112 + 4 * NT].rearrange("p (e t) -> p e t", e=4)
            comb = mo[:, 2304:2304 + NT * E].rearrange("p (t e) -> p t e", t=NT)
            pick = mo[:, 2816:2816 + NT * E].rearrange("p (t e) -> p t e", t=NT)
            c3 = mo[:, 3328:3328 + NT * 3 * E // 2].bitcast(BF16).rearrange("p (t s e) -> p t s e", t=NT, s=3)
            s_lg, s_lc = sem(t + "logits"), sem(t + "logits_out")
            s_dv, s_ex, s_c3, s_ctp, s_ct, s_zero = (sem(t + n) for n in ("gap", "gap_exp", "parts", "weights_turned", "weights_ready", "weights_zeroed"))
            cols = ColumnParts(t + "x", xa, xb, copy_on_dve=False)
            half = NT // 2

            with nc.Block() as block:
                @block.tensor
                def _(pe):
                    for c in range(CH + 3):
                        if c < CH:
                            cols.turn(pe, c)
                        if c >= 3:
                            d = c - 3
                            pe.wait_ge(cols.s_lo, d + 1)
                            if d >= 2:
                                pe.wait_ge(s_lc, d - 1)
                            for k in range(TC):
                                for n, src in enumerate((xa, xa, xb)):
                                    last = nc.tensor.matmul(ps[:, 2 + d % 2, E * k:E * k + E], src[:, d, P * k:P * k + P], w64[:, n, ROUTER], start=(n == 0), stop=(n == 2))
                            last.then_inc(s_lg, 1)
                    for c in range(CH):
                        pe.wait_ge(s_c3, 2 * c // CH + 1)
                        if c >= 2:
                            pe.wait_ge(s_ct, c - 1)
                        bank = ps[0:E3, 6 + c % 2, 0:256].bitcast(BF16)
                        for k in range(TC):
                            last = nc.tensor.transpose(bank[:, P * k:P * k + P], c3[:, TC * c + k].rearrange("p s e -> p (s e)"), ident_b[:])
                        last.then_inc(s_ctp, 1)

                @block.scalar
                def _(act):
                    def gap(n):
                        act.wait_ge(s_dv, n + 1)
                        s = slice(half * n, half * n + half)
                        nc.scalar.activation(wts[:, 0, s], wts[:, 0, s], ACT.Exp).then_inc(s_ex, 1)

                    def weights(c):
                        act.wait_ge(s_ctp, c + 1)
                        act.wait_ge(s_zero, 1)
                        nc.scalar.activation(ct[0:E3, c], ps[0:E3, 6 + c % 2, 0:256].bitcast(BF16), ACT.Copy).then_inc(s_ct, 1)

                    for c in range(CH + 1):
                        if c < CH:
                            cols.high(act, c)
                        if c >= 1:
                            cols.middle(act, c - 1)
                    for n in range(2):
                        gap(n)
                    for c in range(CH):
                        weights(c)

                @block.vector
                def _(dve):
                    link = chain(dve, t + "dve")

                    def best(c):
                        dve.wait_ge(s_lg, c + 1)
                        tl = slice(TC * c, TC * c + TC)
                        lp = ps[:, 2 + c % 2, 0:TC * E].rearrange("p (t e) -> p t e", t=TC)
                        nc.vector.tensor_copy(lg[:, tl], lp).then_inc(s_lc, 1)
                        dve.wait_ge(s_lc, c + 1)
                        for n in range(TC * c, TC * c + TC):
                            last = nc.vector.max(v8[:, n], lg[:, n])
                        link(last)
                        for n in range(TC * c, TC * c + TC):
                            last = nc.vector.max_index(i8[:, n], v8[:, n], lg[:, n])
                        link(last)

                    def difference(n):
                        s = slice(half * n, half * n + half)
                        nc.vector.tensor_tensor(wts[:, 0, s], v8[:, s, 1], v8[:, s, 0], ALU.subtract).then_inc(s_dv, 1)
                        link(nc.vector.tensor_copy(idx[:, s], i8[:, s, 0:2]))

                    def combine(n):
                        s = slice(half * n, half * n + half)
                        shape = [P, half, E]
                        where = lambda dst, i: nc.vector.tensor_tensor(dst[:, s], bc(iota[:, 0:E].unsqueeze(1), shape), bc(idx[:, s, i].unsqueeze(2), shape), ALU.is_equal)
                        link(where(comb, 0))
                        link(where(pick, 1))
                        dve.wait_ge(s_ex, n + 1)
                        link(nc.vector.tensor_scalar(wts[:, 1, s], wts[:, 0, s], 1.0, None, ALU.add))
                        link(nc.vector.reciprocal(wts[:, 2, s], wts[:, 1, s]))
                        link(nc.vector.tensor_tensor(wts[:, 3, s], wts[:, 0, s], wts[:, 2, s], ALU.mult))
                        for i, dst in ((0, comb), (1, pick)):
                            link(nc.vector.tensor_tensor(dst[:, s], dst[:, s], bc(wts[:, 2 + i, s].unsqueeze(2), shape), ALU.mult))
                        link(nc.vector.tensor_tensor(comb[:, s], comb[:, s], pick[:, s], ALU.add))
                        link(nc.vector.tensor_copy(c3[:, s, 0], comb[:, s]))
                        link(nc.vector.tensor_tensor(pick[:, s], comb[:, s], c3[:, s, 0], ALU.subtract))
                        link(nc.vector.tensor_copy(c3[:, s, 1], pick[:, s]))
                        nc.vector.tensor_tensor(c3[:, s, 2], pick[:, s], c3[:, s, 1], ALU.subtract).then_inc(s_c3, 1)

                    for c in range(CH + 3):
                        if c < CH:
                            cols.rest(dve, c)
                        if c >= 3:
                            best(c - 3)
                        if c == 3 + CH // 2 - 1:
                            difference(0)
                    difference(1)
                    combine(0)
                    combine(1)

                @block.gpsimd
                def _(pool):
                    link = chain(pool, t + "pool")
                    nc.gpsimd.memset(ct, 0.0).then_inc(s_zero, 1)
                    pool.wait_ge(s_zero, 1)
                    for c in range(CH):
                        cols.low(pool, c)
                    pool.wait_ge(cols.s_lo, CH)
                    link(nc.gpsimd.memset(selb[:], 0.0))
                    link(nc.gpsimd.tensor_copy(selb[0:E3, 0:4].rearrange("p e f -> p (e f)"), cst[0:E3, o_sel1:o_sel1 + 4 * P]))

        def experts1():
            NS = 4
            t = "e1_"
            DEEP = 4
            hid = [mo[:, 512 * n:512 * n + 512] for n in range(DEEP)]
            wgt = [mo[:, 2048 + 512 * n:2560 + 512 * n] for n in range(DEEP)]
            y_sb = mo[0:D, 4096:4608]
            yy = mo[:, 4608:4864].rearrange("p (t d) -> p t d", t=TC)
            s_h, s_hid, s_cb, s_wgt, s_w2 = (sem(t + n) for n in ("hidden", "activated", "weights_spread", "weighted", "second_done"))
            s_ysb, s_yt, s_fin, s_out = (sem(t + n) for n in ("sum_in_sbuf", "sum_turned", "added", "stored"))
            H1, CB, Y, YT = (lambda e: ps[:, e % 2]), (lambda e: ps[:, 2 + e % 2]), ps[0:D, 4], ps[:, 5]
            LAG = 3
            read_at, turn_at, add_at = 2, 3, 3

            link = chain(nc.vector, t + "dve")

            with nc.Block() as block:
                @block.tensor
                def _(pe):
                    def second(c, e, s):
                        if e == 0:
                            if not isinstance(c, int) or c >= 1:
                                pe.wait_ge(s_ysb, c)
                        pe.wait_ge(s_wgt, s + 1)
                        last = nc.tensor.matmul(Y, w2s[1][:, e], wgt[e % DEEP], start=(e == 0), stop=(e == NS - 1))
                        if e == 0:
                            for n in range(3):
                                last = nc.tensor.matmul(Y, b2p[1][:, n], ct[:, c], start=False, stop=False)
                        last.then_inc(s_w2, 1)

                    def turn(c):
                        for k in range(TC):
                            last = nc.tensor.transpose(YT[:, D * k:D * k + D], y_sb[:, P * k:P * k + P], ident[0:D, 0:D])
                        last.then_inc(s_yt, 1)

                    def chunk(c):
                        known = isinstance(c, int)
                        for e in range(NS):
                            s = NS * c + e
                            if not known or s >= 2:
                                pe.wait_ge(s_hid, s - 1)
                            for n, src in enumerate((xa, xa, xb)):
                                last = nc.tensor.matmul(H1(e), wst[1][:, n, P * e:P * e + P], src[:, c], start=(n == 0), stop=(n == 2))
                            last.then_inc(s_h, 1)
                            if not known or s >= 2:
                                pe.wait_ge(s_wgt, s - 1)
                            nc.tensor.matmul(CB(e), selb[:, e], ct[:, c], start=True, stop=True).then_inc(s_cb, 1)
                            turning = e == turn_at and (not known or c >= 1)
                            if turning:
                                pe.wait_ge(s_ysb, c)
                                if not known or c >= 2:
                                    pe.wait_ge(s_fin, c - 1)
                            if not known or s >= LAG:
                                if e >= LAG:
                                    second(c, e - LAG, s - LAG)
                                else:
                                    second(c - 1, e - LAG + NS, s - LAG)
                            if turning:
                                turn(c - 1)

                    chunk(0)
                    chunk(1)
                    with pe.Fori(2, CH) as c:
                        chunk(c)
                    for e in range(NS - LAG, NS):
                        second(CH - 1, e, NS * (CH - 1) + e)
                    pe.wait_ge(s_ysb, CH)
                    pe.wait_ge(s_fin, CH - 1)
                    turn(CH - 1)

                @block.scalar
                def _(act):
                    def y_out(c):
                        act.wait_ge(s_w2, NS * (c + 1))
                        if not isinstance(c, int) or c >= 1:
                            act.wait_ge(s_yt, c)
                        nc.scalar.activation(y_sb, Y, ACT.Copy).then_inc(s_ysb, 1)

                    def chunk(c):
                        known = isinstance(c, int)
                        for e in range(NS):
                            s = NS * c + e
                            act.wait_ge(s_h, s + 1)
                            if not known or s >= DEEP:
                                act.wait_ge(s_wgt, s + 1 - DEEP)
                            nc.scalar.activation(hid[e % DEEP], H1(e), ACT.Gelu, bias=b1s[1][:, e:e + 1]).then_inc(s_hid, 1)
                            if e == read_at and (not known or c >= 1):
                                y_out(c - 1)

                    chunk(0)
                    chunk(1)
                    with act.Fori(2, CH) as c:
                        chunk(c)
                    y_out(CH - 1)

                @block.vector
                def _(dve):
                    link.eng = dve

                    def finish(c):
                        y = YT[:, 0:TC * D].rearrange("p (t d) -> p t d", t=TC)
                        tl = span(TC * c, TC)
                        dve.wait_ge(s_yt, c + 1)
                        link(nc.vector.tensor_tensor(yy, y, x2[:, tl, 0], ALU.add))
                        nc.vector.tensor_tensor(res[:, tl], res[:, tl], yy, ALU.add).then_inc(s_fin, 1)

                    def chunk(c):
                        known = isinstance(c, int)
                        for e in range(NS):
                            s = NS * c + e
                            dve.wait_ge(s_hid, s + 1)
                            dve.wait_ge(s_cb, s + 1)
                            if not known or s >= DEEP:
                                dve.wait_ge(s_w2, s + 1 - DEEP)
                            nc.vector.tensor_tensor(wgt[e % DEEP], hid[e % DEEP], CB(e), ALU.mult).then_inc(s_wgt, 1)
                            if e == add_at and (not known or c >= 1):
                                finish(c - 1)

                    chunk(0)
                    link.loop(chunk, 1, CH, 1)
                    finish(CH - 1)

                @block.sync
                def _(sp):
                    def store(c):
                        sp.wait_ge(s_fin, c + 1)
                        for tq in range(2):
                            n = P - tq
                            src = res[0:n].rearrange("p (b t) d -> p b t d", t=2)
                            sp.dma_start(out[bass.ds(2 * c, 2), P * tq:P * tq + n].rearrange("b w d -> w b d"),
                                         src[:, bass.ds(2 * c, 2), tq]).then_inc(s_out, 16)

                    with sp.Fori(0, CH) as c:
                        store(c)
                    sp.wait_ge(s_out, 16 * 2 * CH)

        def attention1():
            scale = (D // H) ** -0.5
            pos = [0]
            def take(n, dt=F32):
                a = big[:, pos[0]:pos[0] + n]
                pos[0] += n
                assert pos[0] <= 8192
                return a if dt == F32 else a.bitcast(dt)
            parts = [take(384, BF16).rearrange("p (s q) -> p s q", s=3) for _ in range(2)]
            qs = [take(128, BF16) for _ in range(4)]
            ks = [take(128, BF16) for _ in range(4)]
            qm = [take(128, BF16) for _ in range(2)]
            mhl = [take(128, BF16).rearrange("p (t m) -> p t m", t=2) for _ in range(2)]
            e_sb = [take(1024).rearrange("p (j c q) -> p j c q", j=2, c=2) for _ in range(2)]
            xs = [take(256).bitcast(BF16).rearrange("p (k q) -> p k q", k=2) for _ in range(2)]
            o_sb = [take(256)[0:OW] for _ in range(2)]
            rest = take(256)
            work = take(512)
            mx = work[:, 0:4].rearrange("p (j t) -> p j t", j=2)
            rinv = work[:, 8:24].rearrange("p (t h) -> p t h", t=2)
            rgate = work[:, 24:40].rearrange("p (t h) -> p t h", t=2)
            asum = work[:, 40:56].rearrange("p (t h) -> p t h", t=2)
            hsum = work[:, 64:64 + 2 * D].rearrange("p (t d) -> p t d", t=2)
            blend = work[:, 192:192 + 2 * D].rearrange("p (t d) -> p t d", t=2)
            oT_sb = work[:, 320:320 + P]
            new = take(128).rearrange("p (t d) -> p t d", t=2)

            S = ps[:, 0:2].rearrange("p j (t k) -> p j t k", t=2)
            T = ps[:, 2:4].rearrange("p j (c q) -> p j c q", c=2)
            O = ps[:, 4].rearrange("p (b q) -> p b q", b=2)
            QS, KS = ps[:, 5, 0:256], ps[:, 5, 256:512]
            QK, BT = ps[:, 6, 0:256], ps[:, 6, 256:384]
            MT = ps[:, 7, 0:P].bitcast(BF16)
            OT = ps[:, 7, P:P + 2 * OW].rearrange("p (t d) -> p t d", t=2)
            Y = ps[:, 7, 288:288 + P].rearrange("p (t d) -> p t d", t=2)

            s_xs, s_qkp, s_parts, s_st, s_q, s_k = (sem("L1_" + n) for n in ("xs_ready", "qk_projected", "parts_ready", "stacked", "q_in_sbuf", "k_in_sbuf"))
            s_S, s_mhl, s_mtp, s_qm = (sem("L1_" + n) for n in ("scores", "max_parts", "max_turned", "q_with_max"))
            s_T, s_E, s_v, s_PV, s_O = (sem("L1_" + n) for n in ("turned_scores", "exps", "values_padded", "outputs", "outputs_in_sbuf"))
            s_OT, s_otr, s_bl, s_oTp, s_oT, s_y, s_fin = (sem("L1_" + n) for n in (
                "outputs_turned", "turned_outputs_read", "blended", "blend_turned", "blend_in_sbuf", "projected", "added"))
            s_zero = sem("L1_max_zeroed")
            link = chain(nc.vector, "L1_dve")
            norm = TileNorm("L1", link, take(512), 2)

            def at(k):
                return (k // PAIRS) % 2, k % PAIRS

            def head(j):
                return slice(64 * j, 64 * j + 64)

            with nc.Block() as block:
                @block.tensor
                def _(pe):
                    def project(b, par):
                        pe.wait_ge(s_xs, b + 1)
                        if not isinstance(b, int) or b >= 1:
                            pe.wait_ge(s_parts, b)
                        for n, kind in enumerate((0, 0, 1)):
                            last = nc.tensor.matmul(QK, w64[:, n, QK1], xs[par][:, kind], start=(n == 0), stop=(n == 2))
                        last.then_inc(s_qkp, 1)

                    def stack(par, p):
                        for n, out_ in enumerate((QS, KS)):
                            for part in range(3):
                                last = nc.tensor.matmul(out_, selqk[:, 2 * p + n, part], parts[par][:, part], start=(part == 0), stop=(part == 2))
                        last.then_inc(s_st, 1)

                    def scores(k):
                        for j in range(2):
                            for tq in range(2):
                                last = nc.tensor.matmul(S[:, j, tq], qs[k % 4][head(j), P * tq:P * tq + P], ks[k % 4][head(j)], start=True, stop=True)
                        last.then_inc(s_S, 1)

                    def turned_scores(k):
                        for j in range(2):
                            for c in range(2):
                                last = nc.tensor.matmul(T[:, j, c], ks[k % 4][head(j), P * c:P * c + P], qm[k % 2][head(j)], start=True, stop=True)
                        last.then_inc(s_T, 1)

                    def outputs(k):
                        par, p = at(k)
                        for j in range(2):
                            h = 2 * p + j
                            for c in range(2):
                                n = P - c
                                last = nc.tensor.matmul(O[0:OW, par], v1pad[par][0:n, c, OW * h:OW * h + OW], e_sb[k % 2][0:n, j, c],
                                                        start=(h == 0 and c == 0), stop=(h == H - 1 and c == 1))
                        last.then_inc(s_PV, 1)

                    def slot(j, k, do=("unit", "pv", "tail")):
                        U = 2 * PAIRS * j + k
                        known = isinstance(j, int)
                        par, p = at(k)
                        b = 2 * j + par
                        if "unit" in do:
                            pe.wait_ge(s_mhl, U + 1)
                            if not known or U >= 1:
                                pe.wait_ge(s_qm, U)
                            if p == 3 and (not known or b >= 1):
                                pe.wait_ge(s_otr, b)
                            if p == 1 and (not known or b >= 2):
                                pe.wait_ge(s_fin, b - 1)
                            for tq in range(2):
                                last = nc.tensor.transpose(MT[:, P * tq:P * tq + P], mhl[k % 2][:, tq], ident_b[:])
                            last.then_inc(s_mtp, 1)
                            pe.wait_ge(s_q, U + 2)
                            pe.wait_ge(s_k, U + 2)
                            scores(k + 1)
                            if p == 2:
                                pe.wait_ge(s_parts, b + 2)
                            stack(at(k + 2)[0], at(k + 2)[1])
                        if "tail" in do:
                            if "unit" in do and p in (0, 2) and (not known or b >= (1 if p else 2)):
                                pe.wait_ge(s_qm, U + 1)
                            if p == 2 and "unit" not in do:
                                pe.wait_ge(s_fin, b - 1)
                            if p == 2 and (not known or b >= 1):
                                pe.wait_ge(s_O, b)
                                for tq in range(2):
                                    last = nc.tensor.transpose(OT[:, tq], o_sb[(par + 1) % 2][:, P * tq:P * tq + P], ident[0:OW, 0:OW])
                                last.then_inc(s_OT, 1)
                            if p == 3 and (not known or b >= 1):
                                pe.wait_ge(s_bl, b)
                                if "unit" in do:
                                    pe.wait_ge(s_parts, b + 2)
                                nc.tensor.transpose(BT, blend.rearrange("p t d -> p (t d)"), ident).then_inc(s_oTp, 1)
                            if p == 0 and (not known or b >= 2):
                                pe.wait_ge(s_oT, b - 1)
                                nc.tensor.matmul(Y.rearrange("p t d -> p (t d)"), oT_sb, wps[:], start=True, stop=True).then_inc(s_y, 1)
                            if p == 0 and "unit" in do:
                                project(b + 1, (par + 1) % 2)
                        if "pv" in do and (not known or U >= 2):
                            pe.wait_ge(s_E, U - 1)
                            if p == 2:
                                pe.wait_ge(s_v, b + 1)
                                if not known or b >= 1:
                                    pe.wait_ge(s_O, b)
                            outputs(k - 2)
                        if "unit" in do:
                            pe.wait_ge(s_qm, U + 1)
                            if not known or U >= 1:
                                pe.wait_ge(s_E, U)
                            turned_scores(k)

                    project(0, 0)
                    pe.wait_ge(s_parts, 1)
                    stack(0, 0)
                    pe.wait_ge(s_q, 1)
                    pe.wait_ge(s_k, 1)
                    stack(0, 1)
                    scores(0)
                    for k in range(2 * PAIRS):
                        slot(0, k)
                    with pe.Fori(1, B // 2) as j:
                        for k in range(2 * PAIRS):
                            slot(j, k)
                    for k in range(5):
                        slot(B // 2, k, ("pv", "tail") if k < 2 else ("tail",))

                @block.scalar
                def _(act):
                    def stack_out(U, k):
                        act.wait_ge(s_st, U + 1)
                        if not isinstance(U, int) or U >= 4:
                            act.wait_ge(s_T, U - 3)
                        nc.scalar.activation(qs[k % 4], QS, ACT.Copy).then_inc(s_q, 1)
                        nc.scalar.activation(ks[k % 4], KS, ACT.Identity, bias=cst[:, o_neg:o_neg + 1]).then_inc(s_k, 1)

                    def slot(j, k, do=("unit", "o")):
                        U = 2 * PAIRS * j + k
                        known = isinstance(j, int)
                        par, p = at(k)
                        b = 2 * j + par
                        if "unit" in do:
                            stack_out(U + 2, k + 2)
                        if p == 1 and (not known or b >= 1):
                            act.wait_ge(s_PV, U - 1)
                            pl = (par + 1) % 2
                            if not known or b >= 3:
                                act.wait_ge(s_OT, b - 2)
                            nc.scalar.activation(o_sb[pl], O[0:OW, pl], ACT.Copy).then_inc(s_O, 1)
                        if p == 3 and (not known or b >= 1):
                            act.wait_ge(s_oTp, b)
                            if not known or b >= 2:
                                act.wait_ge(s_y, b - 1)
                            nc.scalar.activation(oT_sb, BT, ACT.Copy).then_inc(s_oT, 1)
                        if "unit" in do:
                            act.wait_ge(s_T, U + 1)
                            if not known or U >= 2:
                                act.wait_ge(s_PV, U - 1)
                            nc.scalar.activation(e_sb[k % 2], T, ACT.Exp, scale=scale).then_inc(s_E, 1)

                    stack_out(0, 0)
                    stack_out(1, 1)
                    for j in range(2):
                        for k in range(2 * PAIRS):
                            slot(j, k)
                    with act.Fori(2, B // 2) as j:
                        for k in range(2 * PAIRS):
                            slot(j, k)
                    for k in range(4):
                        slot(B // 2, k, ("o",))

                @block.vector
                def _(dve):
                    link.eng = dve

                    def split(b, par):
                        dve.wait_ge(s_qkp, b + 1)
                        if not isinstance(b, int) or b >= 2:
                            dve.wait_ge(s_st, PAIRS * (b - 1))
                        hi, md, lo = (parts[par][:, n] for n in range(3))
                        link(nc.vector.tensor_copy(hi, QK))
                        link(nc.vector.tensor_tensor(rest, QK, hi, ALU.subtract))
                        link(nc.vector.tensor_copy(md, rest))
                        nc.vector.tensor_tensor(lo, rest, md, ALU.subtract).then_inc(s_parts, 1)

                    def maxima(U, k):
                        dve.wait_ge(s_S, U + 1)
                        link(nc.vector.tensor_reduce(mx, S[:, :, :, 0:NW], AX.X, ALU.max))
                        if not isinstance(U, int) or U >= 2:
                            dve.wait_ge(s_mtp, U - 1)
                        m = mhl[k % 2].rearrange("p t (j c) -> p t j c", j=2)[:, :, :, ROWS:ROWS + 2]
                        mt = mx.rearrange("p j t -> p t j")
                        link(nc.vector.tensor_copy(m[:, :, :, 0], mt))
                        nc.vector.tensor_tensor(m[:, :, :, 1], mt, m[:, :, :, 0], ALU.subtract).then_inc(s_mhl, 1)

                    def slot(j, k, do=("unit",)):
                        U = 2 * PAIRS * j + k
                        known = isinstance(j, int)
                        par, p = at(k)
                        b = 2 * j + par
                        if "unit" in do:
                            dve.wait_ge(s_mtp, U + 1)
                            if not known or U >= 2:
                                dve.wait_ge(s_T, U - 1)
                            nc.vector.tensor_tensor(qm[k % 2], qs[k % 4], MT, ALU.add).then_inc(s_qm, 1)
                            maxima(U + 1, k + 1)
                        if p == 2 and (not known or 1 <= b <= B):
                            dve.wait_ge(s_OT, b)
                            l = OT[:, :, D:OW]
                            link(nc.vector.reciprocal(rinv, l))
                            link(nc.vector.tensor_tensor(rgate, rinv, bc(omg.unsqueeze(1), [P, 2, H]), ALU.mult))
                            link(nc.vector.tensor_tensor(asum, l, rgate, ALU.mult))
                            shape = [P, 2, H, D // H]
                            by_head = lambda a: a.rearrange("p t (h d) -> p t h d", h=H)
                            if not known or b >= 2:
                                dve.wait_ge(s_oTp, b - 1)
                            nc.vector.tensor_tensor(by_head(blend), by_head(OT[:, :, 0:D]), bc(rgate.unsqueeze(3), shape), ALU.mult).then_inc(s_otr, 1)
                            link(nc.vector.tensor_tensor(asum, asum, gsum, ALU.add))
                            link(nc.vector.reciprocal(asum, asum))
                            dve.wait_ge(s_otr, b)
                            link(nc.vector.tensor_tensor(blend, blend, posv[:, :, b - 1], ALU.add))
                            nc.vector.tensor_tensor(by_head(blend), by_head(blend), bc(asum.unsqueeze(3), shape), ALU.mult).then_inc(s_bl, 1)
                        if p == 0 and (not known or 2 <= b < B + 2):
                            dve.wait_ge(s_y, b - 1)
                            link(nc.vector.tensor_tensor(hsum, Y, bc(bprojb[:].unsqueeze(1), [P, 2, D]), ALU.add))
                            rs = res[:, span(2 * (b - 2), 2)]
                            link(nc.vector.tensor_tensor(new, rs, hsum, ALU.add))
                            nc.vector.tensor_tensor(rs, rs, hsum, ALU.add).then_inc(s_fin, 1)
                            dve.wait_ge(s_fin, b - 1)
                        if p == 0 and "unit" in do:
                            split(b + 1, (par + 1) % 2)
                        if p == 3 and (not known or 2 <= b < B + 2):
                            norm.mean(new)
                            norm.centre(new)
                            norm.square()
                            norm.variance()
                        if p == 1 and (not known or b >= 3):
                            norm.scale_twice(dve, b - 3, x2[:, span(2 * (b - 3), 2)])

                    for n in range(2):
                        nc.vector.memset(mhl[n], 0.0).then_inc(s_zero, 1)
                    dve.wait_ge(s_zero, 2)
                    norm.start()
                    split(0, 0)
                    maxima(0, 0)
                    for j in range(2):
                        for k in range(2 * PAIRS):
                            slot(j, k)
                    per = 2 * (4 * 2 + 6 + 2 + 3 + 5 + 1)
                    link.loop(lambda j: [slot(j, k) for k in range(2 * PAIRS)], 2, B // 2, per)
                    for k in range(10):
                        slot(B // 2 + k // 8, k % 8, ())

                @block.gpsimd
                def _(pool):
                    def fetch(b, par):
                        if not isinstance(b, int) or b >= 2:
                            pool.wait_ge(s_qkp, b - 1)
                        nc.gpsimd.tensor_copy(xs[par], xab[:, :, b]).then_inc(s_xs, 1)

                    def pad(b, par):
                        if not isinstance(b, int) or b >= 2:
                            pool.wait_ge(s_PV, PAIRS * (b - 1))
                        for c in range(2):
                            last = nc.gpsimd.tensor_copy(v1own[par][:, c, :, 0:D // H],
                                                         vall[:, c, :, b])
                        last.then_inc(s_v, 1)

                    def turn(b, par):
                        fetch(b + 2, par)
                        pad(b, par)
                        if not isinstance(b, int) or b >= 3:
                            norm.root(pool, b - 3)

                    for b in range(2):
                        fetch(b, b)
                        pad(b, b)
                    for b in range(2, 4):
                        fetch(b, b - 2)
                    pool.wait_ge(norm.s_nh, 1)
                    turn(2, 0)
                    turn(3, 1)
                    with pool.Fori(2, B // 2 - 1) as j:
                        turn(2 * j, 0)
                        turn(2 * j + 1, 1)
                    turn(B - 2, 0)
                    pad(B - 1, 1)
                    for b in range(B - 4, B):
                        norm.root(pool, b)

        def experts0():
            E, E3 = 16, 48
            DEEP = 4
            LAG = 3
            READ, TURN_SUM, FINISH = 2, 4, 5
            COLUMNS, MIDDLE, LOGITS, BEST, COMBINE, WEIGHTS = 2, 4, 7, 8, 9, 14
            pos = [0]
            def take(n, dt=F32):
                a = big[:, pos[0]:pos[0] + n]
                pos[0] += n
                assert pos[0] <= 11264
                return a if dt == F32 else a.bitcast(dt)
            xa, xb, ct = ([take(256, BF16) for _ in range(2)] for _ in range(3))
            hid, wgt = ([take(512) for _ in range(DEEP)] for _ in range(2))
            xf, rest, y_sb = take(512), take(512), take(512)[0:D]
            yy, yq, new = (take(TC * D).rearrange("p (t d) -> p t d", t=TC) for _ in range(3))
            st = take(16).rearrange("p (s t) -> p s t", s=4)
            nh, step = take(TC), take(2)
            lg, comb, pick = (take(TC * E).rearrange("p (t e) -> p t e", t=TC) for _ in range(3))
            v8 = take(8 * TC).rearrange("p (t e) -> p t e", t=TC)
            i8 = take(8 * TC).bitcast(U32).rearrange("p (t e) -> p t e", t=TC)
            idx = take(2 * TC).rearrange("p (t e) -> p t e", t=TC)
            wts = take(4 * TC).rearrange("p (e t) -> p e t", e=4)
            c3 = take(TC * E3 // 2, BF16).rearrange("p (t s e) -> p t s e", t=TC, s=3)
            norm_work = take(2 * TC * D + 4 * TC)
            raw_sel = mid[:, 0:H * 3 * P]

            s_h, s_hid, s_cb, s_wgt, s_w2, s_y = (sem("e0_" + n) for n in ("hidden", "activated", "weights_spread", "weighted", "second_done", "summed"))
            s_ysb, s_yt, s_fin, s_var, s_rs, s_nh = (sem("e0_" + n) for n in ("sum_in_sbuf", "sum_turned", "added", "var", "rsd", "half"))
            s_xf, s_tr, s_hi, s_h2, s_r, s_md, s_lo = (sem("e0_" + n) for n in ("x_fetched", "x_turned", "x_hi", "x_hi_again", "x_rest", "x_mid", "x_lo"))
            s_lg, s_lc, s_dv, s_ex, s_c3, s_ctp, s_ct = (sem("e0_" + n) for n in (
                "logits", "logits_biased", "gap", "gap_exp", "weight_parts", "weights_turned", "weights_ready"))
            s_zero, s_sel, s_selb = sem("e0_zeroed"), sem("e0_selectors_in"), sem("e0_selectors")
            H1, CB, Y, YT = (lambda e: ps[:, e % 2]), (lambda e: ps[:, 2 + e % 2]), ps[0:D, 4], ps[:, 5]
            X, R = ps[:, 6], ps[:, 7]
            link = chain(nc.vector, "e0_dve")
            norm = TileNorm("e0_next", link, norm_work, TC)

            with nc.Block() as block:
                @block.tensor
                def _(pe):
                    def columns_of(c):
                        pe.wait_ge(s_xf, c + 1)
                        if not isinstance(c, int) or c >= 1:
                            pe.wait_ge(s_r, c)
                        for k in range(TC):
                            last = nc.tensor.transpose(X[:, P * k:P * k + P], xf[:, P * k:P * k + P], ident)
                        last.then_inc(s_tr, 1)

                    def logits(c, q):
                        pe.wait_ge(s_lo, c + 1)
                        if not isinstance(c, int) or c >= 1:
                            pe.wait_ge(s_ct, c)
                        for k in range(TC):
                            for n, src in enumerate((xa, xa, xb)):
                                last = nc.tensor.matmul(R[:, E * k:E * k + E], src[q][:, P * k:P * k + P], w64[:, n, GATE], start=(n == 0), stop=(n == 2))
                        last.then_inc(s_lg, 1)

                    def weights(c):
                        bank = R[0:E3, 0:256].bitcast(BF16)
                        for k in range(TC):
                            last = nc.tensor.transpose(bank[:, P * k:P * k + P], c3[:, k].rearrange("p s e -> p (s e)"), ident_b[:])
                        last.then_inc(s_ctp, 1)

                    def second(c, q, e, s):
                        if e == 0 and (not isinstance(c, int) or c >= 1):
                            pe.wait_ge(s_ysb, c)
                        pe.wait_ge(s_wgt, s + 1)
                        last = nc.tensor.matmul(Y, w2s[0][:, e], wgt[e % DEEP], start=(e == 0), stop=(e == E - 1))
                        if e == 0:
                            for n in range(3):
                                last = nc.tensor.matmul(Y, b2p[0][:, n], ct[q], start=False, stop=False)
                        last.then_inc(s_w2, 1)

                    def sum_turn(c):
                        for k in range(TC):
                            last = nc.tensor.transpose(YT[:, D * k:D * k + D], y_sb[:, P * k:P * k + P], ident[0:D, 0:D])
                        last.then_inc(s_yt, 1)

                    def chunk(c, q):
                        known = isinstance(c, int)
                        for e in range(E):
                            s = E * c + e
                            if e == 0:
                                pe.wait_ge(s_ct, c + 1)
                            if not known or s >= 2:
                                pe.wait_ge(s_hid, s - 1)
                            for n, src in enumerate((xa, xa, xb)):
                                last = nc.tensor.matmul(H1(e), wst[0][:, n, P * e:P * e + P], src[q], start=(n == 0), stop=(n == 2))
                            last.then_inc(s_h, 1)
                            if not known or s >= 2:
                                pe.wait_ge(s_wgt, s - 1)
                            nc.tensor.matmul(CB(e), selb[:, e], ct[q], start=True, stop=True).then_inc(s_cb, 1)
                            turning = e == TURN_SUM and (not known or c >= 1)
                            if turning:
                                pe.wait_ge(s_ysb, c)
                                if not known or c >= 2:
                                    pe.wait_ge(s_fin, c - 1)
                            if e == WEIGHTS:
                                pe.wait_ge(s_c3, c + 2)
                            if e >= LAG:
                                second(c, q, e - LAG, s - LAG)
                            elif not known or s >= LAG:
                                second(c - 1, 1 - q, e - LAG + E, s - LAG)
                            if turning:
                                sum_turn(c - 1)
                            if e == COLUMNS:
                                columns_of(c + 1)
                            if e == LOGITS:
                                logits(c + 1, 1 - q)
                            if e == WEIGHTS:
                                weights(c + 1)

                    columns_of(0)
                    pe.wait_ge(s_h2, 1)
                    logits(0, 0)
                    pe.wait_ge(s_c3, 1)
                    weights(0)
                    chunk(0, 0)
                    chunk(1, 1)
                    with pe.Fori(1, CH // 2) as j:
                        chunk(2 * j, 0)
                        chunk(2 * j + 1, 1)
                    for e in range(E - LAG, E):
                        second(CH - 1, 1, e, E * (CH - 1) + e)
                    pe.wait_ge(s_ysb, CH)
                    pe.wait_ge(s_fin, CH - 1)
                    sum_turn(CH - 1)

                @block.scalar
                def _(act):
                    def high(c, q):
                        act.wait_ge(s_tr, c + 1)
                        if not isinstance(c, int) or c >= 2:
                            act.wait_ge(s_h, E * (c - 1))
                        nc.scalar.activation(xa[q], X, ACT.Copy).then_inc(s_hi, 1)
                        nc.scalar.activation(xb[q][0:D], X[0:D], ACT.Copy).then_inc(s_h2, 1)

                    def middle(c, q):
                        act.wait_ge(s_r, c + 1)
                        nc.scalar.activation(xa[q][D:P], rest[D:P], ACT.Copy).then_inc(s_md, 1)

                    def gap(c):
                        act.wait_ge(s_dv, c + 1)
                        nc.scalar.activation(wts[:, 0], wts[:, 0], ACT.Exp).then_inc(s_ex, 1)

                    def weights(c, q):
                        act.wait_ge(s_ctp, c + 1)
                        if not isinstance(c, int) or c >= 2:
                            act.wait_ge(s_cb, E * (c - 1))
                        nc.scalar.activation(ct[q][0:E3], R[0:E3, 0:256].bitcast(BF16), ACT.Copy).then_inc(s_ct, 1)

                    def y_out(c):
                        act.wait_ge(s_w2, E * (c + 1))
                        if not isinstance(c, int) or c >= 1:
                            act.wait_ge(s_yt, c)
                        nc.scalar.activation(y_sb, Y, ACT.Copy).then_inc(s_ysb, 1)

                    def chunk(c, q):
                        known = isinstance(c, int)
                        for e in range(E):
                            s = E * c + e
                            act.wait_ge(s_h, s + 1)
                            if not known or s >= DEEP:
                                act.wait_ge(s_wgt, s + 1 - DEEP)
                            nc.scalar.activation(hid[e % DEEP], H1(e), ACT.Relu, bias=b1s[0][:, e:e + 1]).then_inc(s_hid, 1)
                            if e == READ and (not known or c >= 1):
                                y_out(c - 1)
                            if e == COLUMNS + 1:
                                high(c + 1, 1 - q)
                            if e == MIDDLE:
                                middle(c + 1, 1 - q)
                            if e == COMBINE:
                                gap(c + 1)
                            if e == WEIGHTS + 1:
                                weights(c + 1, 1 - q)

                    high(0, 0)
                    middle(0, 0)
                    gap(0)
                    act.wait_ge(s_zero, 3)
                    weights(0, 0)
                    chunk(0, 0)
                    chunk(1, 1)
                    with act.Fori(1, CH // 2) as j:
                        chunk(2 * j, 0)
                        chunk(2 * j + 1, 1)
                    y_out(CH - 1)

                @block.vector
                def _(dve):
                    link.eng = dve

                    def rests(c, q):
                        dve.wait_ge(s_hi, c + 1)
                        dve.wait_ge(s_h2, c + 1)
                        if not isinstance(c, int) or c >= 1:
                            dve.wait_ge(s_lo, c)
                        nc.vector.tensor_tensor(rest[D:P], X[D:P], xa[q][D:P], ALU.subtract).then_inc(s_r, 1)

                    def best(c):
                        dve.wait_ge(s_lg, c + 1)
                        nc.vector.tensor_tensor(lg, R[:, 0:TC * E].rearrange("p (t e) -> p t e", t=TC), bc(gbs[:].unsqueeze(1), [P, TC, E]), ALU.add).then_inc(s_lc, 1)
                        dve.wait_ge(s_lc, c + 1)
                        nc.vector.memset(step[:, 0:1], 0.0)
                        for n in range(TC):
                            last = nc.vector.max(v8[:, n], lg[:, n])
                        link(last)
                        nc.vector.memset(step[:, 1:2], 0.0)
                        for n in range(TC):
                            last = nc.vector.max_index(i8[:, n], v8[:, n], lg[:, n])
                        link(last)
                        nc.vector.tensor_tensor(wts[:, 0], v8[:, :, 1], v8[:, :, 0], ALU.subtract).then_inc(s_dv, 1)
                        link(nc.vector.tensor_copy(idx, i8[:, :, 0:2]))

                    def combine(c):
                        shape = [P, TC, E]
                        where = lambda dst, i: nc.vector.tensor_tensor(dst, bc(iota.unsqueeze(1), shape), bc(idx[:, :, i].unsqueeze(2), shape), ALU.is_equal)
                        times = lambda dst, i: nc.vector.tensor_tensor(dst, dst, bc(wts[:, 2 + i].unsqueeze(2), shape), ALU.mult)

                        def places():
                            link(where(comb, 0))
                            link(where(pick, 1))

                        def shares():
                            dve.wait_ge(s_ex, c + 1)
                            link(nc.vector.tensor_scalar(wts[:, 1], wts[:, 0], 1.0, None, ALU.add))
                            link(nc.vector.reciprocal(wts[:, 2], wts[:, 1]))
                            link(nc.vector.tensor_tensor(wts[:, 3], wts[:, 0], wts[:, 2], ALU.mult))

                        def spread():
                            link(times(comb, 0))
                            link(times(pick, 1))
                            link(nc.vector.tensor_tensor(comb, comb, pick, ALU.add))

                        def split():
                            link(nc.vector.tensor_copy(c3[:, :, 0], comb))
                            link(nc.vector.tensor_tensor(pick, comb, c3[:, :, 0], ALU.subtract))
                            link(nc.vector.tensor_copy(c3[:, :, 1], pick))
                            nc.vector.tensor_tensor(c3[:, :, 2], pick, c3[:, :, 1], ALU.subtract).then_inc(s_c3, 1)

                        return [places, shares, spread, split]

                    def next_norm(c):
                        return [lambda: norm.mean(new), lambda: norm.centre(new), norm.square, norm.variance,
                                lambda: norm.scale_twice(dve, c, x2[:, span(TC * c, TC)])]

                    def finish(c):
                        tl = span(TC * c, TC)
                        shape = [P, TC, D]

                        def total():
                            dve.wait_ge(s_yt, c + 1)
                            link(nc.vector.tensor_tensor(yy, YT[:, 0:TC * D].rearrange("p (t d) -> p t d", t=TC), x2[:, tl, 0], ALU.add))

                        def mean():
                            link(nc.vector.tensor_reduce(st[:, 0], yy, AX.X, ALU.add))
                            link(nc.vector.tensor_scalar(st[:, 0], st[:, 0], -1.0 / D, None, ALU.mult))

                        def centre():
                            link(nc.vector.tensor_tensor(yy, yy, bc(st[:, 0].unsqueeze(2), shape), ALU.add))

                        def square():
                            link(nc.vector.tensor_tensor(yq, yy, yy, ALU.mult))

                        def variance():
                            link(nc.vector.tensor_reduce(st[:, 1], yq, AX.X, ALU.add))
                            nc.vector.tensor_scalar(st[:, 2], st[:, 1], 1.0 / D, EPS, ALU.mult, ALU.add).then_inc(s_var, 1)

                        def scale():
                            dve.wait_ge(s_rs, c + 1)
                            link(nc.vector.tensor_tensor(yy, yy, bc(st[:, 3].unsqueeze(2), shape), ALU.mult))

                        def gain():
                            link(nc.vector.tensor_tensor(yy, yy, bc(gb[:, 0].unsqueeze(1), shape), ALU.mult))

                        def shift():
                            link(nc.vector.tensor_tensor(yy, yy, bc(gb[:, 1].unsqueeze(1), shape), ALU.add))

                        def add():
                            link(nc.vector.tensor_tensor(new, res[:, tl], yy, ALU.add))
                            nc.vector.tensor_tensor(res[:, tl], res[:, tl], yy, ALU.add).then_inc(s_fin, 1)
                            dve.wait_ge(s_fin, c + 1)

                        return [total, mean, centre, square, variance, lambda: None, scale, gain, shift, add]

                    def chunk(c, q):
                        known = isinstance(c, int)
                        for e in range(E):
                            s = E * c + e
                            dve.wait_ge(s_hid, s + 1)
                            dve.wait_ge(s_cb, s + 1)
                            if not known or s >= DEEP:
                                dve.wait_ge(s_w2, s + 1 - DEEP)
                            nc.vector.tensor_tensor(wgt[e % DEEP], hid[e % DEEP], CB(e), ALU.mult).then_inc(s_wgt, 1)
                            if e == COLUMNS + 1:
                                rests(c + 1, 1 - q)
                            if FINISH <= e < FINISH + 10 and (not known or c >= 1):
                                finish(c - 1)[e - FINISH]()
                            if e < 5 and (not known or c >= 2):
                                next_norm(c - 2)[e]()
                            if e == BEST:
                                best(c + 1)
                            if COMBINE <= e < COMBINE + 4:
                                combine(c + 1)[e - COMBINE]()

                    rests(0, 0)
                    nc.vector.memset(nh, -0.5).then_inc(s_nh, 1)
                    norm.start()
                    best(0)
                    for part in combine(0):
                        part()
                    chunk(0, 0)
                    chunk(1, 1)

                    def pair(j):
                        chunk(2 * j, 0)
                        chunk(2 * j + 1, 1)

                    link.loop(pair, 1, CH // 2, 2 * (10 + 6 + 3 + 11))
                    for part in next_norm(CH - 2) + finish(CH - 1) + next_norm(CH - 1):
                        part()

                @block.gpsimd
                def _(pool):
                    def fetch(c):
                        if not isinstance(c, int) or c >= 1:
                            pool.wait_ge(s_tr, c)
                        nc.gpsimd.tensor_copy(xf, x2[:, span(TC * c, TC)].rearrange("p t a d -> p (t a d)")).then_inc(s_xf, 1)
                        pool.wait_ge(s_xf, c + 1)

                    def low(c, q):
                        pool.wait_ge(s_md, c + 1)
                        nc.gpsimd.tensor_tensor(xb[q][D:P], rest[D:P], xa[q][D:P], ALU.subtract).then_inc(s_lo, 1)
                        pool.wait_ge(s_lo, c + 1)

                    def rsd(c):
                        pool.wait_ge(s_var, c + 1)
                        nc.gpsimd.tensor_tensor(st[:, 3], st[:, 2], nh, ALU.pow).then_inc(s_rs, 1)

                    def chunk(c, q):
                        known = isinstance(c, int)
                        if not known or c >= 2:
                            norm.root(pool, c - 2)
                            pool.wait_ge(norm.s_rs, c - 1)
                        if not known or c + 2 <= CH:
                            fetch(c + 2)
                        low(c + 1, 1 - q)
                        if not known or c >= 1:
                            rsd(c - 1)

                    fetch(0)
                    for part in (ct[0], ct[1], x2[:, NT:NT + TC]):
                        nc.gpsimd.memset(part, 0.0).then_inc(s_zero, 1)
                        pool.wait_ge(s_zero, 1 if part is ct[0] else 2 if part is ct[1] else 3)
                    low(0, 0)
                    fetch(1)
                    pool.wait_ge(s_sel, 16)
                    nc.gpsimd.tensor_copy(selqk[:].rearrange("p a s m -> p (a s m)"), raw_sel).then_inc(s_selb, 1)
                    pool.wait_ge(s_nh, 1)
                    pool.wait_ge(norm.s_nh, 1)
                    chunk(0, 0)
                    chunk(1, 1)
                    with pool.Fori(1, CH // 2 - 1) as j:
                        chunk(2 * j, 0)
                        chunk(2 * j + 1, 1)
                    chunk(CH - 2, 0)
                    chunk(CH - 1, 1)
                    norm.root(pool, CH - 2)
                    rsd(CH - 1)
                    norm.root(pool, CH - 1)

                @block.sync
                def _(sp):
                    sp.dma_start(raw_sel, split_sel).then_inc(s_sel, 16)
                    sp.wait_ge(s_sel, 16)

        def attention_prep1():
            posT = big[:, 0:4096].rearrange("p (h c q) -> p h c q", h=H, c=2)
            pvT = [big[:, 4096 + 256 * n:4352 + 256 * n] for n in range(2)]
            st = big[:, 4608:4608 + 64]
            pinv = st[:, 0:16].rearrange("p (t h) -> p t h", t=2)
            gt = st[:, 16:24]
            s_v, s_vo, s_g, s_pt, s_ptc = (sem("a1_" + n) for n in ("values", "values_out", "gate_exp", "pos_turned", "pos_turned_out"))
            s_pv, s_pvs, s_pvt, s_pvo, s_pad = (sem("a1_" + n) for n in ("pos_values", "pos_values_in_sbuf", "pos_values_turned", "pos_values_out", "padded"))
            cols = ColumnParts("a1", *columns, copy_on_dve=True)

            with nc.Block() as block:
                @block.tensor
                def _(pe):
                    def pos_turn(h):
                        if h >= 2:
                            pe.wait_ge(s_ptc, h - 1)
                        for n in range(2):
                            for tq in range(2):
                                last = nc.tensor.transpose(ps[:, 4 + h % 2, 256 * n + P * tq:256 * n + P * tq + P], pexp[:, tq, h, P * n:P * n + P], ident)
                        last.then_inc(s_pt, 1)

                    def values(c):
                        pe.wait_ge(cols.s_lo, c + 1)
                        pe.wait_ge(cols.s_h2, c + 1)
                        if c >= 2:
                            pe.wait_ge(s_vo, c - 1)
                        for k in range(TC):
                            for n, src in enumerate((cols.xa, cols.xa, cols.xb)):
                                last = nc.tensor.matmul(ps[:, 2 + c % 2, D * k:D * k + D], src[:, c, P * k:P * k + P], w64[:, n, V1], start=(n == 0), stop=(n == 2))
                        last.then_inc(s_v, 1)

                    def pos_values(h):
                        if h >= 2:
                            pe.wait_ge(s_pvs, h - 1)
                        for c in range(2):
                            n = P - c
                            last = nc.tensor.matmul(ps[:, 6 + h % 2, 0:256], vall[0:n, c, h].rearrange("p b d -> p (b d)"), posT[0:n, h, c], start=(c == 0), stop=(c == 1))
                        last.then_inc(s_pv, 1)

                    def values_turn(h):
                        pe.wait_ge(s_pvs, h + 1)
                        if h >= 2:
                            pe.wait_ge(s_pvo, h - 1)
                        for tq in range(2):
                            last = nc.tensor.transpose(ps[:, 4 + h % 2, P * tq:P * tq + P], pvT[h % 2][:, P * tq:P * tq + P], ident)
                        last.then_inc(s_pvt, 1)

                    for c in range(CH + 3):
                        if c < CH:
                            cols.turn(pe, c)
                            pos_turn(c)
                        if c >= 3:
                            values(c - 3)
                    pe.wait_ge(s_ptc, H)
                    pe.wait_ge(s_vo, CH)
                    for h in range(H + 1):
                        if h < H:
                            pos_values(h)
                        if h >= 1:
                            values_turn(h - 1)

                @block.scalar
                def _(act):
                    nc.scalar.activation(gt, posw[:, 4], ACT.Exp, scale=-1.0).then_inc(s_g, 1)
                    for c in range(CH + 1):
                        if c < CH:
                            cols.high(act, c)
                        if c >= 1:
                            cols.middle(act, c - 1)
                    for h in range(H):
                        act.wait_ge(s_pv, h + 1)
                        if h >= 2:
                            act.wait_ge(s_pvt, h - 1)
                        nc.scalar.activation(pvT[h % 2], ps[:, 6 + h % 2, 0:256], ACT.Copy).then_inc(s_pvs, 1)

                @block.vector
                def _(dve):
                    link = chain(dve, "a1_dve")
                    dve.wait_ge(s_g, 1)
                    link(nc.vector.tensor_scalar(gt, gt, 1.0, None, ALU.add))
                    link(nc.vector.reciprocal(gt, gt))
                    link(nc.vector.tensor_scalar(omg, gt, -1.0, 1.0, ALU.mult, ALU.add))
                    link(nc.vector.reciprocal(pinv, psum[:]))
                    link(nc.vector.tensor_tensor(pinv, pinv, bc(gt.unsqueeze(1), [P, 2, H]), ALU.mult))
                    link(nc.vector.tensor_tensor(gsum, psum[:], pinv, ALU.mult))
                    for c in range(CH + 3):
                        if c < CH:
                            cols.rest(dve, c)
                            dve.wait_ge(s_pt, c + 1)
                            nc.vector.tensor_copy(posT[:, c].rearrange("p c q -> p (c q)"), ps[:, 4 + c % 2]).then_inc(s_ptc, 1)
                        if c >= 3:
                            d = c - 3
                            dve.wait_ge(s_v, d + 1)
                            v = ps[:, 2 + d % 2, 0:TC * D].rearrange("p (b t h d) -> p b t h d", b=2, t=2, h=H)
                            for tk in range(2):
                                last = nc.vector.tensor_copy(vall[:, tk, :, 2 * d:2 * d + 2].rearrange("p h b d -> p b h d"), v[:, :, tk])
                            last.then_inc(s_vo, 1)
                    for h in range(H):
                        dve.wait_ge(s_pvt, h + 1)
                        shape = [P, 2, B, D // H]
                        nc.vector.tensor_tensor(posv[:, :, :, 8 * h:8 * h + 8], ps[:, 4 + h % 2, 0:256].rearrange("p (t b d) -> p t b d", t=2, b=B),
                                                bc(pinv[:, :, h].unsqueeze(2).unsqueeze(3), shape), ALU.mult).then_inc(s_pvo, 1)

                @block.gpsimd
                def _(pool):
                    link = chain(pool, "a1_pad")
                    for n in range(2):
                        link(nc.gpsimd.memset(v1flat[n], 0.0))
                        link(nc.gpsimd.memset(v1flat[n][:, :, D:H * OW:OW + 1], 1.0))
                    for c in range(CH):
                        cols.low(pool, c)

        phase(tokens)
        phase(attention_prep0)
        phase(attention0)
        phase(experts0)
        phase(attention_prep1)
        phase(attention1)
        phase(experts_prep1)
        phase(experts1)


def tap_table():
    f = np.float32
    n = (SIG - 1) * UP + 1
    pos = (np.arange(n, dtype=f) / f(n - 1)) * f(SIG - 1)
    i0 = np.floor(pos)
    frac = (pos - i0).astype(f)
    A = f(-0.75)
    table = np.zeros((2 * P, TAPS, WIN), f)
    for k in range(-1, 3):
        at = np.abs(frac - f(k)).astype(f)
        near = ((A + f(2)) * at - (A + f(3))) * at * at + f(1)
        far = ((A * at - f(5) * A) * at + f(8) * A) * at - f(4) * A
        wk = np.where(at <= 1, near, np.where(at < 2, far, f(0))).astype(f)
        for p in range(NW * WIN):
            w, j = divmod(p, WIN)
            o = int(i0[p]) + k - (HOP * w + j // UP)
            assert -2 <= o <= 2 and (o > -2 or j % UP == 0)
            table[w, o + 2, j] += wk[p]
    table[NW] = table[NW - 1]
    return np.ascontiguousarray(table.reshape(2, P, TAPS, WIN).transpose(1, 0, 2, 3))


def constant_table():
    f = np.float32
    ident = np.eye(P, dtype=f)
    n, k = np.arange(WIN)[:, None], np.arange(WIN)[None, :]
    ang = 2 * np.pi * n / WIN
    cols = np.where(k < NB, np.cos(ang * k), np.sin(ang * (k - NB + 1)))
    dft = np.zeros((P, P))
    dft[:WIN, :WIN] = dft[WIN:, WIN:] = cols
    iota = np.tile(np.arange(16), (P, 1))
    q = np.arange(P)[:, None, None] + P * np.arange(2)[None, :, None]
    dist = (np.arange(256)[None, None, :] - q).reshape(P, 512)
    sel0 = np.zeros((P, 16, P))
    sel1 = np.zeros((P, 4, 2, 64))
    for part in range(3):
        for e in range(16):
            sel0[16 * part + e, e] = 1
        for e in range(8):
            sel1[8 * part + e, e // 2, e % 2] = 1
    neg = np.zeros((P, 1))
    for j in range(2):
        neg[64 * j + ROWS:64 * j + ROWS + 2] = -1
    return np.concatenate([a.reshape(P, -1).astype(f) for a in (ident, dft, iota, dist, sel0, sel1, neg)], axis=1)


def stack_table():
    hd = D // H
    sel = np.zeros((P, H, 3, P), np.float32)
    for p in range(PAIRS):
        for n, takes in enumerate((Q_PART, K_PART)):
            for j in range(2):
                for product, part in enumerate(takes):
                    for d in range(hd):
                        sel[D * n + hd * (2 * p + j) + d, 2 * p + n, part, 64 * j + hd * product + d] = 1
    return sel


def kernel(**inputs):
    import concourse.bacc as _bacc
    from concourse.bass_utils import run_bass_kernel_spmd as _run

    a = {k: np.asarray(v) for k, v in inputs.items()}

    def heads(w):
        return w.transpose(2, 0, 1).reshape(D, -1)

    gamma_beta = np.stack([a["L0_ffn_gamma"], a["L0_ffn_beta"]])
    wpos = np.concatenate([a["L1_attn_Wpos"].T, a["L1_attn_bpos"][None], a["L1_attn_gating"][None]])
    twice = lambda w: np.concatenate([w, w])
    w1_0 = a["L0_ffn_w1"].transpose(1, 0, 2).reshape(D, -1)
    w1_1 = a["L1_ffn_w1"].transpose(1, 0, 2).reshape(D, -1)
    feeds = {
        "x": a["x"], "taps": tap_table(), "consts": constant_table(),
        "w_raw": twice(np.concatenate([heads(a["L0_attn_Q"]), heads(a["L0_attn_K"]), a["L0_attn_VO"].transpose(1, 0, 2).reshape(D, -1),
                                       a["L0_ffn_gate_w"], a["L1_ffn_router_w"].T, a["L1_attn_Wqk"].T, a["L1_attn_Wv"].T], axis=1)),
        "gate_b0": a["L0_ffn_gate_b"][None],
        "w1_01": twice(np.concatenate([w1_0, w1_1], axis=1)), "b1_0": a["L0_ffn_b1"].T, "w2_0": a["L0_ffn_w2"].transpose(1, 0, 2),
        "b2_0": np.concatenate([a["L0_ffn_b2"]] * 3), "gamma": gamma_beta,
        "split_sel": stack_table(), "wpos": wpos,
        "wproj": a["L1_attn_Wproj"].T, "bproj": a["L1_attn_bproj"][None],
        "b1_1": a["L1_ffn_b1"].reshape(4, P).T,
        "w2_1": a["L1_ffn_w2"].reshape(4, P, D).transpose(1, 0, 2),
        "b2_1": np.concatenate([a["L1_ffn_b2"]] * 3),
    }
    nc = _bacc.Bacc("TRN2", target_bir_lowering=False, num_devices=1)
    arrays, args = {}, []
    for name, v in feeds.items():
        v = np.ascontiguousarray(v)
        arrays[f"in_{name}"] = v
        args.append(nc.dram_tensor(f"in_{name}", v.shape, mybir.dt.from_np(v.dtype), kind="ExternalInput").ap())
    args.append(nc.dram_tensor("out_tokens", (B, NW, D), F32, kind="ExternalOutput").ap())
    tower(nc, *args)
    r = _run(nc, [arrays], core_ids=[0])
    return r.results[0]["out_tokens"]
```
